# Optimizing a Trainium2 kernel written in Bass

```python
import numpy as np
import jax
import jax.numpy as jnp

def _softmax(x, axis=-1):
    return jax.nn.softmax(x, axis=axis)

def _gelu(x):
    return jax.nn.gelu(x, approximate=True)

def _silu(x):
    return jax.nn.silu(x)

def _sigmoid(x):
    return jax.nn.sigmoid(x)

def _layernorm(x, axis=-1, eps=1e-05):
    m = jnp.mean(x, axis=axis, keepdims=True)
    v = jnp.var(x, axis=axis, keepdims=True)
    return (x - m) / jnp.sqrt(v + eps)

def _scatter_add(tgt, idx, src, axis=0):
    return tgt.at[idx].add(src)

def _segment_sum(src, seg, n):
    return jax.ops.segment_sum(src, seg, n)
kernel_name = 'mk_gnn_preln_d4_gnn_r32_11d26d'

def setup_inputs(seed: int=0):
    np.random.seed(seed)
    _w = jnp.asarray

    def _rec_inputs():
        import jax
        import jax.numpy as jnp
        _gk = jax.random.key(seed)
        x = -0.000202 + 1 * jax.random.normal(jax.random.fold_in(_gk, 1), (3125, 128), jnp.float32)
        _s = jax.random.randint(jax.random.fold_in(_gk, 2), (50000,), 0, 3125, jnp.int32)
        _d = jax.random.randint(jax.random.fold_in(_gk, 3), (50000,), 0, 3125, jnp.int32)
        _loop = jnp.arange(3125, dtype=jnp.int32)
        src = jnp.concatenate([_s, _d, _loop])
        dst = jnp.concatenate([_d, _s, _loop])
        _o = jnp.argsort(dst, stable=True)
        src = src[_o]
        dst = dst[_o]
        edge_attr_32 = 0.000196303 + 1.00016 * jax.random.normal(jax.random.fold_in(_gk, 11), (103125, 32), jnp.float32)
        edge_weight = jax.random.uniform(jax.random.fold_in(_gk, 13), (103125,), jnp.float32, 0.0, 0.999999)
        return (x, src, dst, edge_attr_32, edge_weight)
    x, src, dst, edge_attr_32, edge_weight = _rec_inputs()

    def _L0_gnn_setup():
        import jax, jax.numpy as jnp
        import numpy as np
        N, E = (50000, 25000)
        NODE_DIM, EDGE_DIM, HIDDEN_DIM = (128, 32, 128)
        LN_EPS = 1e-05
        key = jax.random.key(seed)
        ks = jax.random.split(key, 10)

        def lin(k, fan_in, fan_out):
            bound = 1.0 / np.sqrt(fan_in)
            kw, kb = jax.random.split(k)
            W = jax.random.uniform(kw, (fan_out, fan_in), jnp.float32, -bound, bound)
            b = jax.random.uniform(kb, (fan_out,), jnp.float32, -bound, bound)
            return (W, b)
        x = jax.random.normal(ks[0], (N, NODE_DIM), jnp.float32)
        edge_index = jax.random.randint(ks[1], (2, E), 0, N, jnp.int64)
        edge_attr = jax.random.normal(ks[2], (E, EDGE_DIM), jnp.float32)
        W1, b1 = lin(ks[3], 2 * NODE_DIM + EDGE_DIM, HIDDEN_DIM)
        W2, b2 = lin(ks[4], HIDDEN_DIM, HIDDEN_DIM)
        Wu, bu = lin(ks[5], HIDDEN_DIM, NODE_DIM)
        gamma = jnp.ones((NODE_DIM,), jnp.float32)
        beta = jnp.zeros((NODE_DIM,), jnp.float32)
        return {'x': x, 'edge_attr': edge_attr, 'W1': W1, 'b1': b1, 'W2': W2, 'b2': b2, 'Wu': Wu, 'bu': bu, 'gamma': gamma, 'beta': beta, 'edge_index': edge_index}
    _L0_gnn_all = _L0_gnn_setup()
    _L0_gnn_in = {k: v for k, v in _L0_gnn_all.items() if k in ('W1', 'b1', 'W2', 'b2', 'Wu', 'bu', 'gamma', 'beta')}
    del _L0_gnn_all

    def _L1_gnn_setup():
        import jax, jax.numpy as jnp
        import numpy as np
        N_NODES = 50000
        N_EDGES = 25000
        F_IN = 128
        HIDDEN = 256
        MID = 48
        EMB = 128

        def _sage_conv(h, src, dst, Wl, Wr, b, n):
            agg = jax.ops.segment_sum(h[src], dst, num_segments=n)
            deg = jax.ops.segment_sum(jnp.ones_like(src, h.dtype), dst, num_segments=n)
            mean = agg / jnp.maximum(deg, 1.0)[:, None]
            return mean @ Wl.T + h @ Wr.T + b
        key = jax.random.key(seed)
        ks = jax.random.split(key, 10)
        x = jax.random.normal(ks[0], (N_NODES, F_IN), dtype=jnp.float32)
        edge_index = jax.random.randint(ks[1], (2, N_EDGES), 0, N_NODES, dtype=jnp.int32)

        def lin(k, out_d, in_d):
            s = 1.0 / np.sqrt(in_d)
            return jax.random.uniform(k, (out_d, in_d), jnp.float32, -s, s)
        return {'x': x, 'edge_index': edge_index, 'W1l': lin(ks[2], HIDDEN, F_IN), 'W1r': lin(ks[3], HIDDEN, F_IN), 'b1': jnp.zeros((HIDDEN,), jnp.float32), 'W2l': lin(ks[4], MID, HIDDEN), 'W2r': lin(ks[5], MID, HIDDEN), 'b2': jnp.zeros((MID,), jnp.float32), 'W3l': lin(ks[6], EMB, MID), 'W3r': lin(ks[7], EMB, MID), 'b3': jnp.zeros((EMB,), jnp.float32)}
    _L1_gnn_all = _L1_gnn_setup()
    _L1_gnn_in = {k: v for k, v in _L1_gnn_all.items() if k in ('W1l', 'W1r', 'b1', 'W2l', 'W2r', 'b2', 'W3l', 'W3r', 'b3')}
    del _L1_gnn_all

    def _L2_gnn_setup():
        import jax, jax.numpy as jnp
        import numpy as np
        EPS = 1e-12
        NUM_LAYERS = 3

        def _l2norm(v):
            n = jnp.linalg.norm(v, axis=-1, keepdims=True)
            return v / jnp.maximum(n, EPS)
        key = jax.random.key(seed)
        ks = jax.random.split(key, 6)
        N, E, D = (3125, 625000, 128)
        x = jax.random.normal(ks[0], (N, D), dtype=jnp.float32)
        edge_index = jax.random.randint(ks[1], (2, E), 0, N, dtype=jnp.int64)
        Wl = jax.random.normal(ks[2], (NUM_LAYERS, D, D), dtype=jnp.float32) * 0.05
        bl = jax.random.normal(ks[3], (NUM_LAYERS, D), dtype=jnp.float32) * 0.05
        Wr = jax.random.normal(ks[4], (NUM_LAYERS, D, D), dtype=jnp.float32) * 0.05
        return {'x': x, 'edge_index': edge_index, 'Wl': Wl, 'bl': bl, 'Wr': Wr}
    _L2_gnn_all = _L2_gnn_setup()
    _L2_gnn_in = {k: v for k, v in _L2_gnn_all.items() if k in ('Wl', 'bl', 'Wr')}
    del _L2_gnn_all

    def _L3_gnn_setup():
        import jax, jax.numpy as jnp
        import numpy as np
        N_NODES = 3125

        def gcn_conv(x, src, dst, w, W, b):
            n = x.shape[0]
            deg = jax.ops.segment_sum(w, dst, num_segments=n)
            dinv = jnp.where(deg > 0, jax.lax.rsqrt(deg), 0.0)
            norm = dinv[src] * w * dinv[dst]
            h = x @ W
            msg = h[src] * norm[:, None]
            out = jax.ops.segment_sum(msg, dst, num_segments=n)
            return out + b
        key = jax.random.key(seed)
        k1, k2, k3, k4, k5, k6, k7 = jax.random.split(key, 7)
        n, e = (N_NODES, 50000)
        fin, fhid, fout = (128, 128, 128)
        x = jax.random.normal(k1, (n, fin), dtype=jnp.float32)
        edge_index = jax.random.randint(k2, (2, e), 0, n, dtype=jnp.int64)
        edge_weight = jax.random.uniform(k3, (e,), dtype=jnp.float32)
        W1 = jax.random.normal(k4, (fin, fhid), dtype=jnp.float32) / np.sqrt(fin)
        b1 = jnp.zeros((fhid,), dtype=jnp.float32)
        W2 = jax.random.normal(k5, (fhid, fout), dtype=jnp.float32) / np.sqrt(fhid)
        b2 = jnp.zeros((fout,), dtype=jnp.float32)
        return {'x': x, 'edge_index': edge_index, 'edge_weight': edge_weight, 'W1': W1, 'b1': b1, 'W2': W2, 'b2': b2}
    _L3_gnn_all = _L3_gnn_setup()
    _L3_gnn_in = {k: v for k, v in _L3_gnn_all.items() if k in ('W1', 'b1', 'W2', 'b2')}
    del _L3_gnn_all
    return {'x': x, 'src': src, 'dst': dst, 'edge_attr_32': edge_attr_32, 'edge_weight': edge_weight, 'L0_gnn_W1': _L0_gnn_in['W1'], 'L0_gnn_b1': _L0_gnn_in['b1'], 'L0_gnn_W2': _L0_gnn_in['W2'], 'L0_gnn_b2': _L0_gnn_in['b2'], 'L0_gnn_Wu': _L0_gnn_in['Wu'], 'L0_gnn_bu': _L0_gnn_in['bu'], 'L0_gnn_gamma': _L0_gnn_in['gamma'], 'L0_gnn_beta': _L0_gnn_in['beta'], 'L1_gnn_W1l': _L1_gnn_in['W1l'], 'L1_gnn_W1r': _L1_gnn_in['W1r'], 'L1_gnn_b1': _L1_gnn_in['b1'], 'L1_gnn_W2l': _L1_gnn_in['W2l'], 'L1_gnn_W2r': _L1_gnn_in['W2r'], 'L1_gnn_b2': _L1_gnn_in['b2'], 'L1_gnn_W3l': _L1_gnn_in['W3l'], 'L1_gnn_W3r': _L1_gnn_in['W3r'], 'L1_gnn_b3': _L1_gnn_in['b3'], 'L2_gnn_Wl': _L2_gnn_in['Wl'], 'L2_gnn_bl': _L2_gnn_in['bl'], 'L2_gnn_Wr': _L2_gnn_in['Wr'], 'L3_gnn_W1': _L3_gnn_in['W1'], 'L3_gnn_b1': _L3_gnn_in['b1'], 'L3_gnn_W2': _L3_gnn_in['W2'], 'L3_gnn_b2': _L3_gnn_in['b2']}

def reference(x, src, dst, edge_attr_32, edge_weight, L0_gnn_W1, L0_gnn_b1, L0_gnn_W2, L0_gnn_b2, L0_gnn_Wu, L0_gnn_bu, L0_gnn_gamma, L0_gnn_beta, L1_gnn_W1l, L1_gnn_W1r, L1_gnn_b1, L1_gnn_W2l, L1_gnn_W2r, L1_gnn_b2, L1_gnn_W3l, L1_gnn_W3r, L1_gnn_b3, L2_gnn_Wl, L2_gnn_bl, L2_gnn_Wr, L3_gnn_W1, L3_gnn_b1, L3_gnn_W2, L3_gnn_b2):
    import jax
    import jax.numpy as jnp

    def _L0_gnn_ref(x, edge_attr, W1, b1, W2, b2, Wu, bu, gamma, beta, edge_index):
        import jax, jax.numpy as jnp
        import numpy as np
        N, E = (50000, 25000)
        NODE_DIM, EDGE_DIM, HIDDEN_DIM = (128, 32, 128)
        LN_EPS = 1e-05
        src, dst = (edge_index[0], edge_index[1])
        msg_input = jnp.concatenate([x[src], x[dst], edge_attr], axis=-1)
        h = jax.nn.relu(msg_input @ W1.T + b1)
        messages = h @ W2.T + b2
        agg = jax.ops.segment_sum(messages, dst, num_segments=x.shape[0])
        upd = jax.nn.relu(agg @ Wu.T + bu)
        y = x + upd
        mean = jnp.mean(y, axis=-1, keepdims=True)
        var = jnp.mean(jnp.square(y - mean), axis=-1, keepdims=True)
        return (y - mean) * jax.lax.rsqrt(var + LN_EPS) * gamma + beta

    def _L1_gnn_ref(x, edge_index, W1l, W1r, b1, W2l, W2r, b2, W3l, W3r, b3):
        import jax, jax.numpy as jnp
        import numpy as np
        N_NODES = 50000
        N_EDGES = 25000
        F_IN = 128
        HIDDEN = 256
        MID = 48
        EMB = 128

        def _sage_conv(h, src, dst, Wl, Wr, b, n):
            agg = jax.ops.segment_sum(h[src], dst, num_segments=n)
            deg = jax.ops.segment_sum(jnp.ones_like(src, h.dtype), dst, num_segments=n)
            mean = agg / jnp.maximum(deg, 1.0)[:, None]
            return mean @ Wl.T + h @ Wr.T + b
        src, dst = (edge_index[0], edge_index[1])
        n = x.shape[0]
        h = jax.nn.relu(_sage_conv(x, src, dst, W1l, W1r, b1, n))
        h = jax.nn.relu(_sage_conv(h, src, dst, W2l, W2r, b2, n))
        return _sage_conv(h, src, dst, W3l, W3r, b3, n)

    def _L2_gnn_ref(x, edge_index, Wl, bl, Wr):
        import jax, jax.numpy as jnp
        import numpy as np
        EPS = 1e-12
        NUM_LAYERS = 3

        def _l2norm(v):
            n = jnp.linalg.norm(v, axis=-1, keepdims=True)
            return v / jnp.maximum(n, EPS)
        N = x.shape[0]
        src = edge_index[0]
        dst = edge_index[1]
        ones = jnp.ones((dst.shape[0], 1), dtype=x.dtype)
        cnt = jax.ops.segment_sum(ones, dst, num_segments=N)
        denom = jnp.maximum(cnt, 1.0)
        for i in range(NUM_LAYERS):
            msg = x[src]
            agg = jax.ops.segment_sum(msg, dst, num_segments=N) / denom
            agg = _l2norm(agg)
            out = agg @ Wl[i].T + bl[i]
            out = out + _l2norm(x) @ Wr[i].T
            x = jax.nn.relu(out) if i != NUM_LAYERS - 1 else out
        return x

    def _L3_gnn_ref(x, edge_index, edge_weight, W1, b1, W2, b2):
        import jax, jax.numpy as jnp
        import numpy as np
        N_NODES = 3125

        def gcn_conv(x, src, dst, w, W, b):
            n = x.shape[0]
            deg = jax.ops.segment_sum(w, dst, num_segments=n)
            dinv = jnp.where(deg > 0, jax.lax.rsqrt(deg), 0.0)
            norm = dinv[src] * w * dinv[dst]
            h = x @ W
            msg = h[src] * norm[:, None]
            out = jax.ops.segment_sum(msg, dst, num_segments=n)
            return out + b
        n = x.shape[0]
        loop = jnp.arange(n, dtype=edge_index.dtype)
        src = jnp.concatenate([edge_index[0], loop])
        dst = jnp.concatenate([edge_index[1], loop])
        w = jnp.concatenate([edge_weight, jnp.ones((n,), dtype=edge_weight.dtype)])
        h = gcn_conv(x, src, dst, w, W1, b1)
        h = jax.nn.relu(h)
        return gcn_conv(h, src, dst, w, W2, b2)
    edge_index = jnp.stack([src, dst])
    h = jnp.maximum(_layernorm(x, axis=-1), 0.0)
    x = x + _L0_gnn_ref(h, edge_attr_32, L0_gnn_W1, L0_gnn_b1, L0_gnn_W2, L0_gnn_b2, L0_gnn_Wu, L0_gnn_bu, L0_gnn_gamma, L0_gnn_beta, edge_index)
    h = jnp.maximum(_layernorm(x, axis=-1), 0.0)
    x = x + _L1_gnn_ref(h, edge_index, L1_gnn_W1l, L1_gnn_W1r, L1_gnn_b1, L1_gnn_W2l, L1_gnn_W2r, L1_gnn_b2, L1_gnn_W3l, L1_gnn_W3r, L1_gnn_b3)
    h = jnp.maximum(_layernorm(x, axis=-1), 0.0)
    x = x + _L2_gnn_ref(h, edge_index, L2_gnn_Wl, L2_gnn_bl, L2_gnn_Wr)
    h = jnp.maximum(_layernorm(x, axis=-1), 0.0)
    x = x + _L3_gnn_ref(h, edge_index, edge_weight, L3_gnn_W1, L3_gnn_b1, L3_gnn_W2, L3_gnn_b2)
    return x

_drawn_inputs = setup_inputs


def setup_inputs(seed=0):
    import zlib

    import numpy as np

    out = dict(_drawn_inputs(seed))
    spreads = {'L0_gnn_gamma': (1.0, 0.2),
     'L0_gnn_beta': (0.0, 0.1),
     'L1_gnn_b1': (0.0, 0.484),
     'L1_gnn_b2': (0.0, 0.1),
     'L1_gnn_b3': (0.0, 0.1),
     'L3_gnn_b1': (0.0, 0.1),
     'L3_gnn_b2': (0.0, 0.1)}
    factors = {'edge_weight': 4.787, 'L0_gnn_bu': 4.443}
    for name, (base, spread) in spreads.items():
        noise = np.random.default_rng([zlib.crc32(name.encode()), seed]).standard_normal(out[name].shape)
        drawn = base * np.exp(spread * noise) if base else spread * noise
        out[name] = jnp.asarray(drawn.astype(out[name].dtype))
    for name, factor in factors.items():
        out[name] = (out[name] * factor).astype(out[name].dtype)
    return out
```

```python
from contextlib import ExitStack

import concourse.bass as bass
from concourse import mybir

F32 = mybir.dt.float32
F16 = mybir.dt.float16
BF16 = mybir.dt.bfloat16
I32 = mybir.dt.int32
ALU = mybir.AluOpType
ACT = mybir.ActivationFunctionType
AX = mybir.AxisListType

P = 128
N = 3125
E = 103125
D = 128
ED = 32
NT = (N + P - 1) // P
NPAD = NT * P
W = 16
J = (N + W - 1) // W
NCOL = J * W
CH = 5
BLK = CH * P
CP = -(-(E + BLK) // P)
CP += CP % 2
EPAD = CP * P
NKEY = W * NT
FAR = 4000
REC = 8
R_KEY, R_D25, R_LO, R_W1, R_W2, R_W3, R_ONE, R_SRC = range(REC)
GT = 4
G = (NT + GT - 1) // GT
WG = GT * P // W
SLABS = 3
LN_EPS = 1e-5
L2_EPS = 1e-12


def prepare(nc, new, d):
    with ExitStack() as ctx:
        def sb(name, shape, dt):
            return ctx.enter_context(nc.sbuf_tensor(name, shape, dt))

        dst_i = sb("dst_i", [P, CP], I32)
        nxt_i = sb("nxt_i", [P, CP], I32)
        src_i = sb("src_i", [P, CP], I32)
        hi_i = sb("hi_i", [P, CP], I32)
        lo_i = sb("lo_i", [P, CP], I32)
        win = sb("win", [P, CP], F16)
        win_next = sb("win_next", [P, CP], F16)
        junk = sb("junk", [P, 2, CP], F16)
        w_sb = sb("w_sb", [P, CP], F32)
        w_rest = sb("w_rest", [P, CP], F32)
        w_hi = sb("w_hi", [P, CP], BF16)
        w_mid = sb("w_mid", [P, CP], BF16)
        dst_f = sb("dst_f", [P, CP], F32)
        rec = sb("rec", [P, CP, REC], F32)
        counts = sb("counts", [P, J + 2], F32)
        thresholds = sb("thresholds", [P, J + 1], F32)
        ones = sb("prep_ones", [P, P], F32)
        starts_f = sb("starts_f", [1, J + 2], F32)
        over = sb("over", [1, J], F32)
        x = sb("x_all", [P, NT, D], F32)
        h = sb("h0_all", [P, NT, D], F32)
        pq = sb("pq", [P, 2, NT, D], F32)
        hT = sb("hT", [P, 2, P], F32)
        w_ab = sb("w_ab", [D, 2 * D], F32)
        b1 = sb("b1_row", [1, D], F32)
        stats = sb("stats", [P, NT, 6], F32)
        mv = sb("mv", [P, NT, 2], F32)
        std = sb("std", [P, NT], F32)
        rstd = sb("rstd", [P, NT], F32)
        eps = sb("prep_eps", [P, 1], F32)

        edges_in, x_in, w_in = new("edges_in"), new("x_in"), new("wab_in")
        shifted, counted = new("shifted"), new("counted")
        recs, pool_step = new("recs_built"), new("pool_step")
        consts = new("prep_consts")
        started, start_row, over_row = new("starts_psum"), new("start_row"), new("over_row")
        varied, stded, normed, h_ready = new("varied"), new("stded"), new("normed"), new("h_ready")
        ht_psum, ht_sb, pq_psum, pq_sb = new("ht_psum"), new("ht_sb"), new("pq_psum"), new("pq_sb")
        stored = new("prep_stored")
        compared = new("windows_compared")
        dve_step = new("prep_dve_step")

        with nc.Block() as block:
            @block.sync
            def _(sp):
                for dst, src in ((dst_i, d["dst"][0:EPAD]), (nxt_i, d["dst"][1:EPAD + 1]),
                                 (src_i, d["src"][0:EPAD]), (w_sb, d["w"][0:EPAD])):
                    sp.dma_start(dst[:, :], src.rearrange("(p c) -> p c", p=P)).then_inc(edges_in, 16)
                sp.dma_start(x[:, :, :], d["x"].rearrange("(t p) f -> p t f", p=P)).then_inc(x_in, 16)
                sp.dma_start(w_ab[:, 0:D], d["L0_W1"][0:D, :]).then_inc(w_in, 16)
                sp.dma_start(w_ab[:, D:2 * D], d["L0_W1"][D:2 * D, :]).then_inc(w_in, 16)
                sp.dma_start(b1[:, :], d["L0_b1"].rearrange("(a f) -> a f", a=1)).then_inc(w_in, 16)
                sp.wait_ge(recs, 1)
                sp.dma_start(d["records"].rearrange("(p c) k -> p c k", p=P), rec[:, :, :]).then_inc(stored, 16)
                sp.dma_start(d["dst_row"].rearrange("(p c) -> p c", p=P), dst_f[:, :]).then_inc(stored, 16)
                sp.wait_ge(h_ready, NT)
                sp.dma_start(d["h0"].rearrange("(t p) f -> p t f", p=P), h[:, :, :]).then_inc(stored, 16)
                sp.wait_ge(pq_sb, NT)
                sp.dma_start(d["P"].rearrange("(t p) f -> p t f", p=P), pq[:, 0]).then_inc(stored, 16)
                sp.dma_start(d["Q"].rearrange("(t p) f -> p t f", p=P), pq[:, 1]).then_inc(stored, 16)
                sp.wait_ge(stored, 80)

            @block.gpsimd
            def _(pool):
                steps = [0]

                def step(ins):
                    steps[0] += 1
                    ins.then_inc(pool_step, 1)
                    pool.wait_ge(pool_step, steps[0])

                nc.gpsimd.memset(ones[:, :], 1.0).then_inc(consts, 1)
                nc.gpsimd.memset(eps[:, :], LN_EPS).then_inc(consts, 1)
                nc.gpsimd.iota(thresholds[:, :], [[1, J + 1]], base=0, channel_multiplier=0,
                               allow_small_or_imprecise_dtypes=True).then_inc(consts, 1)
                nc.gpsimd.memset(rec[:, :, R_ONE], 1.0)
                pool.wait_ge(edges_in, 64)
                nc.gpsimd.tensor_copy(rec[:, :, R_SRC].bitcast(I32), src_i[:, :])
                step(nc.gpsimd.tensor_copy(dst_f[:, :], dst_i[:, :]))
                step(nc.gpsimd.tensor_scalar(rec[:, :, R_D25], dst_f[:, :], float(NT), None, ALU.mult))
                step(nc.gpsimd.tensor_copy(w_hi[:, :], w_sb[:, :]))
                nc.gpsimd.tensor_copy(rec[:, :, R_W1], w_hi[:, :])
                step(nc.gpsimd.tensor_tensor(w_rest[:, :], w_sb[:, :], w_hi[:, :], ALU.subtract))
                step(nc.gpsimd.tensor_copy(w_mid[:, :], w_rest[:, :]))
                nc.gpsimd.tensor_copy(rec[:, :, R_W2], w_mid[:, :])
                step(nc.gpsimd.tensor_tensor(rec[:, :, R_W3], w_rest[:, :], w_mid[:, :], ALU.subtract))
                pool.wait_ge(shifted, 1)
                nc.gpsimd.tensor_copy(rec[:, :, R_LO], lo_i[:, :])
                step(nc.gpsimd.tensor_copy(w_rest[:, :], hi_i[:, :]))
                step(nc.gpsimd.tensor_tensor(rec[:, :, R_KEY], rec[:, :, R_D25], w_rest[:, :], ALU.add))
                pool.drain().then_inc(recs, 1)

            @block.vector
            def _(dve):
                steps = [0]

                def step(ins):
                    steps[0] += 1
                    ins.then_inc(dve_step, 1)
                    dve.wait_ge(dve_step, steps[0])

                dve.wait_ge(x_in, 16)
                for t in range(NT):
                    last = nc.vector.bn_stats(stats[:, t, :], x[:, t, :])
                step(last)
                for t in range(NT):
                    last = nc.vector.bn_aggr(mv[:, t, :], stats[:, t, :])
                last.then_inc(varied, 1)
                dve.wait_ge(edges_in, 64)
                nc.vector.tensor_scalar(lo_i[:, :], src_i[:, :], P - 1, None, ALU.bitwise_and)
                step(nc.vector.tensor_scalar(hi_i[:, :], src_i[:, :], 7, None, ALU.logical_shift_right))
                dve.sem_inc(shifted, 1)
                dve.wait_ge(stded, 1)
                step(nc.vector.reciprocal(rstd[:, :], std[:, :]))
                for t in range(NT):
                    nc.vector.tensor_scalar(h[:, t, :], x[:, t, :], mv[:, t, 0:1], rstd[:, t:t + 1],
                                            ALU.subtract, ALU.mult).then_inc(normed, 1)
                dve.wait_ge(pool_step, 1)
                step(nc.vector.tensor_scalar(dst_i[:, :], dst_i[:, :], 4, None, ALU.logical_shift_right))
                nc.vector.tensor_copy(win[:, :], dst_i[:, :])
                step(nc.vector.tensor_scalar(nxt_i[:, :], nxt_i[:, :], 4, None, ALU.logical_shift_right))
                step(nc.vector.tensor_copy(win_next[:, :], nxt_i[:, :]))
                step(nc.vector.tensor_tensor(junk[:, 0], win_next[:, :], win[:, :], ALU.is_lt))
                step(nc.vector.reduce_sum(counts[:, J + 1:J + 2], junk[:, 0], axis=AX.X))
                dve.wait_ge(consts, 3)
                dve.sem_inc(compared, 2)
                with dve.Fori(0, J // 14) as i:
                    for k in range(14):
                        dve.wait_ge(compared, i * 14 + (k + 1))
                        nc.vector.tensor_scalar(junk[:, k % 2], win[:, :], thresholds[:, bass.ds(i * 14 + k, 1)], 0.0,
                                                       ALU.is_lt, ALU.add, accum_out=counts[:, bass.ds(i * 14 + k, 1)]
                                                       ).then_inc(compared, 1)
                dve.wait_ge(compared, J + 2)
                step(nc.vector.tensor_scalar(junk[:, 0], win[:, :], float(J), 0.0, ALU.is_lt, ALU.add,
                                        accum_out=counts[:, J:J + 1]))
                dve.drain().then_inc(counted, 1)
                dve.wait_ge(started, 1)
                step(nc.vector.tensor_copy(starts_f[:, :], d["psum"][0:1, 7, 0:J + 2]))
                nc.vector.tensor_copy(d["starts"][0:1, 0:J + 1], starts_f[:, 0:J + 1])
                step(nc.vector.tensor_tensor(over[:, :], starts_f[:, 1:J + 1], starts_f[:, 0:J], ALU.subtract))
                step(nc.vector.tensor_scalar(over[:, :], over[:, :], float(BLK), None, ALU.is_gt))
                step(nc.vector.reduce_sum(starts_f[:, 0:1], over[:, :], axis=AX.X))
                step(nc.vector.tensor_tensor(starts_f[:, 1:2], starts_f[:, 0:1], starts_f[:, J + 1:J + 2], ALU.add))
                step(nc.vector.tensor_copy(d["starts"][0:1, J + 1:J + 2], starts_f[:, 1:2]))

            def copy_pq(act, t):
                act.wait_ge(pq_psum, t + 1)
                nc.scalar.copy(pq[:, :, t, :], d["psum"][:, 2 + t % 2, 0:2 * D].rearrange("p (a f) -> p a f", a=2)
                               ).then_inc(pq_sb, 1)

            @block.scalar
            def _(act):
                act.wait_ge(consts, 3)
                act.wait_ge(varied, 1)
                nc.scalar.activation(std[:, :], mv[:, :, 1], ACT.Sqrt, bias=eps[:, 0:1]).then_inc(stded, 1)
                for t in range(NT):
                    act.wait_ge(normed, t + 1)
                    nc.scalar.activation(h[:, t, :], h[:, t, :], ACT.Relu).then_inc(h_ready, 1)
                    if t >= 1:
                        copy_pq(act, t - 1)
                    act.wait_ge(ht_psum, t + 1)
                    if t >= 2:
                        act.wait_ge(pq_psum, t - 1)
                    nc.scalar.copy(hT[:, t % 2, :], d["psum"][:, t % 2, 0:P]).then_inc(ht_sb, 1)
                copy_pq(act, NT - 1)

            @block.tensor
            def _(pe):
                psum, ident = d["psum"], d["ident"]
                pe.wait_ge(w_in, 48)
                pe.wait_ge(consts, 3)
                for t in range(NT + 1):
                    if t < NT:
                        pe.wait_ge(h_ready, t + 1)
                        if t >= 2:
                            pe.wait_ge(ht_sb, t - 1)
                        nc.tensor.transpose(psum[:, t % 2, 0:P], h[:, t, :], ident[:, :]).then_inc(ht_psum, 1)
                    if t >= 1:
                        u = t - 1
                        pe.wait_ge(ht_sb, u + 1)
                        if u >= 2:
                            pe.wait_ge(pq_sb, u - 1)
                        out = psum[:, 2 + u % 2, 0:2 * D]
                        nc.tensor.matmul(out, hT[:, u % 2, :], w_ab[:, :], start=True, stop=False)
                        nc.tensor.matmul(out[:, D:2 * D], ones[0:1, :], b1[:, :], start=False,
                                         stop=True).then_inc(pq_psum, 1)
                pe.wait_ge(counted, 1)
                nc.tensor.matmul(psum[0:1, 7, 0:J + 2], ones[:, 0:1], counts[:, :], start=True,
                                 stop=True).then_inc(started, 1)


def edge_pass(nc, new, d):
    S = 4
    CH_ACT = 4
    with ExitStack() as ctx:
        def sb(name, shape, dt):
            return ctx.enter_context(nc.sbuf_tensor(name, shape, dt))

        adj, psum = d["adj"], d["psum"]
        rec = sb("win_rec", [P, S, CH * REC], F32)
        lhs = sb("lhs", [ED + W, 2, BLK], F32)
        rhs = sb("rhs", [ED + W, S, D], F32)
        dst_row = sb("dst_rows", [ED + W, 2, BLK], F32)
        msg = sb("msg", [P, S, CH, D], F32)
        key = sb("key", [P, S, CH, 2], F32)
        wts = sb("wts", [P, S, CH, 4], BF16)
        hot_d = sb("hot_d", [P, S, CH, W], F32)
        hot_db = sb("hot_db", [P, S, CH, W], BF16)
        hot_lo = sb("hot_lo", [P, 2, CH, 4, P], BF16)
        hot_key = sb("hot_key", [P, 2, CH, NKEY], BF16)
        aw_out = sb("aw_out", [P, S, NKEY], F32)
        agg_win = sb("agg_win", [P, S, W], F32)
        deg_win = sb("deg_win", [4, S, W], F32)
        key0 = sb("key0", [P, J], F32)
        dst_of = sb("dst_of", [P, J], F32)
        iota_d = sb("iota_d", [P, W], F32)
        iota_lo = sb("iota_lo", [P, P], BF16)
        iota_key = sb("iota_key", [P, NKEY], F16)

        consts, w_in = new("edge_consts"), new("w1c_in")
        rec_in = [new(f"rec_in{s}") for s in range(S)]
        lhs_in = [new(f"lhs_in{s}") for s in range(S)]
        gathered = [new(f"gathered{s}") for s in range(S)]
        agg_stored = [new(f"agg_stored{s}") for s in range(S)]
        aw_stored = [new(f"aw_stored{s}") for s in range(S)]
        keyed, hots, hot_t, summed = new("keyed"), new("hots"), new("hot_t"), new("summed")
        multiplied, pre, sums = new("multiplied"), new("pre"), new("sums")
        relued, adj_out, agg_out = new("relued"), new("adj_out"), new("agg_out")
        hot_los, weighted = new("hot_los"), new("weighted")
        pace = new("edge_pace")

        def counts_of(u):
            return psum[:, u % 2, 0:NKEY]

        def weights_of(u):
            return psum[:, 2 + u % 2, 0:NKEY]

        def pre_of(k):
            return psum[:, 4 + k // 4, (k % 4) * D:(k % 4 + 1) * D]

        def await_count(eng, sem, count):
            if not isinstance(count, int):
                eng.wait_ge(sem, count)
                eng.sem_inc(pace, 1)
            elif count > 0:
                eng.wait_ge(sem, count)

        def uses(j, s, n):
            return (j - s) * (n // S)

        def by_window(eng, step):
            for j in range(2 * S):
                step(j, j % S)
            with eng.Fori(2, J // S) as i:
                for s in range(S):
                    step(i * S + s, s)

        def before(s):
            return (s - 1) % S

        with nc.Block() as block:
            @block.sync
            def _(sp):
                def store(j, s):
                    await_count(sp, adj_out, j + 1)
                    await_count(sp, agg_out, j + 1)
                    sp.dma_start(d["aw"][bass.ds(j, 1)].rearrange("a p k -> p (a k)"),
                                 aw_out[:, s, :]).then_inc(aw_stored[s], 16)
                    sp.dma_start(d["agg"][:, bass.ds(j * W, W)],
                                 agg_win[:, s, :]).then_inc(agg_stored[s], 16)
                    sp.dma_start(d["deg"][:, bass.ds(j * W, W)],
                                 deg_win[:, s, :]).then_inc(agg_stored[s], 16)

                def load(j, s):
                    start = sp.value_load(d["starts"][0:1, bass.ds(j, 1)], min_val=0, max_val=E)
                    if not isinstance(j, int) or j >= S:
                        store(j - S, s)
                    sp.dma_start(rec[:, s, :], d["records"][bass.ds(start, BLK), :].rearrange(
                        "(p k) c -> p (k c)", p=P)).then_inc(rec_in[s], 16)
                    await_count(sp, pre, j - 1)
                    sp.dma_start(lhs[0:ED, s % 2, :], d["ea"][:, bass.ds(start, BLK)]).then_inc(lhs_in[s], 16)
                    sp.dma_start(dst_row[ED:ED + W, s % 2, :], d["dst_row"][bass.ds(start, BLK)].rearrange(
                        "(a e) -> a e", a=1).broadcast_to([W, BLK])).then_inc(lhs_in[s], 16)
                    sp.dma_start(rhs[ED:ED + W, s, :], d["Q"][bass.ds(j * W, W), :]).then_inc(lhs_in[s], 16)

                with sp.If(d["crowded"]["SP"] < 1):
                    for s in range(S):
                        sp.dma_start(rhs[0:ED, s, :], d["L0_W1"][2 * D:2 * D + ED, :]).then_inc(w_in, 16)
                    by_window(sp, load)
                    for s in range(S):
                        store(J - S + s, s)
                    for s in range(S):
                        sp.wait_ge(aw_stored[s], 16 * (J // S))
                        sp.wait_ge(agg_stored[s], 32 * (J // S))

            @block.gpsimd
            def _(pool):
                nc.gpsimd.iota(key0[:, :], [[NKEY, J]], base=0, channel_multiplier=0,
                               allow_small_or_imprecise_dtypes=True).then_inc(consts, 1)
                nc.gpsimd.iota(dst_of[:, :], [[W, J]], base=-ED, channel_multiplier=1,
                               allow_small_or_imprecise_dtypes=True).then_inc(consts, 1)
                nc.gpsimd.iota(iota_d[:, :], [[NT, W]], base=0, channel_multiplier=0,
                               allow_small_or_imprecise_dtypes=True).then_inc(consts, 1)
                nc.gpsimd.iota(iota_lo[:, :], [[1, P]], base=0, channel_multiplier=0,
                               allow_small_or_imprecise_dtypes=True).then_inc(consts, 1)
                nc.gpsimd.iota(iota_key[:, :], [[1, NKEY]], base=0, channel_multiplier=0,
                               allow_small_or_imprecise_dtypes=True).then_inc(consts, 1)

                def gather(j, s):
                    await_count(pool, rec_in[s], uses(j, s, 16) + 16)
                    await_count(pool, sums, j - S + 1)
                    for k in range(CH):
                        at = k * REC + R_SRC
                        nc.gpsimd.indirect_dma_start(
                            msg[:, s, k, :], None, d["P"],
                            bass.IndirectOffsetOnAxis(ap=rec[:, s, at:at + 1].bitcast(I32), axis=0)
                        ).then_inc(gathered[s], 16)

                with pool.If(d["crowded"]["Pool"] < 1):
                    by_window(pool, gather)

            @block.vector
            def _(dve):
                def one_hots(j, s):
                    u = s % 2
                    row = rec[:, s, :].rearrange("p (k c) -> p k c", c=REC)
                    await_count(dve, rec_in[s], uses(j, s, 16) + 16)
                    await_count(dve, multiplied, j - 1)
                    await_count(dve, sums, j - S + 1)
                    nc.vector.tensor_scalar(key[:, s], row[:, :, 0:2], key0[:, bass.ds(j, 1)], None,
                                            ALU.subtract).then_inc(keyed, 1)
                    nc.vector.tensor_copy(wts[:, s], row[:, :, R_W1:R_ONE + 1])
                    for k in range(CH):
                        lo = row[:, k, R_LO:R_LO + 1]
                        last = nc.vector.tensor_scalar(hot_lo[:, u, k, 0, :], iota_lo[:, :], lo, None, ALU.is_equal)
                    last.then_inc(hot_los, 1)
                    for k in range(CH_ACT, CH):
                        lo = row[:, k, R_LO:R_LO + 1]
                        for q in range(3):
                            nc.vector.tensor_scalar(hot_lo[:, u, k, 1 + q, :], iota_lo[:, :], lo,
                                                    row[:, k, R_W1 + q:R_W1 + q + 1], ALU.is_equal, ALU.mult)
                    await_count(dve, keyed, j + 1)
                    for k in range(CH):
                        nc.vector.tensor_scalar(hot_key[:, u, k, :], iota_key[:, :], key[:, s, k, 0:1], None,
                                                ALU.is_equal)
                    lhs_d = iota_d[:, :].rearrange("p (a w) -> p a w", a=1).broadcast_to([P, CH, W])
                    rhs_d = key[:, s, :, 1:2].broadcast_to([P, CH, W])
                    nc.vector.tensor_tensor(hot_d[:, s], lhs_d, rhs_d, ALU.is_equal)
                    nc.vector.tensor_tensor(hot_db[:, s], lhs_d, rhs_d, ALU.is_equal).then_inc(hots, 1)
                    await_count(dve, lhs_in[s], uses(j, s, 48) + 48)
                    nc.vector.tensor_scalar(lhs[ED:ED + W, s % 2, :], dst_row[ED:ED + W, s % 2, :],
                                            dst_of[ED:ED + W, bass.ds(j, 1)], None, ALU.is_equal).then_inc(hot_t, 1)

                def add(j, s):
                    await_count(dve, pre, j + 1)
                    await_count(dve, gathered[s], uses(j, s, 16 * CH) + 16 * CH)
                    out = msg[:, s].rearrange("p k f -> p (k f)")
                    nc.vector.tensor_tensor(out, psum[:, 4:6, :].rearrange("p b f -> p (b f)")[:, 0:BLK], out,
                                            ALU.add).then_inc(summed, 1)

                def step(j, s):
                    one_hots(j, s)
                    if not isinstance(j, int) or j > 0:
                        add(j - 1, before(s))

                dve.wait_ge(consts, 5)
                with dve.If(d["crowded"]["DVE"] < 1):
                    by_window(dve, step)
                    add(J - 1, S - 1)

            @block.scalar
            def _(act):
                def relu_of(j, s):
                    await_count(act, summed, j + 1)
                    nc.scalar.activation(msg[:, s], msg[:, s], ACT.Relu).then_inc(relued, 1)

                def matrix_out(j, s):
                    await_count(act, multiplied, j + 1)
                    await_count(act, aw_stored[s], uses(j, s, 16))
                    nc.scalar.copy(adj[:, :, bass.ds(j * W, W)], counts_of(s).rearrange("p (w t) -> p t w", t=NT))
                    nc.scalar.copy(aw_out[:, s, :].rearrange("p (t w) -> p t w", w=W),
                                   weights_of(s).rearrange("p (w t) -> p t w", t=NT)).then_inc(adj_out, 1)

                def sums_out(j, s):
                    await_count(act, sums, j + 1)
                    await_count(act, agg_stored[s], uses(j, s, 32))
                    nc.scalar.copy(agg_win[:, s, :], psum[:, 6 + s % 2, 0:W])
                    nc.scalar.copy(deg_win[:, s, :], psum[0:4, 6 + s % 2, 32:32 + W]).then_inc(agg_out, 1)

                def weigh(j, s):
                    row = rec[:, s, :].rearrange("p (k c) -> p k c", c=REC)
                    await_count(act, hot_los, j + 1)
                    for k in range(CH_ACT):
                        for q in range(3):
                            last = nc.scalar.activation(hot_lo[:, s % 2, k, 1 + q, :], hot_lo[:, s % 2, k, 0, :],
                                                        ACT.Copy, scale=row[:, k, R_W1 + q:R_W1 + q + 1])
                    last.then_inc(weighted, 1)

                def step(j, s):
                    weigh(j, s)
                    if not isinstance(j, int) or j > 1:
                        sums_out(j - 2, before(before(s)))
                    if not isinstance(j, int) or j > 0:
                        matrix_out(j - 1, before(s))
                        relu_of(j - 1, before(s))

                with act.If(d["crowded"]["Activation"] < 1):
                    by_window(act, step)
                    sums_out(J - 2, S - 2)
                    matrix_out(J - 1, S - 1)
                    relu_of(J - 1, S - 1)
                    sums_out(J - 1, S - 1)

            @block.tensor
            def _(pe):
                def multiply(j, s):
                    u = s % 2
                    await_count(pe, hots, j + 1)
                    await_count(pe, adj_out, j - 1)
                    for k in range(CH):
                        nc.tensor.matmul(counts_of(s), hot_lo[:, u, k, 0, :], hot_key[:, u, k, :],
                                         start=(k == 0), stop=(k == CH - 1))
                    await_count(pe, weighted, j + 1)
                    for k in range(CH):
                        for q in range(3):
                            last = nc.tensor.matmul(weights_of(s), hot_lo[:, u, k, 1 + q, :], hot_key[:, u, k, :],
                                                    start=(k == 0 and q == 0), stop=(k == CH - 1 and q == 2))
                    last.then_inc(multiplied, 1)
                    await_count(pe, hot_t, j + 1)
                    await_count(pe, summed, j)
                    for k in range(CH):
                        last = nc.tensor.matmul(pre_of(k), lhs[:, s % 2, k:BLK:CH], rhs[:, s, :],
                                                start=True, stop=True)
                    last.then_inc(pre, 1)
                    await_count(pe, agg_out, j - 1)
                    for k in range(CH):
                        nc.tensor.matmul(psum[0:4, 6 + u, 32:32 + W], wts[:, s, k, :], hot_db[:, s, k, :],
                                         start=(k == 0), stop=(k == CH - 1))

                def sum_up(j, s):
                    u = s % 2
                    await_count(pe, relued, j + 1)
                    for k in range(CH):
                        last = nc.tensor.matmul(psum[:, 6 + u, 0:W], msg[:, s, k, :], hot_d[:, s, k, :],
                                                start=(k == 0), stop=(k == CH - 1))
                    last.then_inc(sums, 1)

                def step(j, s):
                    multiply(j, s)
                    if not isinstance(j, int) or j > 0:
                        sum_up(j - 1, before(s))

                with pe.If(d["crowded"]["PE"] < 1):
                    pe.wait_ge(w_in, 16 * S)
                    by_window(pe, step)
                    sum_up(J - 1, S - 1)



def crowded_edge_pass(nc, new, d):
    R = -(-E // BLK)
    STEPS = 6
    with ExitStack() as ctx:
        def sb(name, shape, dt):
            return ctx.enter_context(nc.sbuf_tensor("any_" + name, shape, dt))

        def sem(name):
            return new("any_" + name)

        psum = d["psum"]
        rec = sb("rec", [P, CH * REC], F32)
        lhs = sb("lhs", [ED + W, BLK], F32)
        rhs = sb("rhs", [ED + W, D], F32)
        dst_row = sb("dst_row", [ED + W, BLK], F32)
        msg = sb("msg", [P, CH, D], F32)
        key = sb("key", [P, CH, 2], F32)
        wts = sb("wts", [P, CH, 4], BF16)
        hot_d = sb("hot_d", [P, CH, W], F32)
        hot_db = sb("hot_db", [P, CH, W], BF16)
        hot_lo = sb("hot_lo", [P, CH, 4, P], BF16)
        hot_key = sb("hot_key", [P, CH, NKEY], BF16)
        matrix = sb("matrix", [P, 2, NKEY], F32)
        agg_win = sb("agg_win", [P, W], F32)
        deg_win = sb("deg_win", [4, W], F32)
        key0 = sb("key0", [P, J], F32)
        dst_of = sb("dst_of", [P, J], F32)
        iota_d = sb("iota_d", [P, W], F32)
        iota_lo = sb("iota_lo", [P, P], BF16)
        iota_key = sb("iota_key", [P, NKEY], F16)

        consts, w_in, loaded, gathered = sem("consts"), sem("w_in"), sem("loaded"), sem("gathered")
        hots, multiplied, relued, sums = sem("hots"), sem("multiplied"), sem("relued"), sem("sums")
        rec_in, p_stored = sem("rec_in"), sem("p_stored")
        block_done, cleared, stored, out_free = sem("block_done"), sem("cleared"), sem("stored"), sem("out_free")
        dve_step, pace = sem("dve_step"), sem("pace")

        def await_count(eng, sem, count):
            eng.wait_ge(sem, count)
            eng.sem_inc(pace, 1)

        with nc.Block() as block:
            @block.sync
            def _(sp):
                with sp.If(d["crowded"]["SP"] >= 1):
                    sp.dma_start(rhs[0:ED, :], d["L0_W1"][2 * D:2 * D + ED, :]).then_inc(w_in, 16)
                    sp.wait_ge(w_in, 16)
                    sp.sem_inc(out_free, 1)
                    with sp.Fori(0, J) as j:
                        with sp.Fori(0, R) as r:
                            await_count(sp, block_done, j * R + r + 1)
                            sp.dma_start(rec[:, :], d["records"][bass.ds(r * BLK, BLK), :].rearrange(
                                "(p k) c -> p (k c)", p=P)).then_inc(loaded, 16)
                            sp.dma_start(lhs[0:ED, :], d["ea"][:, bass.ds(r * BLK, BLK)]).then_inc(loaded, 16)
                            sp.dma_start(dst_row[ED:ED + W, :], d["dst_row"][bass.ds(r * BLK, BLK)].rearrange(
                                "(a e) -> a e", a=1).broadcast_to([W, BLK])).then_inc(loaded, 16)
                            sp.dma_start(rhs[ED:ED + W, :], d["Q"][bass.ds(j * W, W), :]).then_inc(loaded, 16)
                            sp.dma_start(msg[:, :, :], d["P_src"][bass.ds(r * BLK, BLK), :].rearrange(
                                "(p k) f -> p k f", p=P)).then_inc(loaded, 16)
                        await_count(sp, block_done, (j + 1) * R + 1)
                        sp.dma_start(d["counts"][bass.ds(j, 1)].rearrange("a p k -> p (a k)"),
                                     matrix[:, 0]).then_inc(stored, 16)
                        sp.dma_start(d["aw"][bass.ds(j, 1)].rearrange("a p k -> p (a k)"),
                                     matrix[:, 1]).then_inc(stored, 16)
                        sp.dma_start(d["agg"][:, bass.ds(j * W, W)], agg_win[:, :]).then_inc(stored, 16)
                        sp.dma_start(d["deg"][:, bass.ds(j * W, W)], deg_win[:, :]).then_inc(stored, 16)
                        await_count(sp, stored, (j + 1) * 64)
                        sp.sem_inc(out_free, 1)

            @block.gpsimd
            def _(pool):
                with pool.If(d["crowded"]["Pool"] >= 1):
                    for out, pattern, base, rows in (
                            (key0, [[NKEY, J]], 0, 0), (dst_of, [[W, J]], -ED, 1), (iota_d, [[NT, W]], 0, 0),
                            (iota_lo, [[1, P]], 0, 0), (iota_key, [[1, NKEY]], 0, 0)):
                        nc.gpsimd.iota(out[:, :], pattern, base=base, channel_multiplier=rows,
                                       allow_small_or_imprecise_dtypes=True).then_inc(consts, 1)
                    with pool.Fori(0, R) as r:
                        pool.dma_start(rec[:, :], d["records"][bass.ds(r * BLK, BLK), :].rearrange(
                            "(p k) c -> p (k c)", p=P)).then_inc(rec_in, 16)
                        await_count(pool, rec_in, (r + 1) * 16)
                        for k in range(CH):
                            at = k * REC + R_SRC
                            nc.gpsimd.indirect_dma_start(
                                msg[:, k, :], None, d["P"],
                                bass.IndirectOffsetOnAxis(ap=rec[:, at:at + 1].bitcast(I32), axis=0)
                            ).then_inc(gathered, 16)
                        await_count(pool, gathered, (r + 1) * 16 * CH)
                        pool.dma_start(d["P_src"][bass.ds(r * BLK, BLK), :].rearrange("(p k) f -> p k f", p=P),
                                       msg[:, :, :]).then_inc(p_stored, 16)
                        await_count(pool, p_stored, (r + 1) * 16)
                    pool.sem_inc(block_done, 1)

            @block.vector
            def _(dve):
                def block_of(j, n):
                    steps = [0]

                    def link(ins):
                        steps[0] += 1
                        ins.then_inc(dve_step, 1)
                        await_count(dve, dve_step, n * STEPS + steps[0])

                    row = rec[:, :].rearrange("p (k c) -> p k c", c=REC)
                    await_count(dve, loaded, (n + 1) * 80)
                    nc.vector.tensor_copy(wts[:, :], row[:, :, R_W1:R_ONE + 1])
                    for k in range(CH):
                        lo = row[:, k, R_LO:R_LO + 1]
                        nc.vector.tensor_scalar(hot_lo[:, k, 0, :], iota_lo[:, :], lo, None, ALU.is_equal)
                        for q in range(3):
                            nc.vector.tensor_scalar(hot_lo[:, k, 1 + q, :], iota_lo[:, :], lo,
                                                    row[:, k, R_W1 + q:R_W1 + q + 1], ALU.is_equal, ALU.mult)
                    nc.vector.tensor_scalar(lhs[ED:ED + W, :], dst_row[ED:ED + W, :], dst_of[ED:ED + W, bass.ds(j, 1)],
                                            None, ALU.is_equal)
                    link(nc.vector.tensor_scalar(key[:, :], row[:, :, 0:2], key0[:, bass.ds(j, 1)], None,
                                                 ALU.subtract))
                    for k in range(CH):
                        nc.vector.tensor_scalar(hot_key[:, k, :], iota_key[:, :], key[:, k, 0:1], None,
                                                ALU.is_equal)
                    lhs_d = iota_d[:, :].rearrange("p (a w) -> p a w", a=1).broadcast_to([P, CH, W])
                    rhs_d = key[:, :, 1:2].broadcast_to([P, CH, W])
                    nc.vector.tensor_tensor(hot_d[:, :], lhs_d, rhs_d, ALU.is_equal)
                    link(nc.vector.tensor_tensor(hot_db[:, :], lhs_d, rhs_d, ALU.is_equal))
                    dve.sem_inc(hots, 1)
                    await_count(dve, multiplied, n + 1)
                    out = msg[:, :].rearrange("p k f -> p (k f)")
                    link(nc.vector.tensor_tensor(out, psum[:, 4:6, :].rearrange("p b f -> p (b f)")[:, 0:BLK], out,
                                                 ALU.add))
                    link(nc.vector.tensor_scalar(out, out, 0.0, None, ALU.max))
                    dve.sem_inc(relued, 1)
                    for q in range(2):
                        link(nc.vector.tensor_tensor(
                            matrix[:, q].rearrange("p (t w) -> p t w", w=W), matrix[:, q].rearrange(
                                "p (t w) -> p t w", w=W),
                            psum[:, 2 * q, 0:NKEY].rearrange("p (w t) -> p t w", t=NT), ALU.add))
                    assert steps[0] == STEPS
                    await_count(dve, sums, n + 1)
                    nc.vector.tensor_tensor(agg_win[:, :], agg_win[:, :], psum[:, 6, 0:W], ALU.add)
                    nc.vector.tensor_tensor(deg_win[:, :], deg_win[:, :], psum[0:4, 7, 0:W], ALU.add)
                    dve.drain().then_inc(block_done, 1)
                    await_count(dve, block_done, n + 2)

                with dve.If(d["crowded"]["DVE"] >= 1):
                    dve.wait_ge(consts, 5)
                    with dve.Fori(0, J) as j:
                        await_count(dve, out_free, j + 1)
                        for out in (matrix[:, :], agg_win[:, :], deg_win[:, :]):
                            nc.vector.memset(out, 0.0).then_inc(cleared, 1)
                        await_count(dve, cleared, (j + 1) * 3)
                        with dve.Fori(0, R) as r:
                            block_of(j, j * R + r)

            @block.tensor
            def _(pe):
                with pe.If(d["crowded"]["PE"] >= 1):
                    with pe.Fori(0, J) as j:
                        with pe.Fori(0, R) as r:
                            n = j * R + r
                            await_count(pe, hots, n + 1)
                            for k in range(CH):
                                nc.tensor.matmul(psum[:, 0, 0:NKEY], hot_lo[:, k, 0, :], hot_key[:, k, :],
                                                 start=(k == 0), stop=(k == CH - 1))
                            for k in range(CH):
                                for q in range(3):
                                    nc.tensor.matmul(psum[:, 2, 0:NKEY], hot_lo[:, k, 1 + q, :], hot_key[:, k, :],
                                                     start=(k == 0 and q == 0), stop=(k == CH - 1 and q == 2))
                            for k in range(CH):
                                nc.tensor.matmul(psum[:, 4 + k // 4, (k % 4) * D:(k % 4 + 1) * D], lhs[:, k:BLK:CH],
                                                 rhs[:, :], start=True, stop=True)
                            for k in range(CH):
                                last = nc.tensor.matmul(psum[0:4, 7, 0:W], wts[:, k, :], hot_db[:, k, :],
                                                        start=(k == 0), stop=(k == CH - 1))
                            last.then_inc(multiplied, 1)
                            await_count(pe, relued, n + 1)
                            for k in range(CH):
                                last = nc.tensor.matmul(psum[:, 6, 0:W], msg[:, k, :], hot_d[:, k, :],
                                                        start=(k == 0), stop=(k == CH - 1))
                            last.then_inc(sums, 1)


def counts_slab(d):
    return d["adj"][:, :, :].rearrange("p t n -> p (t n)").bitcast(F32)[:, 0:SLABS * WG * NKEY].rearrange(
        "p (s j k) -> p s j k", s=SLABS, k=NKEY)


def h_copy(d):
    return counts_slab(d)[:, SLABS - 1].rearrange("p j k -> p (j k)")[:, 0:NT * D].rearrange("p (t f) -> p t f", f=D)


def tiles_of(c):
    return range(c * GT, min((c + 1) * GT, NT))


def linker(eng, sem):
    count = [0]

    def link(ins):
        count[0] += 1
        ins.then_inc(sem, 1)
        eng.wait_ge(sem, count[0])

    return link


def group_ap(dram, c):
    t0, t1 = tiles_of(c)[0], tiles_of(c)[-1] + 1
    return dram[t0 * P:t1 * P, :].rearrange("(t p) f -> p t f", p=P)


class Norm:

    def __init__(self, nc, new, sb, name):
        self.nc = nc
        self.stats = sb(name + "_stats", [P, GT, 6], F32)
        self.mv = sb(name + "_mv", [P, GT, 2], F32)
        self.std = sb(name + "_std", [P, GT], F32)
        self.varied, self.rooted = new(name + "_varied"), new(name + "_rooted")

    def on_vector(self, dve, link, out, x, c):
        nc, n = self.nc, len(tiles_of(c))
        for i in range(n):
            last = nc.vector.bn_stats(self.stats[:, i, :], x[:, i, :])
        link(last)
        for i in range(n):
            last = nc.vector.bn_aggr(self.mv[:, i, :], self.stats[:, i, :])
        last.then_inc(self.varied, 1)
        dve.wait_ge(self.rooted, c + 1)
        link(nc.vector.reciprocal(self.std[:, 0:n], self.std[:, 0:n]))
        for i in range(n):
            last = nc.vector.tensor_scalar(out[:, i, :], x[:, i, :], self.mv[:, i, 0:1], self.std[:, i:i + 1],
                                           ALU.subtract, ALU.mult)
        return last

    def on_scalar(self, act, eps, c):
        n = len(tiles_of(c))
        act.wait_ge(self.varied, c + 1)
        self.nc.scalar.activation(self.std[:, 0:n], self.mv[:, 0:n, 1], ACT.Sqrt,
                                  bias=eps[:, 0:1]).then_inc(self.rooted, 1)


def first_tail(nc, new, d):
    with ExitStack() as ctx:
        def sb(name, shape, dt):
            return ctx.enter_context(nc.sbuf_tensor(name, shape, dt))

        psum, ident, ones, h = d["psum"], d["ident"], d["ones"], d["h"]
        deg_rows = sb("deg_rows", [4, NPAD], F32)
        deg_row = sb("deg_row", [1, GT * P], F32)
        agg = sb("agg_in", [D, GT * P], F32)
        mT = sb("mT", [D, GT * P], F32)
        h0 = sb("h0_in", [P, GT, D], F32)
        x = sb("x_group", [P, GT, D], F32)
        w2, wu = sb("w2", [D, D], F32), sb("wu", [D, D], F32)
        b2, bu = sb("b2_row", [1, D], F32), sb("bu_row", [1, D], F32)
        gamma, beta = sb("gamma_rows", [P, D], F32), sb("beta_rows", [P, D], F32)
        wsum, positive = sb("wsum", [P, NT], F32), sb("positive", [P, NT], F32)
        norm_y, norm_x = Norm(nc, new, sb, "ty"), Norm(nc, new, sb, "tx")

        w_in, deg_in, cleared = new("t_w_in"), new("t_deg_in"), new("t_cleared")
        agg_in, node_in = new("t_agg_in"), new("t_node_in")
        deg_t, wsum_ready, wroot = new("t_deg_t"), new("t_wsum"), new("t_wroot")
        m_psum, m_sb, u_psum = new("t_m_psum"), new("t_m_sb"), new("t_u_psum")
        y_ready, x_ready, x_stored, normed, h_done = (new("t_y"), new("t_x"), new("t_x_stored"), new("t_normed"),
                                                      new("t_h"))
        dve_sem = new("t_dve")

        with nc.Block() as block:
            @block.sync
            def _(sp):
                for out, src in ((w2[:, :], d["L0_W2"]), (wu[:, :], d["L0_Wu"])):
                    sp.dma_start(out, src).then_inc(w_in, 16)
                for out, src in ((b2, d["L0_b2"]), (bu, d["L0_bu"])):
                    sp.dma_start(out[:, :], src.rearrange("(a f) -> a f", a=1)).then_inc(w_in, 16)
                for out, src in ((gamma, d["L0_gamma"]), (beta, d["L0_beta"])):
                    sp.dma_start(out[:, :], src.rearrange("(a f) -> a f", a=1).broadcast_to([P, D])
                                 ).then_inc(w_in, 16)
                sp.wait_ge(cleared, 3)
                sp.dma_start(deg_rows[:, 0:NCOL], d["deg"][:, 0:NCOL]).then_inc(deg_in, 16)
                for c in range(G):
                    n = min(GT * P, NCOL - c * GT * P)
                    if c >= 1:
                        sp.wait_ge(m_psum, c)
                    sp.dma_start(agg[:, 0:n], d["agg"][:, c * GT * P:c * GT * P + n]).then_inc(agg_in, 16)
                    sp.dma_start(deg_row[:, 0:n], d["deg"][3:4, c * GT * P:c * GT * P + n]).then_inc(agg_in, 16)
                    if c >= 1:
                        sp.wait_ge(x_ready, c)
                        sp.dma_start(group_ap(d["x1"], c - 1), x[:, 0:len(tiles_of(c - 1))]).then_inc(x_stored, 16)
                        sp.wait_ge(x_stored, 16 * c)
                        sp.wait_ge(normed, c)
                    m = len(tiles_of(c))
                    sp.dma_start(h0[:, 0:m], group_ap(d["h0"], c)).then_inc(node_in, 16)
                    sp.dma_start(x[:, 0:m], group_ap(d["x"], c)).then_inc(node_in, 16)
                sp.wait_ge(x_ready, G)
                sp.dma_start(group_ap(d["x1"], G - 1), x[:, 0:len(tiles_of(G - 1))]).then_inc(x_stored, 16)
                sp.wait_ge(x_stored, 16 * G)

            @block.tensor
            def _(pe):
                pe.wait_ge(deg_in, 16)
                for t in range(NT):
                    last = nc.tensor.transpose(psum[:, 0, 4 * t:4 * t + 4], deg_rows[0:4, t * P:(t + 1) * P],
                                               ident[0:4, 0:4])
                last.then_inc(deg_t, 1)
                pe.wait_ge(w_in, 96)
                for c in range(G):
                    n = len(tiles_of(c)) * P
                    pe.wait_ge(agg_in, 32 * (c + 1))
                    if c >= 1:
                        pe.wait_ge(m_sb, c)
                    nc.tensor.matmul(psum[:, 1, 0:n], w2[:, :], agg[:, 0:n], start=True, stop=False)
                    nc.tensor.matmul(psum[:, 1, 0:n], b2[:, :], deg_row[:, 0:n], start=False,
                                     stop=True).then_inc(m_psum, 1)
                    pe.wait_ge(m_sb, c + 1)
                    if c >= 1:
                        pe.wait_ge(y_ready, c)
                    for i in range(n // P):
                        out = psum[:, 2, i * D:(i + 1) * D]
                        nc.tensor.matmul(out, mT[:, i * P:(i + 1) * P], wu[:, :], start=True, stop=False)
                        last = nc.tensor.matmul(out, ones[0:1, :], bu[:, :], start=False, stop=True)
                    last.then_inc(u_psum, 1)

            @block.scalar
            def _(act):
                act.wait_ge(wsum_ready, 1)
                nc.scalar.activation(wsum[:, :], wsum[:, :], ACT.Sqrt).then_inc(wroot, 1)
                for c in range(G):
                    n = len(tiles_of(c))
                    act.wait_ge(m_psum, c + 1)
                    if c >= 1:
                        act.wait_ge(u_psum, c)
                    nc.scalar.copy(mT[:, 0:n * P], psum[:, 1, 0:n * P]).then_inc(m_sb, 1)
                    norm_y.on_scalar(act, d["eps"], c)
                    norm_x.on_scalar(act, d["eps"], c)
                    act.wait_ge(normed, c + 1)
                    t0 = tiles_of(c)[0]
                    nc.scalar.activation(h[:, t0:t0 + n], h[:, t0:t0 + n], ACT.Relu).then_inc(h_done, 1)
                act.wait_ge(h_done, G)

            @block.vector
            def _(dve):
                link = linker(dve, dve_sem)
                nc.vector.memset(deg_rows[:, NCOL:NPAD], 0.0).then_inc(cleared, 1)
                nc.vector.memset(deg_row[:, :], 0.0).then_inc(cleared, 1)
                nc.vector.memset(agg[:, :], 0.0).then_inc(cleared, 1)
                dve.wait_ge(deg_t, 1)
                parts = psum[:, 0, 0:4 * NT].rearrange("p (t q) -> p t q", q=4)
                link(nc.vector.tensor_scalar(d["eps_deg"][:, :], parts[:, :, 3], 1.0, None, ALU.max))
                nc.vector.reciprocal(d["inv_deg"][:, :], d["eps_deg"][:, :])
                link(nc.vector.tensor_scalar(wsum[:, :], parts[:, :, 0], 1.0, None, ALU.add))
                link(nc.vector.tensor_tensor(wsum[:, :], wsum[:, :], parts[:, :, 1], ALU.add))
                link(nc.vector.tensor_tensor(wsum[:, :], wsum[:, :], parts[:, :, 2], ALU.add))
                link(nc.vector.tensor_scalar(d["eps_deg"][:, :], d["eps_deg"][:, :], L2_EPS, None, ALU.mult))
                link(nc.vector.tensor_scalar(positive[:, :], wsum[:, :], 0.0, None, ALU.is_gt))
                nc.vector.tensor_scalar(wsum[:, :], wsum[:, :], 1e-38, None, ALU.max).then_inc(wsum_ready, 1)
                dve.wait_ge(wroot, 1)
                link(nc.vector.reciprocal(d["dinv"][:, :], wsum[:, :]))
                link(nc.vector.tensor_tensor(d["dinv"][:, :], d["dinv"][:, :], positive[:, :], ALU.mult))
                for c in range(G):
                    n = len(tiles_of(c))
                    t0 = tiles_of(c)[0]
                    y = h0[:, 0:n]
                    dve.wait_ge(u_psum, c + 1)
                    dve.wait_ge(node_in, 32 * (c + 1))
                    link(nc.vector.scalar_tensor_tensor(
                        out=y, in0=psum[:, 2, 0:n * D].rearrange("p (t f) -> p t f", f=D), scalar=0.0, in1=y,
                        op0=ALU.max, op1=ALU.add))
                    dve.sem_inc(y_ready, 1)
                    link(norm_y.on_vector(dve, link, y, y, c))
                    for row, op in ((gamma, ALU.mult), (beta, ALU.add)):
                        rows = row[:, :].rearrange("p (a f) -> p a f", a=1).broadcast_to([P, n, D])
                        link(nc.vector.tensor_tensor(y, y, rows, op))
                    link(nc.vector.tensor_tensor(x[:, 0:n], x[:, 0:n], y, ALU.add))
                    dve.sem_inc(x_ready, 1)
                    norm_x.on_vector(dve, link, h[:, t0:t0 + n], x[:, 0:n], c).then_inc(normed, 1)


class Layer:

    def __init__(self, nc, new, d, name, ctx):
        self.nc, self.d, self.name, self.ctx = nc, d, name, ctx
        self.new = lambda n: new(name + "_" + n)
        self.psum, self.ident, self.ones, self.h = d["psum"], d["ident"], d["ones"], d["h"]
        self.aggT = self.sb("aggT", [P, 2, GT * P], F32)
        self.hT = self.sb("hT", [P, 2, GT * P], F32)
        self.summed, self.agg_sb, self.agg_read = self.new("summed"), self.new("agg_sb"), self.new("agg_read")
        self.ht_psum, self.ht_sb = self.new("ht_psum"), self.new("ht_sb")
        self.w_in, self.counts_in, self.h_copied = self.new("w_in"), self.new("counts_in"), self.new("h_copied")
        self.split_hi, self.split_rest = self.new("split_hi"), self.new("split_rest")
        self.split_mid, self.split_done = self.new("split_mid"), self.new("split_done")
        self.dve_sem, self.act_sem = self.new("dve"), self.new("act")
        self.u_psum, self.combined, self.h_done = self.new("u_psum"), self.new("combined"), self.new("h_done")

    def sb(self, name, shape, dt):
        return self.ctx.enter_context(self.nc.sbuf_tensor(self.name + "_" + name, shape, dt))

    def split_on_scalar(self, act):
        nc, parts = self.nc, self.d["parts"]
        for c in range(G):
            t = slice(tiles_of(c)[0], tiles_of(c)[-1] + 1)
            nc.scalar.copy(parts[:, 0, t], self.h[:, t]).then_inc(self.split_hi, 1)
            if c >= 1:
                self.split_mid_of(act, c - 1)
        self.split_mid_of(act, G - 1)

    def split_mid_of(self, act, c):
        n = len(tiles_of(c))
        t = slice(tiles_of(c)[0], tiles_of(c)[-1] + 1)
        act.wait_ge(self.split_rest, c + 1)
        self.nc.scalar.copy(self.d["parts"][:, 1, t], self.rest[:, c % 2, 0:n]).then_inc(self.split_mid, 1)

    def split_on_vector(self, dve):
        for c in range(G + 1):
            if c < G:
                n = len(tiles_of(c))
                t = slice(tiles_of(c)[0], tiles_of(c)[-1] + 1)
                dve.wait_ge(self.split_hi, c + 1)
                if c >= 2:
                    dve.wait_ge(self.split_done, c - 1)
                self.nc.vector.tensor_tensor(self.rest[:, c % 2, 0:n], self.h[:, t], self.d["parts"][:, 0, t],
                                             ALU.subtract).then_inc(self.split_rest, 1)
            if c >= 1:
                b = c - 1
                n = len(tiles_of(b))
                t = slice(tiles_of(b)[0], tiles_of(b)[-1] + 1)
                dve.wait_ge(self.split_mid, c)
                self.nc.vector.tensor_tensor(self.d["parts"][:, 2, t], self.rest[:, b % 2, 0:n],
                                             self.d["parts"][:, 1, t], ALU.subtract).then_inc(self.split_done, 1)

    def sum_group(self, pe, c):
        with pe.If(self.d["crowded"]["PE"] < 1):
            self.sum_from_adj(pe, c)
        with pe.If(self.d["crowded"]["PE"] >= 1):
            self.sum_from_dram(pe, c)

    def sum_from_dram(self, pe, c):
        if c == 0:
            pe.wait_ge(self.h_copied, 1)
        pe.wait_ge(self.counts_in, 16 * (c + 1))
        if c >= 1:
            pe.wait_ge(self.agg_sb, c)
        m = min(WG, J - c * WG)
        for t in range(NT):
            last = self.nc.tensor.matmul(self.psum[:, 0, 0:m * W], h_copy(self.d)[:, t, :],
                                         counts_slab(self.d)[:, 0, 0:m, t * W:(t + 1) * W], start=(t == 0),
                                         stop=(t == NT - 1))
        last.then_inc(self.summed, 1)

    def load_counts(self, pool):
        with pool.If(self.d["crowded"]["Pool"] >= 1):
            self.nc.gpsimd.tensor_copy(h_copy(self.d), self.h[:, :, :]).then_inc(self.h_copied, 1)
            pool.wait_ge(self.h_copied, 1)
            for c in range(G):
                m = min(WG, J - c * WG)
                if c >= 1:
                    pool.wait_ge(self.summed, c)
                pool.dma_start(counts_slab(self.d)[:, 0, 0:m, :], self.d["counts"][c * WG:c * WG + m].rearrange(
                    "j p k -> p j k")).then_inc(self.counts_in, 16)

    def sum_from_adj(self, pe, c):
        nc, adj, parts = self.nc, self.d["adj"], self.d["parts"]
        n = min(GT * P, NCOL - c * GT * P)
        cols = slice(c * GT * P, c * GT * P + n)
        out = self.psum[:, 0, 0:n]
        if c >= 1:
            pe.wait_ge(self.agg_sb, c)
        if c == 0:
            for t in range(NT):
                if t % GT == 0:
                    pe.wait_ge(self.split_done, t // GT + 1)
                for q in range(3):
                    last = nc.tensor.matmul(out, parts[:, q, t, :], adj[:, t, cols], start=(t == 0 and q == 0),
                                            stop=(t == NT - 1 and q == 2))
        else:
            for q in range(3):
                nc.tensor.matmul(out, parts[:, q, 0, :], adj[:, 0, cols], start=(q == 0), stop=False)
            flat = parts[:, :, :, :].rearrange("p q t f -> p q (t f)")
            flat_adj = adj[:, :, :].rearrange("p t n -> p (t n)")
            with pe.Fori(1, NT - 1) as t:
                for q in range(3):
                    nc.tensor.matmul(out, flat[:, q, bass.ds(t * D, D)],
                                     flat_adj[:, bass.ds(t * NCOL + c * GT * P, n)], start=False, stop=False)
            for q in range(3):
                last = nc.tensor.matmul(out, parts[:, q, NT - 1, :], adj[:, NT - 1, cols], start=False, stop=(q == 2))
        last.then_inc(self.summed, 1)

    def copy_sums(self, act, c, rows=P):
        n = len(tiles_of(c)) * P
        act.wait_ge(self.summed, c + 1)
        if c >= 2:
            act.wait_ge(self.agg_read, c - 1)
        n = min(n, NCOL - c * GT * P)
        self.nc.scalar.copy(self.aggT[0:rows, c % 2, 0:n], self.psum[0:rows, 0, 0:n]).then_inc(self.agg_sb, 1)

    def transpose_h(self, pe, c, rows=P, bank_free=None):
        if c >= 1:
            pe.wait_ge(self.ht_sb, c)
        if bank_free is not None and c >= 4:
            pe.wait_ge(bank_free, c - 3)
        for i, t in enumerate(tiles_of(c)):
            last = self.nc.tensor.transpose(self.psum[0:rows, 1, i * P:(i + 1) * P], self.h[:, t, 0:rows],
                                            self.ident[:, :])
        last.then_inc(self.ht_psum, 1)

    def copy_ht(self, act, c, rows=P):
        n = len(tiles_of(c)) * P
        act.wait_ge(self.ht_psum, c + 1)
        if c >= 2:
            act.wait_ge(self.u_psum, c - 1)
        self.nc.scalar.copy(self.hT[0:rows, c % 2, 0:n], self.psum[0:rows, 1, 0:n]).then_inc(self.ht_sb, 1)


def wide_layer(nc, new, d):
    H1, M2 = 2 * D, 48
    with ExitStack() as ctx:
        L = Layer(nc, new, d, "wide", ctx)
        psum, h = L.psum, L.h
        w1l, w1r, b1 = L.sb("w1l", [D, H1], F32), L.sb("w1r", [D, H1], F32), L.sb("b1", [1, H1], F32)
        w2 = L.sb("w2", [P, 2, 2 * M2], F32)
        b2 = L.sb("b2", [1, M2], F32)
        h1 = L.sb("h1", [P, GT, H1], F32)
        L.rest = h1[:, :, :].rearrange("p t f -> p (t f)").rearrange("p (a t f) -> p a t f", a=2, f=D)
        h1T = L.sb("h1T", [P, GT, 2, P], F32)
        relued, t_psum, t_sb, yz_psum = L.new("relued"), L.new("t_psum"), L.new("t_sb"), L.new("yz_psum")
        with nc.Block() as block:
            @block.sync
            def _(sp):
                sp.dma_start(w1l[:, :], d["L1_W1l"]).then_inc(L.w_in, 16)
                sp.dma_start(w1r[:, :], d["L1_W1r"]).then_inc(L.w_in, 16)
                sp.dma_start(b1[:, :], d["L1_b1"].rearrange("(a f) -> a f", a=1)).then_inc(L.w_in, 16)
                sp.dma_start(b2[:, :], d["L1_b2"].rearrange("(a f) -> a f", a=1)).then_inc(L.w_in, 16)
                sp.dma_start(w2[:, :, 0:M2], d["L1_W2l"].rearrange("(k p) f -> p k f", p=P)).then_inc(L.w_in, 16)
                sp.dma_start(w2[:, :, M2:2 * M2], d["L1_W2r"].rearrange("(k p) f -> p k f", p=P)).then_inc(L.w_in, 16)

            @block.gpsimd
            def _(pool):
                L.load_counts(pool)

            @block.tensor
            def _(pe):
                def products(c):
                    pe.wait_ge(L.agg_sb, c + 1)
                    pe.wait_ge(L.ht_sb, c + 1)
                    if c >= 1:
                        pe.wait_ge(L.combined, c)
                    for i in range(len(tiles_of(c))):
                        at = slice((i % 2) * H1, (i % 2 + 1) * H1)
                        nc.tensor.matmul(psum[:, 2 + i // 2, at], L.aggT[:, c % 2, i * P:(i + 1) * P], w1l[:, :],
                                         start=True, stop=True)
                        nc.tensor.matmul(psum[:, 4 + i // 2, at], L.hT[:, c % 2, i * P:(i + 1) * P], w1r[:, :],
                                         start=True, stop=False)
                        last = nc.tensor.matmul(psum[:, 4 + i // 2, at], L.ones[0:1, :], b1[:, :], start=False,
                                                stop=True)
                    last.then_inc(L.u_psum, 1)

                def transposes(c):
                    pe.wait_ge(relued, c + 1)
                    if c >= 1:
                        pe.wait_ge(t_sb, c)
                    for i in range(len(tiles_of(c))):
                        for k in range(2):
                            at = (2 * i + k) % 4
                            last = nc.tensor.transpose(psum[:, 6 + i // 2, at * P:(at + 1) * P],
                                                       h1[:, i, k * P:(k + 1) * P], L.ident[:, :])
                    last.then_inc(t_psum, 1)

                def second(c):
                    pe.wait_ge(t_sb, c + 1)
                    if c < G - 3:
                        pe.wait_ge(L.ht_sb, c + 4)
                    if c >= 1:
                        pe.wait_ge(L.h_done, c)
                    for i in range(len(tiles_of(c))):
                        out = psum[:, 1, i * 2 * M2:(i + 1) * 2 * M2]
                        nc.tensor.matmul(out, h1T[:, i, 0, :], w2[:, 0, :], start=True, stop=False)
                        nc.tensor.matmul(out, h1T[:, i, 1, :], w2[:, 1, :], start=False, stop=False)
                        last = nc.tensor.matmul(out[:, M2:2 * M2], L.ones[0:1, :], b2[:, :], start=False, stop=True)
                    last.then_inc(yz_psum, 1)

                pe.wait_ge(L.w_in, 96)
                for c in range(G + 3):
                    if c < G:
                        L.transpose_h(pe, c, bank_free=L.h_done)
                        L.sum_group(pe, c)
                    if 0 <= c - 1 < G:
                        products(c - 1)
                    if 0 <= c - 2 < G:
                        transposes(c - 2)
                    if 0 <= c - 3 < G:
                        second(c - 3)

            @block.scalar
            def _(act):
                L.split_on_scalar(act)
                for c in range(G + 3):
                    if c < G:
                        L.copy_ht(act, c)
                        L.copy_sums(act, c)
                    if 0 <= c - 1 < G:
                        n = len(tiles_of(c - 1))
                        act.wait_ge(L.combined, c)
                        nc.scalar.activation(h1[:, 0:n], h1[:, 0:n], ACT.Relu).then_inc(relued, 1)
                    if 0 <= c - 2 < G:
                        n = len(tiles_of(c - 2))
                        act.wait_ge(t_psum, c - 1)
                        if c >= 3:
                            act.wait_ge(yz_psum, c - 2)
                        nc.scalar.copy(h1T[:, 0:n].rearrange("p t k f -> p (t k f)"),
                                       psum[:, 6:8, :].rearrange("p b f -> p (b f)")[:, 0:n * H1]).then_inc(t_sb, 1)

            @block.vector
            def _(dve):
                link = linker(dve, L.dve_sem)
                L.split_on_vector(dve)
                dve.wait_ge(L.split_done, G)
                for c in range(G + 3):
                    if 0 <= c - 1 < G:
                        b = c - 1
                        dve.wait_ge(L.u_psum, b + 1)
                        if b >= 1:
                            dve.wait_ge(t_psum, b)
                        for i, t in enumerate(tiles_of(b)):
                            at = slice((i % 2) * H1, (i % 2 + 1) * H1)
                            last = nc.vector.tensor_copy(h1[:, i, :], psum[:, 4 + i // 2, at])
                        link(last)
                        for i, t in enumerate(tiles_of(b)):
                            at = slice((i % 2) * H1, (i % 2 + 1) * H1)
                            last = nc.vector.scalar_tensor_tensor(
                                out=h1[:, i, :], in0=psum[:, 2 + i // 2, at], scalar=d["inv_deg"][:, t:t + 1],
                                in1=h1[:, i, :], op0=ALU.mult, op1=ALU.add)
                        last.then_inc(L.combined, 1)
                        dve.wait_ge(L.agg_sb, b + 1)
                        dve.sem_inc(L.agg_read, 1)
                    if 0 <= c - 3 < G:
                        b = c - 3
                        n = len(tiles_of(b))
                        t0 = tiles_of(b)[0]
                        dve.wait_ge(yz_psum, b + 1)
                        nc.vector.tensor_copy(h[:, t0:t0 + n, 0:2 * M2], psum[:, 1, 0:n * 2 * M2].rearrange(
                            "p (t f) -> p t f", f=2 * M2)).then_inc(L.h_done, 1)


def narrow_layer(nc, new, d):
    M2 = 48
    with ExitStack() as ctx:
        L = Layer(nc, new, d, "narrow", ctx)
        L.rest = L.sb("rest", [P, 2, GT, D], F32)
        psum, h = L.psum, L.h
        with nc.Block() as block:
            @block.gpsimd
            def _(pool):
                L.load_counts(pool)

            @block.tensor
            def _(pe):
                for c in range(G + 1):
                    if c < G:
                        L.sum_group(pe, c)
                    if c >= 1:
                        pe.wait_ge(L.agg_sb, c)
                        if c >= 2:
                            pe.wait_ge(L.combined, c - 1)
                        for i in range(len(tiles_of(c - 1))):
                            last = nc.tensor.transpose(psum[:, 2, i * M2:(i + 1) * M2],
                                                       L.aggT[0:M2, (c - 1) % 2, i * P:(i + 1) * P],
                                                       L.ident[0:M2, 0:M2])
                        last.then_inc(L.u_psum, 1)

            @block.scalar
            def _(act):
                L.split_on_scalar(act)
                for c in range(G + 1):
                    if c < G:
                        L.copy_sums(act, c, M2)
                    if c >= 1:
                        t = slice(tiles_of(c - 1)[0], tiles_of(c - 1)[-1] + 1)
                        act.wait_ge(L.combined, c)
                        nc.scalar.activation(h[:, t, 0:M2], h[:, t, 0:M2], ACT.Relu).then_inc(L.h_done, 1)

            @block.vector
            def _(dve):
                L.split_on_vector(dve)
                for c in range(G):
                    dve.wait_ge(L.u_psum, c + 1)
                    dve.sem_inc(L.agg_read, 1)
                    for i, t in enumerate(tiles_of(c)):
                        last = nc.vector.scalar_tensor_tensor(
                            out=h[:, t, 0:M2], in0=psum[:, 2, i * M2:(i + 1) * M2], scalar=d["inv_deg"][:, t:t + 1],
                            in1=h[:, t, M2:2 * M2], op0=ALU.mult, op1=ALU.add)
                    last.then_inc(L.combined, 1)


def out_layer(nc, new, d):
    M2 = 48
    with ExitStack() as ctx:
        L = Layer(nc, new, d, "out", ctx)
        L.rest = L.sb("rest", [P, 2, GT, D], F32)
        psum, h = L.psum, L.h
        wl, wr, b = L.sb("w3l", [M2, D], F32), L.sb("w3r", [M2, D], F32), L.sb("b3", [1, D], F32)
        x = L.sb("x", [P, GT, D], F32)
        norm = Norm(nc, L.new, L.sb, "norm")
        x_in, x_ready, x_stored, normed = L.new("x_in"), L.new("x_ready"), L.new("x_stored"), L.new("normed")
        with nc.Block() as block:
            @block.sync
            def _(sp):
                sp.dma_start(wl[:, :], d["L1_W3l"]).then_inc(L.w_in, 16)
                sp.dma_start(wr[:, :], d["L1_W3r"]).then_inc(L.w_in, 16)
                sp.dma_start(b[:, :], d["L1_b3"].rearrange("(a f) -> a f", a=1)).then_inc(L.w_in, 16)
                stream_x(sp, d["x1"], d["x2"], x, x_in, x_ready, x_stored, normed)

            @block.gpsimd
            def _(pool):
                L.load_counts(pool)

            @block.tensor
            def _(pe):
                pe.wait_ge(L.w_in, 48)
                for c in range(G + 1):
                    if c < G:
                        L.transpose_h(pe, c, M2)
                        L.sum_group(pe, c)
                    if c >= 1:
                        g = c - 1
                        pe.wait_ge(L.agg_sb, c)
                        pe.wait_ge(L.ht_sb, c)
                        if c >= 2:
                            pe.wait_ge(L.combined, c - 1)
                        for i in range(len(tiles_of(g))):
                            at, nodes = slice(i * D, (i + 1) * D), slice(i * P, (i + 1) * P)
                            nc.tensor.matmul(psum[:, 2, at], L.aggT[0:M2, g % 2, nodes], wl[:, :], start=True,
                                             stop=True)
                            nc.tensor.matmul(psum[:, 3, at], L.hT[0:M2, g % 2, nodes], wr[:, :], start=True,
                                             stop=False)
                            last = nc.tensor.matmul(psum[:, 3, at], L.ones[0:1, :], b[:, :], start=False, stop=True)
                        last.then_inc(L.u_psum, 1)

            @block.scalar
            def _(act):
                L.split_on_scalar(act)
                for c in range(G + 1):
                    if c < G:
                        L.copy_ht(act, c, M2)
                        L.copy_sums(act, c, M2)
                    if c >= 1:
                        norm.on_scalar(act, d["eps"], c - 1)
                        t = slice(tiles_of(c - 1)[0], tiles_of(c - 1)[-1] + 1)
                        act.wait_ge(normed, c)
                        nc.scalar.activation(h[:, t], h[:, t], ACT.Relu).then_inc(L.h_done, 1)

            @block.vector
            def _(dve):
                link = linker(dve, L.dve_sem)
                L.split_on_vector(dve)
                for c in range(G):
                    n = len(tiles_of(c))
                    t0 = tiles_of(c)[0]
                    dve.wait_ge(L.u_psum, c + 1)
                    dve.sem_inc(L.agg_read, 1)
                    dve.wait_ge(x_in, 16 * (c + 1))
                    link(nc.vector.tensor_tensor(x[:, 0:n], x[:, 0:n], psum[:, 3, 0:n * D].rearrange(
                        "p (t f) -> p t f", f=D), ALU.add))
                    for i, t in enumerate(tiles_of(c)):
                        last = nc.vector.scalar_tensor_tensor(
                            out=x[:, i, :], in0=psum[:, 2, i * D:(i + 1) * D], scalar=d["inv_deg"][:, t:t + 1],
                            in1=x[:, i, :], op0=ALU.mult, op1=ALU.add)
                    link(last)
                    dve.sem_inc(L.combined, 1)
                    dve.sem_inc(x_ready, 1)
                    norm.on_vector(dve, link, h[:, t0:t0 + n], x[:, 0:n], c).then_inc(normed, 1)


def stream_x(sp, source, target, x, x_in, x_ready, x_stored, normed):
    for c in range(G):
        n = len(tiles_of(c))
        if c >= 1:
            sp.wait_ge(x_stored, 16 * c)
            sp.wait_ge(normed, c)
        sp.dma_start(x[:, 0:n], group_ap(source, c)).then_inc(x_in, 16)
        sp.wait_ge(x_ready, c + 1)
        sp.dma_start(group_ap(target, c), x[:, 0:n]).then_inc(x_stored, 16)
    sp.wait_ge(x_stored, 16 * G)


def norm_layer(nc, new, d, number, layers):
    final = number == layers - 1
    with ExitStack() as ctx:
        L = Layer(nc, new, d, f"l2n{number}", ctx)
        psum, h = L.psum, L.h
        wl, wr, b = L.sb("wl", [D, D], F32), L.sb("wr", [D, D], F32), L.sb("b", [P, D], F32)
        L.rest = L.sb("rest", [P, 2, GT, D], F32)
        square = L.sb("square", [P, GT * P], F32)
        tmp = L.sb("tmp", [P, GT, D], F32)
        tmp_sq = L.sb("tmp_sq", [P, D], F32)
        x = L.sb("x", [P, GT, D], F32)
        h_sq = L.sb("h_sq", [P, 2, GT], F32)
        s_h = L.sb("s_h", [P, GT], F32)
        s_agg = L.sb("s_agg", [P, GT], F32)
        norm = Norm(nc, L.new, L.sb, "norm")
        x_in, x_ready, x_stored, normed = L.new("x_in"), L.new("x_ready"), L.new("x_stored"), L.new("normed")
        squared, n2_psum, rooted, h_squared = L.new("squared"), L.new("n2_psum"), L.new("rooted"), L.new("h_squared")
        scales = L.new("scales")
        with nc.Block() as block:
            @block.sync
            def _(sp):
                sp.dma_start(wl[:, :], d["L2_Wl"][number]).then_inc(L.w_in, 16)
                sp.dma_start(wr[:, :], d["L2_Wr"][number]).then_inc(L.w_in, 16)
                sp.dma_start(b[:, :], d["L2_bl"][number:number + 1, :].broadcast_to([P, D])).then_inc(L.w_in, 16)
                if final:
                    stream_x(sp, d["x2"], d["x3"], x, x_in, x_ready, x_stored, normed)

            @block.gpsimd
            def _(pool):
                L.load_counts(pool)

            @block.tensor
            def _(pe):
                pe.wait_ge(L.w_in, 48)
                for c in range(G + 1):
                    if c < G:
                        L.transpose_h(pe, c)
                        L.sum_group(pe, c)
                    if c >= 1:
                        g = c - 1
                        pe.wait_ge(L.agg_sb, c)
                        pe.wait_ge(L.ht_sb, c)
                        pe.wait_ge(squared, c)
                        if c >= 2:
                            pe.wait_ge(L.combined, c - 1)
                        for i in range(len(tiles_of(g))):
                            last = nc.tensor.matmul(psum[:, 4, i:i + 1], square[:, i * P:(i + 1) * P],
                                                    L.ones[:, 0:1], start=True, stop=True)
                        last.then_inc(n2_psum, 1)
                        for i in range(len(tiles_of(g))):
                            at, nodes = slice(i * D, (i + 1) * D), slice(i * P, (i + 1) * P)
                            nc.tensor.matmul(psum[:, 2, at], L.aggT[:, g % 2, nodes], wl[:, :], start=True, stop=True)
                            last = nc.tensor.matmul(psum[:, 3, at], L.hT[:, g % 2, nodes], wr[:, :], start=True,
                                                    stop=True)
                        last.then_inc(L.u_psum, 1)

            @block.scalar
            def _(act):
                L.split_on_scalar(act)
                for c in range(G + 1):
                    if c < G:
                        n = len(tiles_of(c)) * P
                        L.copy_ht(act, c)
                        if c >= 2:
                            act.wait_ge(scales, c - 1)
                        for i, t in enumerate(tiles_of(c)):
                            if i or c:
                                act.wait_ge(h_squared, sum(len(tiles_of(g)) for g in range(c)) + i)
                            nc.scalar.activation(tmp_sq[:, :], h[:, t, :], ACT.Square,
                                                 accum_out=h_sq[:, c % 2, i:i + 1]).then_inc(h_squared, 1)
                        L.copy_sums(act, c)
                        act.wait_ge(L.agg_sb, c + 1)
                        if c >= 1:
                            act.wait_ge(n2_psum, c)
                        nc.scalar.activation(square[:, 0:n], L.aggT[:, c % 2, 0:n], ACT.Square).then_inc(squared, 1)
                    if c >= 1:
                        g = c - 1
                        n = len(tiles_of(g))
                        act.wait_ge(n2_psum, c)
                        if c >= 2:
                            act.wait_ge(L.combined, c - 1)
                        nc.scalar.activation(s_agg[:, 0:n], psum[:, 4, 0:n], ACT.Sqrt)
                        act.wait_ge(h_squared, sum(len(tiles_of(k)) for k in range(c)))
                        nc.scalar.activation(s_h[:, 0:n], h_sq[:, g % 2, 0:n], ACT.Sqrt).then_inc(rooted, 1)
                        t = slice(tiles_of(g)[0], tiles_of(g)[-1] + 1)
                        if final:
                            norm.on_scalar(act, d["eps"], g)
                            act.wait_ge(normed, c)
                            nc.scalar.activation(h[:, t], h[:, t], ACT.Relu).then_inc(L.h_done, 1)
                        else:
                            act.wait_ge(L.combined, c)
                            nc.scalar.activation(h[:, t], tmp[:, 0:n], ACT.Relu).then_inc(L.h_done, 1)

            @block.vector
            def _(dve):
                link = linker(dve, L.dve_sem)
                L.split_on_vector(dve)
                dve.wait_ge(L.w_in, 48)
                for c in range(G):
                    n = len(tiles_of(c))
                    t0 = tiles_of(c)[0]
                    dve.wait_ge(rooted, c + 1)
                    nc.vector.tensor_scalar(s_h[:, 0:n], s_h[:, 0:n], L2_EPS, None, ALU.max)
                    link(nc.vector.tensor_tensor(s_agg[:, 0:n], s_agg[:, 0:n], d["eps_deg"][:, t0:t0 + n], ALU.max))
                    nc.vector.reciprocal(s_h[:, 0:n], s_h[:, 0:n])
                    link(nc.vector.reciprocal(s_agg[:, 0:n], s_agg[:, 0:n]))
                    dve.sem_inc(scales, 1)
                    dve.wait_ge(L.u_psum, c + 1)
                    dve.sem_inc(L.agg_read, 1)
                    if c >= 1 and not final:
                        dve.wait_ge(L.h_done, c)
                    for i, t in enumerate(tiles_of(c)):
                        last = nc.vector.scalar_tensor_tensor(
                            out=tmp[:, i, :], in0=psum[:, 3, i * D:(i + 1) * D], scalar=s_h[:, i:i + 1],
                            in1=b[:, :], op0=ALU.mult, op1=ALU.add)
                    link(last)
                    for i, t in enumerate(tiles_of(c)):
                        last = nc.vector.scalar_tensor_tensor(
                            out=tmp[:, i, :], in0=psum[:, 2, i * D:(i + 1) * D], scalar=s_agg[:, i:i + 1],
                            in1=tmp[:, i, :], op0=ALU.mult, op1=ALU.add)
                    link(last)
                    dve.sem_inc(L.combined, 1)
                    if final:
                        dve.wait_ge(x_in, 16 * (c + 1))
                        link(nc.vector.tensor_tensor(x[:, 0:n], x[:, 0:n], tmp[:, 0:n], ALU.add))
                        dve.sem_inc(x_ready, 1)
                        norm.on_vector(dve, link, h[:, t0:t0 + n], x[:, 0:n], c).then_inc(normed, 1)


def weighted_layers(nc, new, d):
    SL = SLABS
    with ExitStack() as ctx:
        def sb(name, shape, dt):
            return ctx.enter_context(nc.sbuf_tensor("wl_" + name, shape, dt))

        def sem(name):
            return new("wl_" + name)

        psum, ident, h = d["psum"], d["ident"], d["h"]
        slab = counts_slab(d)
        g = [sb("g1", [P, NT, D], F32), sb("g2", [P, NT, D], F32)]
        w = [sb("w1", [D, D], F32), sb("w2", [D, D], F32)]
        b = [sb("b1", [P, D], F32), sb("b2", [P, D], F32)]
        hT = sb("hT", [P, GT * P], F32)
        aggT = sb("aggT", [P, 2, GT * P], F32)
        out = sb("out", [P, GT, D], F32)
        x = sb("x", [P, GT, D], F32)

        w_in, slab_in = sem("w_in"), [sem(f"slab_in{i}") for i in range(SL)]
        ht_psum, ht_sb, p_psum, scaled = sem("ht_psum"), sem("ht_sb"), sem("p_psum"), sem("scaled")
        summed, agg_sb, t_psum, combined, relued = (sem("summed"), sem("agg_sb"), sem("t_psum"), sem("combined"),
                                                    sem("relued"))
        x_in, x_ready, stored = sem("x_in"), sem("x_ready"), sem("stored")
        dve_sem = sem("dve")

        with nc.Block() as block:
            @block.sync
            def _(sp):
                for k in range(2):
                    sp.dma_start(w[k][:, :], d[f"L3_W{k + 1}"]).then_inc(w_in, 16)
                    sp.dma_start(b[k][:, :], d[f"L3_b{k + 1}"].rearrange("(a f) -> a f", a=1).broadcast_to([P, D])
                                 ).then_inc(w_in, 16)
                for n in range(2 * G):
                    c = n % G
                    m = min(WG, J - c * WG)
                    if n >= SL:
                        sp.wait_ge(summed, n - SL + 1)
                    sp.dma_start(slab[:, n % SL, 0:m, :], d["aw"][c * WG:c * WG + m].rearrange("j p k -> p j k")
                                 ).then_inc(slab_in[n % SL], 16)
                for c in range(G):
                    m = len(tiles_of(c))
                    if c >= 1:
                        sp.wait_ge(stored, 16 * c)
                    sp.dma_start(x[:, 0:m], group_ap(d["x3"], c)).then_inc(x_in, 16)
                    sp.wait_ge(x_ready, c + 1)
                    if c < G - 1:
                        sp.dma_start(group_ap(d["out"], c), x[:, 0:m]).then_inc(stored, 16)
                    else:
                        rows = N - c * GT * P
                        sp.dma_start(d["out"][c * GT * P:N, :], x[0:rows, 0, :]).then_inc(stored, 16)
                sp.wait_ge(stored, 16 * G)

            @block.tensor
            def _(pe):
                def transposed(m, source):
                    c = m % G
                    k = m // G
                    if m >= 1:
                        pe.wait_ge(ht_sb, m)
                    for i, t in enumerate(tiles_of(c)):
                        src = h[:, t, :] if k == 0 else out[:, i, :]
                        last = nc.tensor.transpose(psum[:, 1, i * P:(i + 1) * P], src, ident[:, :])
                    last.then_inc(ht_psum, 1)

                def product(m):
                    c, k = m % G, m // G
                    pe.wait_ge(ht_sb, m + 1)
                    if m >= 1:
                        pe.wait_ge(scaled, m)
                    for i in range(len(tiles_of(c))):
                        last = nc.tensor.matmul(psum[:, 3, i * D:(i + 1) * D], hT[:, i * P:(i + 1) * P], w[k][:, :],
                                                start=True, stop=True)
                    last.then_inc(p_psum, 1)

                def sum_group(n):
                    c, k = n % G, n // G
                    m = min(WG, J - c * WG)
                    pe.wait_ge(slab_in[n % SL], 16 * (n // SL + 1))
                    if n >= 1:
                        pe.wait_ge(agg_sb, n)
                    for t in range(NT):
                        last = nc.tensor.matmul(psum[:, 0, 0:m * W], g[k][:, t, :],
                                                slab[:, n % SL, 0:m, t * W:(t + 1) * W], start=(t == 0),
                                                stop=(t == NT - 1))
                    last.then_inc(summed, 1)

                def back(n):
                    pe.wait_ge(agg_sb, n + 1)
                    if n >= 1:
                        pe.wait_ge(combined, n)
                    for i in range(len(tiles_of(n % G))):
                        last = nc.tensor.transpose(psum[:, 2, i * P:(i + 1) * P], aggT[:, n % 2, i * P:(i + 1) * P],
                                                   ident[:, :])
                    last.then_inc(t_psum, 1)

                pe.wait_ge(w_in, 64)
                for m in range(G):
                    transposed(m, h)
                    product(m)
                pe.wait_ge(scaled, G)
                for c in range(G + 1):
                    if c < G:
                        sum_group(c)
                    if c >= 1:
                        back(c - 1)
                        pe.wait_ge(relued, c)
                        transposed(G + c - 1, out)
                        product(G + c - 1)
                pe.wait_ge(scaled, 2 * G)
                for c in range(G + 1):
                    if c < G:
                        sum_group(G + c)
                    if c >= 1:
                        back(G + c - 1)

            @block.scalar
            def _(act):
                def copy_t(m):
                    n = len(tiles_of(m % G)) * P
                    act.wait_ge(ht_psum, m + 1)
                    if m >= 1:
                        act.wait_ge(p_psum, m)
                    nc.scalar.copy(hT[:, 0:n], psum[:, 1, 0:n]).then_inc(ht_sb, 1)

                def copy_sums(n):
                    c = n % G
                    m = min(GT * P, NCOL - c * GT * P)
                    act.wait_ge(summed, n + 1)
                    if n >= 2:
                        act.wait_ge(t_psum, n - 1)
                    nc.scalar.copy(aggT[:, n % 2, 0:m], psum[:, 0, 0:m]).then_inc(agg_sb, 1)

                for m in range(G):
                    copy_t(m)
                for c in range(G + 1):
                    if c < G:
                        copy_sums(c)
                    if c >= 1:
                        n = len(tiles_of(c - 1))
                        act.wait_ge(combined, c)
                        nc.scalar.activation(out[:, 0:n], out[:, 0:n], ACT.Relu).then_inc(relued, 1)
                        copy_t(G + c - 1)
                for c in range(G):
                    copy_sums(G + c)

            @block.vector
            def _(dve):
                link = linker(dve, dve_sem)
                dinv = d["dinv"]

                def scale(m):
                    c, k = m % G, m // G
                    dve.wait_ge(p_psum, m + 1)
                    for i, t in enumerate(tiles_of(c)):
                        last = nc.vector.tensor_scalar(g[k][:, t, :], psum[:, 3, i * D:(i + 1) * D],
                                                       dinv[:, t:t + 1], None, ALU.mult)
                    last.then_inc(scaled, 1)

                def combine(n):
                    c, k = n % G, n // G
                    m = len(tiles_of(c))
                    t0 = tiles_of(c)[0]
                    dve.wait_ge(t_psum, n + 1)
                    if 1 <= n <= G:
                        dve.wait_ge(ht_psum, G + n)
                    link(nc.vector.tensor_tensor(out[:, 0:m], psum[:, 2, 0:m * D].rearrange("p (t f) -> p t f", f=D),
                                                 g[k][:, t0:t0 + m], ALU.add))
                    for i, t in enumerate(tiles_of(c)):
                        last = nc.vector.scalar_tensor_tensor(out=out[:, i, :], in0=out[:, i, :],
                                                              scalar=dinv[:, t:t + 1], in1=b[k][:, :],
                                                              op0=ALU.mult, op1=ALU.add)
                    link(last)
                    dve.sem_inc(combined, 1)

                dve.wait_ge(w_in, 64)
                for m in range(G):
                    scale(m)
                for c in range(G):
                    combine(c)
                    scale(G + c)
                for c in range(G):
                    m = len(tiles_of(c))
                    combine(G + c)
                    dve.wait_ge(x_in, 16 * (c + 1))
                    link(nc.vector.tensor_tensor(x[:, 0:m], x[:, 0:m], out[:, 0:m], ALU.add))
                    dve.sem_inc(x_ready, 1)


def load_crowded(nc, d):
    flag = d["starts"][0:1, J + 1:J + 2]
    d["crowded"] = {}
    with nc.Block() as block:
        @block.sync
        def _(sp):
            d["crowded"]["SP"] = sp.value_load(flag, min_val=0, max_val=E + J)

        @block.gpsimd
        def _(pool):
            d["crowded"]["Pool"] = pool.value_load(flag, min_val=0, max_val=E + J)

        @block.vector
        def _(dve):
            d["crowded"]["DVE"] = dve.value_load(flag, min_val=0, max_val=E + J)

        @block.scalar
        def _(act):
            d["crowded"]["Activation"] = act.value_load(flag, min_val=0, max_val=E + J)

        @block.tensor
        def _(pe):
            d["crowded"]["PE"] = pe.value_load(flag, min_val=0, max_val=E + J)


def build(nc, d):
    with ExitStack() as ctx:
        held = []

        def new(name):
            held.append(nc.alloc_semaphore(name=name))
            return held[-1]

        def end_phase():
            nc.all_engine_barrier()
            nc.clear_and_free_semaphores(held)
            nc.all_engine_barrier()
            held.clear()

        def keep(name, shape, dt):
            d[name] = ctx.enter_context(nc.sbuf_tensor(name, shape, dt))

        d["psum"] = ctx.enter_context(nc.psum_tensor("psum", [P, 8, 512], F32))
        keep("ident", [P, P], F32)
        keep("ones", [P, P], F32)
        keep("eps", [P, 1], F32)
        keep("starts", [1, J + 2], I32)
        keep("inv_deg", [P, NT], F32)
        keep("eps_deg", [P, NT], F32)
        keep("dinv", [P, NT], F32)
        made = new("ident_made")
        with nc.Block() as block:
            @block.gpsimd
            def _(pool):
                nc.gpsimd.memset(d["ident"][:, :], 0.0).then_inc(made, 1)
                nc.gpsimd.memset(d["ones"][:, :], 1.0).then_inc(made, 1)
                nc.gpsimd.memset(d["eps"][:, :], LN_EPS).then_inc(made, 1)
                pool.wait_ge(made, 3)
                nc.gpsimd.affine_select(out=d["ident"][:, :], in_=d["ident"][:, :], compare_op=ALU.not_equal, fill=1.0,
                                        base=0, pattern=[[-1, P]], channel_multiplier=1).then_inc(made, 1)
                pool.wait_ge(made, 4)
        prepare(nc, new, d)
        end_phase()
        load_crowded(nc, d)
        keep("adj", [P, NT, NCOL], F16)
        edge_pass(nc, new, d)
        end_phase()
        crowded_edge_pass(nc, new, d)
        end_phase()
        keep("h", [P, NT, D], F32)
        first_tail(nc, new, d)
        end_phase()
        with ExitStack() as split:
            d["parts"] = split.enter_context(nc.sbuf_tensor("parts", [P, 3, NT, D], BF16))
            wide_layer(nc, new, d)
            end_phase()
            narrow_layer(nc, new, d)
            end_phase()
            out_layer(nc, new, d)
            end_phase()
            for number in range(3):
                norm_layer(nc, new, d, number, 3)
                end_phase()
        weighted_layers(nc, new, d)


def kernel(**inputs):
    import numpy as np
    import concourse.bacc as bacc
    from concourse.bass_utils import run_bass_kernel_spmd

    arr = {k: np.ascontiguousarray(v) for k, v in inputs.items()}

    def padded(a, n, value):
        return np.concatenate([a, np.full((n - a.shape[0],) + a.shape[1:], value, a.dtype)])

    send = {
        "x": padded(arr["x"], NPAD, 0),
        "src": padded(arr["src"], EPAD, 0),
        "dst": padded(arr["dst"], EPAD + P, FAR),
        "w": padded(arr["edge_weight"], EPAD, 0),
        "ea": np.ascontiguousarray(padded(arr["edge_attr_32"], EPAD, 0).T),
        "L0_W1": np.ascontiguousarray(arr["L0_gnn_W1"].T),
        "L0_b1": arr["L0_gnn_b1"],
        "L0_W2": np.ascontiguousarray(arr["L0_gnn_W2"].T),
        "L0_Wu": np.ascontiguousarray(arr["L0_gnn_Wu"].T),
        "L2_Wl": np.ascontiguousarray(arr["L2_gnn_Wl"].transpose(0, 2, 1)),
        "L2_Wr": np.ascontiguousarray(arr["L2_gnn_Wr"].transpose(0, 2, 1)),
    }
    for name in ("L0_b2", "L0_bu", "L0_gamma", "L0_beta", "L1_b1", "L1_b2", "L1_b3", "L2_bl", "L3_W1", "L3_b1",
                 "L3_W2", "L3_b2"):
        send[name] = arr[name.replace("_", "_gnn_")]
    for name in ("L1_W1l", "L1_W1r", "L1_W2l", "L1_W2r", "L1_W3l", "L1_W3r"):
        send[name] = np.ascontiguousarray(arr[name.replace("_", "_gnn_")].T)
    nc = bacc.Bacc("TRN2", target_bir_lowering=False, num_devices=1)
    d = {k: nc.dram_tensor("in_" + k, v.shape, mybir.dt.from_np(v.dtype), kind="ExternalInput").ap()
         for k, v in send.items()}
    for name, shape in (("records", (EPAD, REC)), ("dst_row", (EPAD,)), ("h0", (NPAD, D)), ("P", (NPAD, D)),
                        ("Q", (NPAD, D)), ("aw", (J, P, NKEY)), ("counts", (J, P, NKEY)),
                        ("P_src", (-(-E // BLK) * BLK, D)),
                        ("agg", (D, NPAD)), ("deg", (4, NPAD)),
                        ("x1", (NPAD, D)), ("x2", (NPAD, D)), ("x3", (NPAD, D))):
        d[name] = nc.dram_tensor("dram_" + name, shape, F32, kind="Internal").ap()
    d["out"] = nc.dram_tensor("out", (N, D), F32, kind="ExternalOutput").ap()
    build(nc, d)
    r = run_bass_kernel_spmd(nc, [{"in_" + k: v for k, v in send.items()}], core_ids=[0])
    return r.results[0]["out"]
```

```python
from contextlib import ExitStack

import concourse.bass as bass
from concourse import mybir

F32 = mybir.dt.float32
F16 = mybir.dt.float16
BF16 = mybir.dt.bfloat16
I32 = mybir.dt.int32
ALU = mybir.AluOpType
ACT = mybir.ActivationFunctionType
AX = mybir.AxisListType

P = 128
N = 3125
E = 103125
D = 128
ED = 32
NT = (N + P - 1) // P
NPAD = NT * P
W = 16
J = (N + W - 1) // W
NCOL = J * W
CH = 5
BLK = CH * P
CP = -(-(E + BLK) // P)
CP += CP % 2
EPAD = CP * P
NKEY = W * NT
FAR = 4000
REC = 8
R_KEY, R_D25, R_LO, R_W1, R_W2, R_W3, R_ONE, R_SRC = range(REC)
GT = 4
G = (NT + GT - 1) // GT
WG = GT * P // W
SLABS = 3
H1, M2 = 2 * D, 48
UNROLL = 7
LN_EPS = 1e-5
L2_EPS = 1e-12


def prepare(nc, new, d):
    with ExitStack() as ctx:
        def sb(name, shape, dt):
            return ctx.enter_context(nc.sbuf_tensor(name, shape, dt))

        dst_i = sb("dst_i", [P, CP], I32)
        nxt_i = sb("nxt_i", [P, CP], I32)
        src_i = sb("src_i", [P, CP], I32)
        hi_i = sb("hi_i", [P, CP], I32)
        lo_i = sb("lo_i", [P, CP], I32)
        win = sb("win", [P, CP], F16)
        win_next = sb("win_next", [P, CP], F16)
        junk = sb("junk", [P, 2, CP], F16)
        w_sb = sb("w_sb", [P, CP], F32)
        w_rest = sb("w_rest", [P, CP], F32)
        w_hi = sb("w_hi", [P, CP], BF16)
        w_mid = sb("w_mid", [P, CP], BF16)
        dst_f = sb("dst_f", [P, CP], F32)
        rec = sb("rec", [P, CP, REC], F32)
        counts = sb("counts", [P, J + 2], F32)
        thresholds = sb("thresholds", [P, J + 1], F32)
        ones = sb("prep_ones", [P, P], F32)
        starts_f = sb("starts_f", [1, J + 2], F32)
        over = sb("over", [1, J], F32)
        x = sb("x_all", [P, NT, D], F32)
        h = sb("h0_all", [P, NT, D], F32)
        pq = sb("pq", [P, 2, NT, D], F32)
        hT = sb("hT", [P, 2, P], F32)
        w_ab = sb("w_ab", [D, 2 * D], F32)
        b1 = sb("b1_row", [1, D], F32)
        stats = sb("stats", [P, NT, 6], F32)
        mv = sb("mv", [P, NT, 2], F32)
        std = sb("std", [P, NT], F32)
        rstd = sb("rstd", [P, NT], F32)
        eps = sb("prep_eps", [P, 1], F32)

        edges_in, x_in, w_in = new("edges_in"), new("x_in"), new("wab_in")
        shifted, counted = new("shifted"), new("counted")
        recs, pool_step = new("recs_built"), new("pool_step")
        consts = new("prep_consts")
        started, start_row, over_row = new("starts_psum"), new("start_row"), new("over_row")
        varied, stded, normed, h_ready = new("varied"), new("stded"), new("normed"), new("h_ready")
        ht_psum, ht_sb, pq_psum, pq_sb = new("ht_psum"), new("ht_sb"), new("pq_psum"), new("pq_sb")
        stored = new("prep_stored")
        compared = new("windows_compared")
        dve_step = new("prep_dve_step")

        with nc.Block() as block:
            @block.sync
            def _(sp):
                for dst, src in ((dst_i, d["dst"][0:EPAD]), (nxt_i, d["dst"][1:EPAD + 1]),
                                 (src_i, d["src"][0:EPAD]), (w_sb, d["w"][0:EPAD])):
                    sp.dma_start(dst[:, :], src.rearrange("(p c) -> p c", p=P)).then_inc(edges_in, 16)
                sp.dma_start(x[:, :, :], d["x"].rearrange("(t p) f -> p t f", p=P)).then_inc(x_in, 16)
                sp.dma_start(w_ab[:, 0:D], d["L0_W1"][0:D, :]).then_inc(w_in, 16)
                sp.dma_start(w_ab[:, D:2 * D], d["L0_W1"][D:2 * D, :]).then_inc(w_in, 16)
                sp.dma_start(b1[:, :], d["L0_b1"].rearrange("(a f) -> a f", a=1)).then_inc(w_in, 16)
                sp.wait_ge(recs, 1)
                sp.dma_start(d["records"].rearrange("(p c) k -> p c k", p=P), rec[:, :, :]).then_inc(stored, 16)
                sp.dma_start(d["dst_row"].rearrange("(p c) -> p c", p=P), dst_f[:, :]).then_inc(stored, 16)
                sp.wait_ge(h_ready, NT)
                sp.dma_start(d["h0"].rearrange("(t p) f -> p t f", p=P), h[:, :, :]).then_inc(stored, 16)
                sp.wait_ge(pq_sb, NT)
                sp.dma_start(d["P"].rearrange("(t p) f -> p t f", p=P), pq[:, 0]).then_inc(stored, 16)
                sp.dma_start(d["Q"].rearrange("(t p) f -> p t f", p=P), pq[:, 1]).then_inc(stored, 16)
                sp.wait_ge(stored, 80)

            @block.gpsimd
            def _(pool):
                steps = [0]

                def step(ins):
                    steps[0] += 1
                    ins.then_inc(pool_step, 1)
                    pool.wait_ge(pool_step, steps[0])

                nc.gpsimd.memset(ones[:, :], 1.0).then_inc(consts, 1)
                nc.gpsimd.memset(eps[:, :], LN_EPS).then_inc(consts, 1)
                nc.gpsimd.iota(thresholds[:, :], [[1, J + 1]], base=0, channel_multiplier=0,
                               allow_small_or_imprecise_dtypes=True).then_inc(consts, 1)
                nc.gpsimd.memset(rec[:, :, R_ONE], 1.0)
                pool.wait_ge(edges_in, 64)
                nc.gpsimd.tensor_copy(rec[:, :, R_SRC].bitcast(I32), src_i[:, :])
                step(nc.gpsimd.tensor_copy(dst_f[:, :], dst_i[:, :]))
                step(nc.gpsimd.tensor_scalar(rec[:, :, R_D25], dst_f[:, :], float(NT), None, ALU.mult))
                step(nc.gpsimd.tensor_copy(w_hi[:, :], w_sb[:, :]))
                nc.gpsimd.tensor_copy(rec[:, :, R_W1], w_hi[:, :])
                step(nc.gpsimd.tensor_tensor(w_rest[:, :], w_sb[:, :], w_hi[:, :], ALU.subtract))
                step(nc.gpsimd.tensor_copy(w_mid[:, :], w_rest[:, :]))
                nc.gpsimd.tensor_copy(rec[:, :, R_W2], w_mid[:, :])
                step(nc.gpsimd.tensor_tensor(rec[:, :, R_W3], w_rest[:, :], w_mid[:, :], ALU.subtract))
                pool.wait_ge(shifted, 1)
                nc.gpsimd.tensor_copy(rec[:, :, R_LO], lo_i[:, :])
                step(nc.gpsimd.tensor_copy(w_rest[:, :], hi_i[:, :]))
                step(nc.gpsimd.tensor_tensor(rec[:, :, R_KEY], rec[:, :, R_D25], w_rest[:, :], ALU.add))
                pool.drain().then_inc(recs, 1)

            @block.vector
            def _(dve):
                steps = [0]

                def step(ins):
                    steps[0] += 1
                    ins.then_inc(dve_step, 1)
                    dve.wait_ge(dve_step, steps[0])

                dve.wait_ge(x_in, 16)
                for t in range(NT):
                    last = nc.vector.bn_stats(stats[:, t, :], x[:, t, :])
                step(last)
                for t in range(NT):
                    last = nc.vector.bn_aggr(mv[:, t, :], stats[:, t, :])
                last.then_inc(varied, 1)
                dve.wait_ge(edges_in, 64)
                nc.vector.tensor_scalar(lo_i[:, :], src_i[:, :], P - 1, None, ALU.bitwise_and)
                step(nc.vector.tensor_scalar(hi_i[:, :], src_i[:, :], 7, None, ALU.logical_shift_right))
                dve.sem_inc(shifted, 1)
                dve.wait_ge(stded, 1)
                step(nc.vector.reciprocal(rstd[:, :], std[:, :]))
                for t in range(NT):
                    nc.vector.tensor_scalar(h[:, t, :], x[:, t, :], mv[:, t, 0:1], rstd[:, t:t + 1],
                                            ALU.subtract, ALU.mult).then_inc(normed, 1)
                dve.wait_ge(pool_step, 1)
                step(nc.vector.tensor_scalar(dst_i[:, :], dst_i[:, :], 4, None, ALU.logical_shift_right))
                nc.vector.tensor_copy(win[:, :], dst_i[:, :])
                step(nc.vector.tensor_scalar(nxt_i[:, :], nxt_i[:, :], 4, None, ALU.logical_shift_right))
                step(nc.vector.tensor_copy(win_next[:, :], nxt_i[:, :]))
                step(nc.vector.tensor_tensor(junk[:, 0], win_next[:, :], win[:, :], ALU.is_lt))
                step(nc.vector.reduce_sum(counts[:, J + 1:J + 2], junk[:, 0], axis=AX.X))
                dve.wait_ge(consts, 3)
                dve.sem_inc(compared, 2)
                with dve.Fori(0, J // 14) as i:
                    for k in range(14):
                        dve.wait_ge(compared, i * 14 + (k + 1))
                        nc.vector.tensor_scalar(junk[:, k % 2], win[:, :], thresholds[:, bass.ds(i * 14 + k, 1)], 0.0,
                                                       ALU.is_lt, ALU.add, accum_out=counts[:, bass.ds(i * 14 + k, 1)]
                                                       ).then_inc(compared, 1)
                dve.wait_ge(compared, J + 2)
                step(nc.vector.tensor_scalar(junk[:, 0], win[:, :], float(J), 0.0, ALU.is_lt, ALU.add,
                                        accum_out=counts[:, J:J + 1]))
                dve.drain().then_inc(counted, 1)
                dve.wait_ge(started, 1)
                step(nc.vector.tensor_copy(starts_f[:, :], d["psum"][0:1, 7, 0:J + 2]))
                nc.vector.tensor_copy(d["starts"][0:1, 0:J + 1], starts_f[:, 0:J + 1])
                step(nc.vector.tensor_tensor(over[:, :], starts_f[:, 1:J + 1], starts_f[:, 0:J], ALU.subtract))
                step(nc.vector.tensor_scalar(over[:, :], over[:, :], float(BLK), None, ALU.is_gt))
                step(nc.vector.reduce_sum(starts_f[:, 0:1], over[:, :], axis=AX.X))
                step(nc.vector.tensor_tensor(starts_f[:, 1:2], starts_f[:, 0:1], starts_f[:, J + 1:J + 2], ALU.add))
                step(nc.vector.tensor_copy(d["starts"][0:1, J + 1:J + 2], starts_f[:, 1:2]))

            def copy_pq(act, t):
                act.wait_ge(pq_psum, t + 1)
                nc.scalar.copy(pq[:, :, t, :], d["psum"][:, 2 + t % 2, 0:2 * D].rearrange("p (a f) -> p a f", a=2)
                               ).then_inc(pq_sb, 1)

            @block.scalar
            def _(act):
                act.wait_ge(consts, 3)
                act.wait_ge(varied, 1)
                nc.scalar.activation(std[:, :], mv[:, :, 1], ACT.Sqrt, bias=eps[:, 0:1]).then_inc(stded, 1)
                for t in range(NT):
                    act.wait_ge(normed, t + 1)
                    nc.scalar.activation(h[:, t, :], h[:, t, :], ACT.Relu).then_inc(h_ready, 1)
                    if t >= 1:
                        copy_pq(act, t - 1)
                    act.wait_ge(ht_psum, t + 1)
                    if t >= 2:
                        act.wait_ge(pq_psum, t - 1)
                    nc.scalar.copy(hT[:, t % 2, :], d["psum"][:, t % 2, 0:P]).then_inc(ht_sb, 1)
                copy_pq(act, NT - 1)

            @block.tensor
            def _(pe):
                psum, ident = d["psum"], d["ident"]
                pe.wait_ge(w_in, 48)
                pe.wait_ge(consts, 3)
                for t in range(NT + 1):
                    if t < NT:
                        pe.wait_ge(h_ready, t + 1)
                        if t >= 2:
                            pe.wait_ge(ht_sb, t - 1)
                        nc.tensor.transpose(psum[:, t % 2, 0:P], h[:, t, :], ident[:, :]).then_inc(ht_psum, 1)
                    if t >= 1:
                        u = t - 1
                        pe.wait_ge(ht_sb, u + 1)
                        if u >= 2:
                            pe.wait_ge(pq_sb, u - 1)
                        out = psum[:, 2 + u % 2, 0:2 * D]
                        nc.tensor.matmul(out, hT[:, u % 2, :], w_ab[:, :], start=True, stop=False)
                        nc.tensor.matmul(out[:, D:2 * D], ones[0:1, :], b1[:, :], start=False,
                                         stop=True).then_inc(pq_psum, 1)
                pe.wait_ge(counted, 1)
                nc.tensor.matmul(psum[0:1, 7, 0:J + 2], ones[:, 0:1], counts[:, :], start=True,
                                 stop=True).then_inc(started, 1)


def edge_pass(nc, new, d):
    S = 4
    CH_ACT = 4
    with ExitStack() as ctx:
        def sb(name, shape, dt):
            return ctx.enter_context(nc.sbuf_tensor(name, shape, dt))

        adj, psum = d["adj"], d["psum"]
        rec = sb("win_rec", [P, S, CH * REC], F32)
        lhs = sb("lhs", [ED + W, 2, BLK], F32)
        rhs = sb("rhs", [ED + W, S, D], F32)
        dst_row = sb("dst_rows", [ED + W, 2, BLK], F32)
        msg = sb("msg", [P, S, CH, D], F32)
        key = sb("key", [P, S, CH, 2], F32)
        wts = sb("wts", [P, S, CH, 4], BF16)
        hot_d = sb("hot_d", [P, S, CH, W], F32)
        hot_db = sb("hot_db", [P, S, CH, W], BF16)
        hot_lo = sb("hot_lo", [P, 2, CH, 4, P], BF16)
        hot_key = sb("hot_key", [P, 2, CH, NKEY], BF16)
        aw_out = sb("aw_out", [P, S, NKEY], F32)
        agg_win = sb("agg_win", [P, S, W], F32)
        deg_win = sb("deg_win", [4, S, W], F32)
        key0 = sb("key0", [P, J], F32)
        dst_of = sb("dst_of", [P, J], F32)
        iota_d = sb("iota_d", [P, W], F32)
        iota_lo = sb("iota_lo", [P, P], BF16)
        iota_key = sb("iota_key", [P, NKEY], F16)

        consts, w_in = new("edge_consts"), new("w1c_in")
        rec_in = [new(f"rec_in{s}") for s in range(S)]
        lhs_in = [new(f"lhs_in{s}") for s in range(S)]
        gathered = [new(f"gathered{s}") for s in range(S)]
        agg_stored = [new(f"agg_stored{s}") for s in range(S)]
        aw_stored = [new(f"aw_stored{s}") for s in range(S)]
        keyed, hots, hot_t, summed = new("keyed"), new("hots"), new("hot_t"), new("summed")
        multiplied, pre, sums = new("multiplied"), new("pre"), new("sums")
        relued, adj_out, agg_out = new("relued"), new("adj_out"), new("agg_out")
        hot_los, weighted = new("hot_los"), new("weighted")
        pace = new("edge_pace")

        def counts_of(u):
            return psum[:, u % 2, 0:NKEY]

        def weights_of(u):
            return psum[:, 2 + u % 2, 0:NKEY]

        def pre_of(k):
            return psum[:, 4 + k // 4, (k % 4) * D:(k % 4 + 1) * D]

        def await_count(eng, sem, count):
            if not isinstance(count, int):
                eng.wait_ge(sem, count)
                eng.sem_inc(pace, 1)
            elif count > 0:
                eng.wait_ge(sem, count)

        def uses(j, s, n):
            return (j - s) * (n // S)

        def by_window(eng, step):
            for j in range(2 * S):
                step(j, j % S)
            with eng.Fori(2, J // S) as i:
                for s in range(S):
                    step(i * S + s, s)

        def before(s):
            return (s - 1) % S

        with nc.Block() as block:
            @block.sync
            def _(sp):
                def store(j, s):
                    await_count(sp, adj_out, j + 1)
                    await_count(sp, agg_out, j + 1)
                    sp.dma_start(d["aw"][bass.ds(j, 1)].rearrange("a p k -> p (a k)"),
                                 aw_out[:, s, :]).then_inc(aw_stored[s], 16)
                    sp.dma_start(d["agg"][:, bass.ds(j * W, W)],
                                 agg_win[:, s, :]).then_inc(agg_stored[s], 16)
                    sp.dma_start(d["deg"][:, bass.ds(j * W, W)],
                                 deg_win[:, s, :]).then_inc(agg_stored[s], 16)

                def load(j, s):
                    start = sp.value_load(d["starts"][0:1, bass.ds(j, 1)], min_val=0, max_val=E)
                    if not isinstance(j, int) or j >= S:
                        store(j - S, s)
                    sp.dma_start(rec[:, s, :], d["records"][bass.ds(start, BLK), :].rearrange(
                        "(p k) c -> p (k c)", p=P)).then_inc(rec_in[s], 16)
                    await_count(sp, pre, j - 1)
                    sp.dma_start(lhs[0:ED, s % 2, :], d["ea"][:, bass.ds(start, BLK)]).then_inc(lhs_in[s], 16)
                    sp.dma_start(dst_row[ED:ED + W, s % 2, :], d["dst_row"][bass.ds(start, BLK)].rearrange(
                        "(a e) -> a e", a=1).broadcast_to([W, BLK])).then_inc(lhs_in[s], 16)
                    sp.dma_start(rhs[ED:ED + W, s, :], d["Q"][bass.ds(j * W, W), :]).then_inc(lhs_in[s], 16)

                with sp.If(d["crowded"]["SP"] < 1):
                    for s in range(S):
                        sp.dma_start(rhs[0:ED, s, :], d["L0_W1"][2 * D:2 * D + ED, :]).then_inc(w_in, 16)
                    by_window(sp, load)
                    for s in range(S):
                        store(J - S + s, s)
                    for s in range(S):
                        sp.wait_ge(aw_stored[s], 16 * (J // S))
                        sp.wait_ge(agg_stored[s], 32 * (J // S))

            @block.gpsimd
            def _(pool):
                nc.gpsimd.iota(key0[:, :], [[NKEY, J]], base=0, channel_multiplier=0,
                               allow_small_or_imprecise_dtypes=True).then_inc(consts, 1)
                nc.gpsimd.iota(dst_of[:, :], [[W, J]], base=-ED, channel_multiplier=1,
                               allow_small_or_imprecise_dtypes=True).then_inc(consts, 1)
                nc.gpsimd.iota(iota_d[:, :], [[NT, W]], base=0, channel_multiplier=0,
                               allow_small_or_imprecise_dtypes=True).then_inc(consts, 1)
                nc.gpsimd.iota(iota_lo[:, :], [[1, P]], base=0, channel_multiplier=0,
                               allow_small_or_imprecise_dtypes=True).then_inc(consts, 1)
                nc.gpsimd.iota(iota_key[:, :], [[1, NKEY]], base=0, channel_multiplier=0,
                               allow_small_or_imprecise_dtypes=True).then_inc(consts, 1)

                def gather(j, s):
                    await_count(pool, rec_in[s], uses(j, s, 16) + 16)
                    await_count(pool, sums, j - S + 1)
                    for k in range(CH):
                        at = k * REC + R_SRC
                        nc.gpsimd.indirect_dma_start(
                            msg[:, s, k, :], None, d["P"],
                            bass.IndirectOffsetOnAxis(ap=rec[:, s, at:at + 1].bitcast(I32), axis=0)
                        ).then_inc(gathered[s], 16)

                with pool.If(d["crowded"]["Pool"] < 1):
                    by_window(pool, gather)

            @block.vector
            def _(dve):
                def one_hots(j, s):
                    u = s % 2
                    row = rec[:, s, :].rearrange("p (k c) -> p k c", c=REC)
                    await_count(dve, rec_in[s], uses(j, s, 16) + 16)
                    await_count(dve, multiplied, j - 1)
                    await_count(dve, sums, j - S + 1)
                    nc.vector.tensor_scalar(key[:, s], row[:, :, 0:2], key0[:, bass.ds(j, 1)], None,
                                            ALU.subtract).then_inc(keyed, 1)
                    nc.vector.tensor_copy(wts[:, s], row[:, :, R_W1:R_ONE + 1])
                    for k in range(CH):
                        lo = row[:, k, R_LO:R_LO + 1]
                        last = nc.vector.tensor_scalar(hot_lo[:, u, k, 0, :], iota_lo[:, :], lo, None, ALU.is_equal)
                    last.then_inc(hot_los, 1)
                    for k in range(CH_ACT, CH):
                        lo = row[:, k, R_LO:R_LO + 1]
                        for q in range(3):
                            nc.vector.tensor_scalar(hot_lo[:, u, k, 1 + q, :], iota_lo[:, :], lo,
                                                    row[:, k, R_W1 + q:R_W1 + q + 1], ALU.is_equal, ALU.mult)
                    await_count(dve, keyed, j + 1)
                    for k in range(CH):
                        nc.vector.tensor_scalar(hot_key[:, u, k, :], iota_key[:, :], key[:, s, k, 0:1], None,
                                                ALU.is_equal)
                    lhs_d = iota_d[:, :].rearrange("p (a w) -> p a w", a=1).broadcast_to([P, CH, W])
                    rhs_d = key[:, s, :, 1:2].broadcast_to([P, CH, W])
                    nc.vector.tensor_tensor(hot_d[:, s], lhs_d, rhs_d, ALU.is_equal)
                    nc.vector.tensor_tensor(hot_db[:, s], lhs_d, rhs_d, ALU.is_equal).then_inc(hots, 1)
                    await_count(dve, lhs_in[s], uses(j, s, 48) + 48)
                    nc.vector.tensor_scalar(lhs[ED:ED + W, s % 2, :], dst_row[ED:ED + W, s % 2, :],
                                            dst_of[ED:ED + W, bass.ds(j, 1)], None, ALU.is_equal).then_inc(hot_t, 1)

                def add(j, s):
                    await_count(dve, pre, j + 1)
                    await_count(dve, gathered[s], uses(j, s, 16 * CH) + 16 * CH)
                    out = msg[:, s].rearrange("p k f -> p (k f)")
                    nc.vector.tensor_tensor(out, psum[:, 4:6, :].rearrange("p b f -> p (b f)")[:, 0:BLK], out,
                                            ALU.add).then_inc(summed, 1)

                def step(j, s):
                    one_hots(j, s)
                    if not isinstance(j, int) or j > 0:
                        add(j - 1, before(s))

                dve.wait_ge(consts, 5)
                with dve.If(d["crowded"]["DVE"] < 1):
                    by_window(dve, step)
                    add(J - 1, S - 1)

            @block.scalar
            def _(act):
                def relu_of(j, s):
                    await_count(act, summed, j + 1)
                    nc.scalar.activation(msg[:, s], msg[:, s], ACT.Relu).then_inc(relued, 1)

                def matrix_out(j, s):
                    await_count(act, multiplied, j + 1)
                    await_count(act, aw_stored[s], uses(j, s, 16))
                    nc.scalar.copy(adj[:, :, bass.ds(j * W, W)], counts_of(s).rearrange("p (w t) -> p t w", t=NT))
                    nc.scalar.copy(aw_out[:, s, :].rearrange("p (t w) -> p t w", w=W),
                                   weights_of(s).rearrange("p (w t) -> p t w", t=NT)).then_inc(adj_out, 1)

                def sums_out(j, s):
                    await_count(act, sums, j + 1)
                    await_count(act, agg_stored[s], uses(j, s, 32))
                    nc.scalar.copy(agg_win[:, s, :], psum[:, 6 + s % 2, 0:W])
                    nc.scalar.copy(deg_win[:, s, :], psum[0:4, 6 + s % 2, 32:32 + W]).then_inc(agg_out, 1)

                def weigh(j, s):
                    row = rec[:, s, :].rearrange("p (k c) -> p k c", c=REC)
                    await_count(act, hot_los, j + 1)
                    for k in range(CH_ACT):
                        for q in range(3):
                            last = nc.scalar.activation(hot_lo[:, s % 2, k, 1 + q, :], hot_lo[:, s % 2, k, 0, :],
                                                        ACT.Copy, scale=row[:, k, R_W1 + q:R_W1 + q + 1])
                    last.then_inc(weighted, 1)

                def step(j, s):
                    weigh(j, s)
                    if not isinstance(j, int) or j > 1:
                        sums_out(j - 2, before(before(s)))
                    if not isinstance(j, int) or j > 0:
                        matrix_out(j - 1, before(s))
                        relu_of(j - 1, before(s))

                with act.If(d["crowded"]["Activation"] < 1):
                    by_window(act, step)
                    sums_out(J - 2, S - 2)
                    matrix_out(J - 1, S - 1)
                    relu_of(J - 1, S - 1)
                    sums_out(J - 1, S - 1)

            @block.tensor
            def _(pe):
                def multiply(j, s):
                    u = s % 2
                    await_count(pe, hots, j + 1)
                    await_count(pe, adj_out, j - 1)
                    for k in range(CH):
                        nc.tensor.matmul(counts_of(s), hot_lo[:, u, k, 0, :], hot_key[:, u, k, :],
                                         start=(k == 0), stop=(k == CH - 1))
                    await_count(pe, weighted, j + 1)
                    for k in range(CH):
                        for q in range(3):
                            last = nc.tensor.matmul(weights_of(s), hot_lo[:, u, k, 1 + q, :], hot_key[:, u, k, :],
                                                    start=(k == 0 and q == 0), stop=(k == CH - 1 and q == 2))
                    last.then_inc(multiplied, 1)
                    await_count(pe, hot_t, j + 1)
                    await_count(pe, summed, j)
                    for k in range(CH):
                        last = nc.tensor.matmul(pre_of(k), lhs[:, s % 2, k:BLK:CH], rhs[:, s, :],
                                                start=True, stop=True)
                    last.then_inc(pre, 1)
                    await_count(pe, agg_out, j - 1)
                    for k in range(CH):
                        nc.tensor.matmul(psum[0:4, 6 + u, 32:32 + W], wts[:, s, k, :], hot_db[:, s, k, :],
                                         start=(k == 0), stop=(k == CH - 1))

                def sum_up(j, s):
                    u = s % 2
                    await_count(pe, relued, j + 1)
                    for k in range(CH):
                        last = nc.tensor.matmul(psum[:, 6 + u, 0:W], msg[:, s, k, :], hot_d[:, s, k, :],
                                                start=(k == 0), stop=(k == CH - 1))
                    last.then_inc(sums, 1)

                def step(j, s):
                    multiply(j, s)
                    if not isinstance(j, int) or j > 0:
                        sum_up(j - 1, before(s))

                with pe.If(d["crowded"]["PE"] < 1):
                    pe.wait_ge(w_in, 16 * S)
                    by_window(pe, step)
                    sum_up(J - 1, S - 1)



def crowded_edge_pass(nc, new, d):
    R = -(-E // BLK)
    STEPS = 6
    with ExitStack() as ctx:
        def sb(name, shape, dt):
            return ctx.enter_context(nc.sbuf_tensor("any_" + name, shape, dt))

        def sem(name):
            return new("any_" + name)

        psum = d["psum"]
        rec = sb("rec", [P, CH * REC], F32)
        lhs = sb("lhs", [ED + W, BLK], F32)
        rhs = sb("rhs", [ED + W, D], F32)
        dst_row = sb("dst_row", [ED + W, BLK], F32)
        msg = sb("msg", [P, CH, D], F32)
        key = sb("key", [P, CH, 2], F32)
        wts = sb("wts", [P, CH, 4], BF16)
        hot_d = sb("hot_d", [P, CH, W], F32)
        hot_db = sb("hot_db", [P, CH, W], BF16)
        hot_lo = sb("hot_lo", [P, CH, 4, P], BF16)
        hot_key = sb("hot_key", [P, CH, NKEY], BF16)
        matrix = sb("matrix", [P, 2, NKEY], F32)
        agg_win = sb("agg_win", [P, W], F32)
        deg_win = sb("deg_win", [4, W], F32)
        key0 = sb("key0", [P, J], F32)
        dst_of = sb("dst_of", [P, J], F32)
        iota_d = sb("iota_d", [P, W], F32)
        iota_lo = sb("iota_lo", [P, P], BF16)
        iota_key = sb("iota_key", [P, NKEY], F16)

        consts, w_in, loaded, gathered = sem("consts"), sem("w_in"), sem("loaded"), sem("gathered")
        hots, multiplied, relued, sums = sem("hots"), sem("multiplied"), sem("relued"), sem("sums")
        rec_in, p_stored = sem("rec_in"), sem("p_stored")
        block_done, cleared, stored, out_free = sem("block_done"), sem("cleared"), sem("stored"), sem("out_free")
        dve_step, pace = sem("dve_step"), sem("pace")

        def await_count(eng, sem, count):
            eng.wait_ge(sem, count)
            eng.sem_inc(pace, 1)

        with nc.Block() as block:
            @block.sync
            def _(sp):
                with sp.If(d["crowded"]["SP"] >= 1):
                    sp.dma_start(rhs[0:ED, :], d["L0_W1"][2 * D:2 * D + ED, :]).then_inc(w_in, 16)
                    sp.wait_ge(w_in, 16)
                    sp.sem_inc(out_free, 1)
                    with sp.Fori(0, J) as j:
                        with sp.Fori(0, R) as r:
                            await_count(sp, block_done, j * R + r + 1)
                            sp.dma_start(rec[:, :], d["records"][bass.ds(r * BLK, BLK), :].rearrange(
                                "(p k) c -> p (k c)", p=P)).then_inc(loaded, 16)
                            sp.dma_start(lhs[0:ED, :], d["ea"][:, bass.ds(r * BLK, BLK)]).then_inc(loaded, 16)
                            sp.dma_start(dst_row[ED:ED + W, :], d["dst_row"][bass.ds(r * BLK, BLK)].rearrange(
                                "(a e) -> a e", a=1).broadcast_to([W, BLK])).then_inc(loaded, 16)
                            sp.dma_start(rhs[ED:ED + W, :], d["Q"][bass.ds(j * W, W), :]).then_inc(loaded, 16)
                            sp.dma_start(msg[:, :, :], d["P_src"][bass.ds(r * BLK, BLK), :].rearrange(
                                "(p k) f -> p k f", p=P)).then_inc(loaded, 16)
                        await_count(sp, block_done, (j + 1) * R + 1)
                        sp.dma_start(d["counts"][bass.ds(j, 1)].rearrange("a p k -> p (a k)"),
                                     matrix[:, 0]).then_inc(stored, 16)
                        sp.dma_start(d["aw"][bass.ds(j, 1)].rearrange("a p k -> p (a k)"),
                                     matrix[:, 1]).then_inc(stored, 16)
                        sp.dma_start(d["agg"][:, bass.ds(j * W, W)], agg_win[:, :]).then_inc(stored, 16)
                        sp.dma_start(d["deg"][:, bass.ds(j * W, W)], deg_win[:, :]).then_inc(stored, 16)
                        await_count(sp, stored, (j + 1) * 64)
                        sp.sem_inc(out_free, 1)

            @block.gpsimd
            def _(pool):
                with pool.If(d["crowded"]["Pool"] >= 1):
                    for out, pattern, base, rows in (
                            (key0, [[NKEY, J]], 0, 0), (dst_of, [[W, J]], -ED, 1), (iota_d, [[NT, W]], 0, 0),
                            (iota_lo, [[1, P]], 0, 0), (iota_key, [[1, NKEY]], 0, 0)):
                        nc.gpsimd.iota(out[:, :], pattern, base=base, channel_multiplier=rows,
                                       allow_small_or_imprecise_dtypes=True).then_inc(consts, 1)
                    with pool.Fori(0, R) as r:
                        pool.dma_start(rec[:, :], d["records"][bass.ds(r * BLK, BLK), :].rearrange(
                            "(p k) c -> p (k c)", p=P)).then_inc(rec_in, 16)
                        await_count(pool, rec_in, (r + 1) * 16)
                        for k in range(CH):
                            at = k * REC + R_SRC
                            nc.gpsimd.indirect_dma_start(
                                msg[:, k, :], None, d["P"],
                                bass.IndirectOffsetOnAxis(ap=rec[:, at:at + 1].bitcast(I32), axis=0)
                            ).then_inc(gathered, 16)
                        await_count(pool, gathered, (r + 1) * 16 * CH)
                        pool.dma_start(d["P_src"][bass.ds(r * BLK, BLK), :].rearrange("(p k) f -> p k f", p=P),
                                       msg[:, :, :]).then_inc(p_stored, 16)
                        await_count(pool, p_stored, (r + 1) * 16)
                    pool.sem_inc(block_done, 1)

            @block.vector
            def _(dve):
                def block_of(j, n):
                    steps = [0]

                    def link(ins):
                        steps[0] += 1
                        ins.then_inc(dve_step, 1)
                        await_count(dve, dve_step, n * STEPS + steps[0])

                    row = rec[:, :].rearrange("p (k c) -> p k c", c=REC)
                    await_count(dve, loaded, (n + 1) * 80)
                    nc.vector.tensor_copy(wts[:, :], row[:, :, R_W1:R_ONE + 1])
                    for k in range(CH):
                        lo = row[:, k, R_LO:R_LO + 1]
                        nc.vector.tensor_scalar(hot_lo[:, k, 0, :], iota_lo[:, :], lo, None, ALU.is_equal)
                        for q in range(3):
                            nc.vector.tensor_scalar(hot_lo[:, k, 1 + q, :], iota_lo[:, :], lo,
                                                    row[:, k, R_W1 + q:R_W1 + q + 1], ALU.is_equal, ALU.mult)
                    nc.vector.tensor_scalar(lhs[ED:ED + W, :], dst_row[ED:ED + W, :], dst_of[ED:ED + W, bass.ds(j, 1)],
                                            None, ALU.is_equal)
                    link(nc.vector.tensor_scalar(key[:, :], row[:, :, 0:2], key0[:, bass.ds(j, 1)], None,
                                                 ALU.subtract))
                    for k in range(CH):
                        nc.vector.tensor_scalar(hot_key[:, k, :], iota_key[:, :], key[:, k, 0:1], None,
                                                ALU.is_equal)
                    lhs_d = iota_d[:, :].rearrange("p (a w) -> p a w", a=1).broadcast_to([P, CH, W])
                    rhs_d = key[:, :, 1:2].broadcast_to([P, CH, W])
                    nc.vector.tensor_tensor(hot_d[:, :], lhs_d, rhs_d, ALU.is_equal)
                    link(nc.vector.tensor_tensor(hot_db[:, :], lhs_d, rhs_d, ALU.is_equal))
                    dve.sem_inc(hots, 1)
                    await_count(dve, multiplied, n + 1)
                    out = msg[:, :].rearrange("p k f -> p (k f)")
                    link(nc.vector.tensor_tensor(out, psum[:, 4:6, :].rearrange("p b f -> p (b f)")[:, 0:BLK], out,
                                                 ALU.add))
                    link(nc.vector.tensor_scalar(out, out, 0.0, None, ALU.max))
                    dve.sem_inc(relued, 1)
                    for q in range(2):
                        link(nc.vector.tensor_tensor(
                            matrix[:, q].rearrange("p (t w) -> p t w", w=W), matrix[:, q].rearrange(
                                "p (t w) -> p t w", w=W),
                            psum[:, 2 * q, 0:NKEY].rearrange("p (w t) -> p t w", t=NT), ALU.add))
                    assert steps[0] == STEPS
                    await_count(dve, sums, n + 1)
                    nc.vector.tensor_tensor(agg_win[:, :], agg_win[:, :], psum[:, 6, 0:W], ALU.add)
                    nc.vector.tensor_tensor(deg_win[:, :], deg_win[:, :], psum[0:4, 7, 0:W], ALU.add)
                    dve.drain().then_inc(block_done, 1)
                    await_count(dve, block_done, n + 2)

                with dve.If(d["crowded"]["DVE"] >= 1):
                    dve.wait_ge(consts, 5)
                    with dve.Fori(0, J) as j:
                        await_count(dve, out_free, j + 1)
                        for out in (matrix[:, :], agg_win[:, :], deg_win[:, :]):
                            nc.vector.memset(out, 0.0).then_inc(cleared, 1)
                        await_count(dve, cleared, (j + 1) * 3)
                        with dve.Fori(0, R) as r:
                            block_of(j, j * R + r)

            @block.tensor
            def _(pe):
                with pe.If(d["crowded"]["PE"] >= 1):
                    with pe.Fori(0, J) as j:
                        with pe.Fori(0, R) as r:
                            n = j * R + r
                            await_count(pe, hots, n + 1)
                            for k in range(CH):
                                nc.tensor.matmul(psum[:, 0, 0:NKEY], hot_lo[:, k, 0, :], hot_key[:, k, :],
                                                 start=(k == 0), stop=(k == CH - 1))
                            for k in range(CH):
                                for q in range(3):
                                    nc.tensor.matmul(psum[:, 2, 0:NKEY], hot_lo[:, k, 1 + q, :], hot_key[:, k, :],
                                                     start=(k == 0 and q == 0), stop=(k == CH - 1 and q == 2))
                            for k in range(CH):
                                nc.tensor.matmul(psum[:, 4 + k // 4, (k % 4) * D:(k % 4 + 1) * D], lhs[:, k:BLK:CH],
                                                 rhs[:, :], start=True, stop=True)
                            for k in range(CH):
                                last = nc.tensor.matmul(psum[0:4, 7, 0:W], wts[:, k, :], hot_db[:, k, :],
                                                        start=(k == 0), stop=(k == CH - 1))
                            last.then_inc(multiplied, 1)
                            await_count(pe, relued, n + 1)
                            for k in range(CH):
                                last = nc.tensor.matmul(psum[:, 6, 0:W], msg[:, k, :], hot_d[:, k, :],
                                                        start=(k == 0), stop=(k == CH - 1))
                            last.then_inc(sums, 1)


def counts_slab(d):
    return d["adj"][:, :, :].rearrange("p t n -> p (t n)").bitcast(F32)[:, 0:SLABS * WG * NKEY].rearrange(
        "p (s j k) -> p s j k", s=SLABS, k=NKEY)


def h_copy(d):
    return counts_slab(d)[:, SLABS - 1].rearrange("p j k -> p (j k)")[:, 0:NT * D].rearrange("p (t f) -> p t f", f=D)


def tiles_of(c):
    return range(c * GT, min((c + 1) * GT, NT))


def linker(eng, sem):
    count = [0]

    def link(ins):
        count[0] += 1
        ins.then_inc(sem, 1)
        eng.wait_ge(sem, count[0])

    return link


def group_ap(dram, c):
    t0, t1 = tiles_of(c)[0], tiles_of(c)[-1] + 1
    return dram[t0 * P:t1 * P, :].rearrange("(t p) f -> p t f", p=P)


class Norm:

    def __init__(self, nc, new, sb, name):
        self.nc = nc
        self.stats = sb(name + "_stats", [P, GT, 6], F32)
        self.mv = sb(name + "_mv", [P, GT, 2], F32)
        self.std = sb(name + "_std", [P, GT], F32)
        self.varied, self.rooted = new(name + "_varied"), new(name + "_rooted")

    def on_vector(self, dve, link, out, x, c):
        nc, n = self.nc, len(tiles_of(c))
        for i in range(n):
            last = nc.vector.bn_stats(self.stats[:, i, :], x[:, i, :])
        link(last)
        for i in range(n):
            last = nc.vector.bn_aggr(self.mv[:, i, :], self.stats[:, i, :])
        last.then_inc(self.varied, 1)
        dve.wait_ge(self.rooted, c + 1)
        link(nc.vector.reciprocal(self.std[:, 0:n], self.std[:, 0:n]))
        for i in range(n):
            last = nc.vector.tensor_scalar(out[:, i, :], x[:, i, :], self.mv[:, i, 0:1], self.std[:, i:i + 1],
                                           ALU.subtract, ALU.mult)
        return last

    def on_scalar(self, act, eps, c):
        n = len(tiles_of(c))
        act.wait_ge(self.varied, c + 1)
        self.nc.scalar.activation(self.std[:, 0:n], self.mv[:, 0:n, 1], ACT.Sqrt,
                                  bias=eps[:, 0:1]).then_inc(self.rooted, 1)


class Parts:

    def __init__(self, buffer, dt, width, number):
        self.width, self.number, self.block = width, number, width * (4 if width == M2 else number)
        self.flat = (buffer[:, :] if dt == F16 else buffer[:, :].bitcast(BF16))[:, 0:NT * self.block]
        self.tiles = self.flat.rearrange("p (t f) -> p t f", f=self.block)
        self.rows = 2 * width if width == M2 else width
        self.taken = [(0, 2 * width), (2 * width, 2 * width)] if width == M2 else [(q * width, width)
                                                                               for q in range(number)]

    def clear(self, nc, pool, cleared):
        nc.gpsimd.memset(self.of(3, slice(0, NT)), 0.0).then_inc(cleared, 1)
        pool.wait_ge(cleared, 1)

    def of(self, q, tiles):
        return self.tiles[:, tiles, q * self.width:(q + 1) * self.width]


class Split:

    def __init__(self, nc, new, name, v, parts, squares=None, trash=None):
        self.nc, self.v, self.parts, self.squares, self.trash = nc, v, parts, squares, trash
        self.given, self.relued, self.hi = new(name + "_given"), new(name + "_relued"), new(name + "_hi")
        self.rest, self.mid, self.done = new(name + "_rest"), new(name + "_mid"), new(name + "_cut")
        self.squared = new(name + "_squared")

    def on_scalar(self, act, c):
        n, tiles = len(tiles_of(c)), slice(tiles_of(c)[0], tiles_of(c)[-1] + 1)
        v = self.v[:, 0:n, 0:self.parts.width]
        act.wait_ge(self.given, c + 1)
        self.nc.scalar.activation(v, v, ACT.Relu).then_inc(self.relued, 1)
        act.wait_ge(self.relued, c + 1)
        self.nc.scalar.copy(self.parts.of(0, tiles), v).then_inc(self.hi, 1)
        if self.squares is not None:
            for i, t in enumerate(tiles_of(c)):
                if t:
                    act.wait_ge(self.squared, t)
                self.nc.scalar.activation(self.trash[:, :], v[:, i, :], ACT.Square,
                                          accum_out=self.squares[:, t:t + 1]).then_inc(self.squared, 1)
        if self.parts.number == 3:
            act.wait_ge(self.rest, c + 1)
            self.nc.scalar.copy(self.parts.of(1, tiles), v).then_inc(self.mid, 1)

    def on_vector(self, dve, c):
        n, tiles = len(tiles_of(c)), slice(tiles_of(c)[0], tiles_of(c)[-1] + 1)
        v = self.v[:, 0:n, 0:self.parts.width]
        sub = self.nc.vector.tensor_tensor
        dve.wait_ge(self.hi, c + 1)
        if self.squares is not None:
            dve.wait_ge(self.squared, tiles_of(c)[-1] + 1)
        if self.parts.number == 2:
            sub(self.parts.of(1, tiles), v, self.parts.of(0, tiles), ALU.subtract).then_inc(self.done, 1)
        else:
            sub(v, v, self.parts.of(0, tiles), ALU.subtract).then_inc(self.rest, 1)
            dve.wait_ge(self.mid, c + 1)
            sub(self.parts.of(2, tiles), v, self.parts.of(1, tiles), ALU.subtract).then_inc(self.done, 1)
        dve.wait_ge(self.done, c + 1)


def first_tail(nc, new, d):
    with ExitStack() as ctx:
        def sb(name, shape, dt):
            return ctx.enter_context(nc.sbuf_tensor(name, shape, dt))

        psum, ident, ones = d["psum"], d["ident"], d["ones"]
        free = d["parts_b"][:, :].bitcast(F32)
        deg_rows = free[0:4, 0:NPAD]
        deg_row = free[0:1, NPAD:NPAD + GT * P]
        agg = sb("agg_in", [D, GT * P], F32)
        mT = free[:, NPAD + GT * P:NPAD + 2 * GT * P]
        h0 = sb("h0_in", [P, GT, D], F32)
        x = sb("x_group", [P, GT, D], F32)
        w2, wu = sb("w2", [D, D], F32), sb("wu", [D, D], F32)
        b2, bu = sb("b2_row", [1, D], F32), sb("bu_row", [1, D], F32)
        gamma, beta = sb("gamma_rows", [P, D], F32), sb("beta_rows", [P, D], F32)
        wsum, positive = sb("wsum", [P, NT], F32), sb("positive", [P, NT], F32)
        v = sb("v_group", [P, GT, D], F32)
        split = Split(nc, new, "t_split", v, d["h_out"])
        norm_y, norm_x = Norm(nc, new, sb, "ty"), Norm(nc, new, sb, "tx")

        w_in, deg_in, cleared = new("t_w_in"), new("t_deg_in"), new("t_cleared")
        agg_in, node_in = new("t_agg_in"), new("t_node_in")
        deg_t, wsum_ready, wroot = new("t_deg_t"), new("t_wsum"), new("t_wroot")
        m_psum, m_sb, u_psum = new("t_m_psum"), new("t_m_sb"), new("t_u_psum")
        y_ready, x_ready, x_stored, normed = new("t_y"), new("t_x"), new("t_x_stored"), new("t_normed")
        dve_sem = new("t_dve")

        ident_made = new("t_ident_b")

        with nc.Block() as block:
            @block.gpsimd
            def _(pool):
                nc.gpsimd.tensor_copy(d["ident_b"][:, :], ident[:, :]).then_inc(ident_made, 1)
                pool.wait_ge(ident_made, 1)

            @block.sync
            def _(sp):
                for out, src in ((w2[:, :], d["L0_W2"]), (wu[:, :], d["L0_Wu"])):
                    sp.dma_start(out, src).then_inc(w_in, 16)
                for out, src in ((b2, d["L0_b2"]), (bu, d["L0_bu"])):
                    sp.dma_start(out[:, :], src.rearrange("(a f) -> a f", a=1)).then_inc(w_in, 16)
                for out, src in ((gamma, d["L0_gamma"]), (beta, d["L0_beta"])):
                    sp.dma_start(out[:, :], src.rearrange("(a f) -> a f", a=1).broadcast_to([P, D])
                                 ).then_inc(w_in, 16)
                sp.wait_ge(cleared, 3)
                sp.dma_start(deg_rows[:, 0:NCOL], d["deg"][:, 0:NCOL]).then_inc(deg_in, 16)
                for c in range(G):
                    n = min(GT * P, NCOL - c * GT * P)
                    if c >= 1:
                        sp.wait_ge(m_psum, c)
                    sp.dma_start(agg[:, 0:n], d["agg"][:, c * GT * P:c * GT * P + n]).then_inc(agg_in, 16)
                    sp.dma_start(deg_row[:, 0:n], d["deg"][3:4, c * GT * P:c * GT * P + n]).then_inc(agg_in, 16)
                    if c >= 1:
                        sp.wait_ge(x_ready, c)
                        sp.dma_start(group_ap(d["x1"], c - 1), x[:, 0:len(tiles_of(c - 1))]).then_inc(x_stored, 16)
                        sp.wait_ge(x_stored, 16 * c)
                        sp.wait_ge(normed, c)
                    m = len(tiles_of(c))
                    sp.dma_start(h0[:, 0:m], group_ap(d["h0"], c)).then_inc(node_in, 16)
                    sp.dma_start(x[:, 0:m], group_ap(d["x"], c)).then_inc(node_in, 16)
                sp.wait_ge(x_ready, G)
                sp.dma_start(group_ap(d["x1"], G - 1), x[:, 0:len(tiles_of(G - 1))]).then_inc(x_stored, 16)
                sp.wait_ge(x_stored, 16 * G)

            @block.tensor
            def _(pe):
                pe.wait_ge(deg_in, 16)
                for t in range(NT):
                    last = nc.tensor.transpose(psum[:, 0, 4 * t:4 * t + 4], deg_rows[0:4, t * P:(t + 1) * P],
                                               ident[0:4, 0:4])
                last.then_inc(deg_t, 1)
                pe.wait_ge(w_in, 96)
                for c in range(G):
                    n = len(tiles_of(c)) * P
                    pe.wait_ge(agg_in, 32 * (c + 1))
                    if c >= 1:
                        pe.wait_ge(m_sb, c)
                    nc.tensor.matmul(psum[:, 1, 0:n], w2[:, :], agg[:, 0:n], start=True, stop=False)
                    nc.tensor.matmul(psum[:, 1, 0:n], b2[:, :], deg_row[:, 0:n], start=False,
                                     stop=True).then_inc(m_psum, 1)
                    pe.wait_ge(m_sb, c + 1)
                    if c >= 1:
                        pe.wait_ge(y_ready, c)
                    for i in range(n // P):
                        out = psum[:, 2, i * D:(i + 1) * D]
                        nc.tensor.matmul(out, mT[:, i * P:(i + 1) * P], wu[:, :], start=True, stop=False)
                        last = nc.tensor.matmul(out, ones[0:1, :], bu[:, :], start=False, stop=True)
                    last.then_inc(u_psum, 1)

            @block.scalar
            def _(act):
                act.wait_ge(wsum_ready, 1)
                nc.scalar.activation(wsum[:, :], wsum[:, :], ACT.Sqrt).then_inc(wroot, 1)
                for c in range(G):
                    n = len(tiles_of(c))
                    act.wait_ge(m_psum, c + 1)
                    if c >= 1:
                        act.wait_ge(u_psum, c)
                    nc.scalar.copy(mT[:, 0:n * P], psum[:, 1, 0:n * P]).then_inc(m_sb, 1)
                    norm_y.on_scalar(act, d["eps"], c)
                    norm_x.on_scalar(act, d["eps"], c)
                    split.on_scalar(act, c)

            @block.vector
            def _(dve):
                link = linker(dve, dve_sem)
                nc.vector.memset(deg_rows[:, NCOL:NPAD], 0.0).then_inc(cleared, 1)
                nc.vector.memset(deg_row[:, :], 0.0).then_inc(cleared, 1)
                nc.vector.memset(agg[:, :], 0.0).then_inc(cleared, 1)
                dve.wait_ge(deg_t, 1)
                parts = psum[:, 0, 0:4 * NT].rearrange("p (t q) -> p t q", q=4)
                link(nc.vector.tensor_scalar(d["eps_deg"][:, :], parts[:, :, 3], 1.0, None, ALU.max))
                nc.vector.reciprocal(d["inv_deg"][:, :], d["eps_deg"][:, :])
                link(nc.vector.tensor_scalar(wsum[:, :], parts[:, :, 0], 1.0, None, ALU.add))
                link(nc.vector.tensor_tensor(wsum[:, :], wsum[:, :], parts[:, :, 1], ALU.add))
                link(nc.vector.tensor_tensor(wsum[:, :], wsum[:, :], parts[:, :, 2], ALU.add))
                link(nc.vector.tensor_scalar(d["eps_deg"][:, :], d["eps_deg"][:, :], L2_EPS, None, ALU.mult))
                link(nc.vector.tensor_scalar(positive[:, :], wsum[:, :], 0.0, None, ALU.is_gt))
                nc.vector.tensor_scalar(wsum[:, :], wsum[:, :], 1e-38, None, ALU.max).then_inc(wsum_ready, 1)
                dve.wait_ge(wroot, 1)
                link(nc.vector.reciprocal(d["dinv"][:, :], wsum[:, :]))
                link(nc.vector.tensor_tensor(d["dinv"][:, :], d["dinv"][:, :], positive[:, :], ALU.mult))
                for c in range(G):
                    n = len(tiles_of(c))
                    y = h0[:, 0:n]
                    dve.wait_ge(u_psum, c + 1)
                    dve.wait_ge(node_in, 32 * (c + 1))
                    link(nc.vector.scalar_tensor_tensor(
                        out=y, in0=psum[:, 2, 0:n * D].rearrange("p (t f) -> p t f", f=D), scalar=0.0, in1=y,
                        op0=ALU.max, op1=ALU.add))
                    dve.sem_inc(y_ready, 1)
                    link(norm_y.on_vector(dve, link, y, y, c))
                    for row, op in ((gamma, ALU.mult), (beta, ALU.add)):
                        rows = row[:, :].rearrange("p (a f) -> p a f", a=1).broadcast_to([P, n, D])
                        link(nc.vector.tensor_tensor(y, y, rows, op))
                    link(nc.vector.tensor_tensor(x[:, 0:n], x[:, 0:n], y, ALU.add))
                    dve.sem_inc(x_ready, 1)
                    link(norm_x.on_vector(dve, link, v[:, 0:n], x[:, 0:n], c))
                    dve.sem_inc(normed, 1)
                    dve.sem_inc(split.given, 1)
                    split.on_vector(dve, c)


class Layer:

    def __init__(self, nc, new, d, name, ctx, parts):
        self.nc, self.d, self.name, self.ctx, self.parts = nc, d, name, ctx, parts
        self.new = lambda n: new(name + "_" + n)
        self.psum, self.ident, self.ones = d["psum"], d["ident"], d["ones"]
        self.aggT = self.sb("aggT", [P, 2, GT * P], F32)
        self.hT = self.sb("hT", [P, 2, GT * P], F32)
        self.summed, self.agg_sb, self.agg_read = self.new("summed"), self.new("agg_sb"), self.new("agg_read")
        self.ht_psum, self.ht_sb = self.new("ht_psum"), self.new("ht_sb")
        self.w_in, self.counts_in, self.h_copied = self.new("w_in"), self.new("counts_in"), self.new("h_copied")
        self.dve_sem, self.u_psum, self.combined = self.new("dve"), self.new("u_psum"), self.new("combined")

    def sb(self, name, shape, dt):
        return self.ctx.enter_context(self.nc.sbuf_tensor(self.name + "_" + name, shape, dt))

    def sum_group(self, pe, c):
        with pe.If(self.d["crowded"]["PE"] < 1):
            self.sum_from_adj(pe, c)
        with pe.If(self.d["crowded"]["PE"] >= 1):
            self.sum_from_dram(pe, c)

    def sum_from_dram(self, pe, c):
        if c == 0:
            pe.wait_ge(self.h_copied, self.parts.number)
        pe.wait_ge(self.counts_in, 16 * (c + 1))
        if c >= 1:
            pe.wait_ge(self.agg_sb, c)
        m, rows = min(WG, J - c * WG), self.parts.rows
        for t in range(NT):
            last = self.nc.tensor.matmul(self.psum[0:rows, 0, 0:m * W], h_copy(self.d)[:, t, 0:rows],
                                         counts_slab(self.d)[:, 0, 0:m, t * W:(t + 1) * W], start=(t == 0),
                                         stop=(t == NT - 1))
        last.then_inc(self.summed, 1)

    def load_counts(self, pool):
        every = slice(0, NT)
        copy = h_copy(self.d)
        with pool.If(self.d["crowded"]["Pool"] >= 1):
            self.nc.gpsimd.memset(copy, 0.0).then_inc(self.h_copied, 1)
            for q in range(1, self.parts.number):
                pool.wait_ge(self.h_copied, q)
                first = self.parts.of(0, every) if q == 1 else copy[:, :, 0:self.parts.width]
                self.nc.gpsimd.tensor_tensor(copy[:, :, 0:self.parts.width], first, self.parts.of(q, every),
                                             ALU.add).then_inc(self.h_copied, 1)
            for c in range(G):
                m = min(WG, J - c * WG)
                if c >= 1:
                    pool.wait_ge(self.summed, c)
                pool.dma_start(counts_slab(self.d)[:, 0, 0:m, :], self.d["counts"][c * WG:c * WG + m].rearrange(
                    "j p k -> p j k")).then_inc(self.counts_in, 16)

    def sum_from_adj(self, pe, c):
        nc, adj, parts = self.nc, self.d["adj"], self.parts
        n = min(GT * P, NCOL - c * GT * P)
        flat_adj = adj[:, :, :].rearrange("p t n -> p (t n)")
        last_taken = len(parts.taken) - 1
        if c >= 1:
            pe.wait_ge(self.agg_sb, c)

        def tile_sum(t, start=False, stop=False):
            for q, (at, width) in enumerate(parts.taken):
                last = nc.tensor.matmul(self.psum[0:width, 0, 0:n], parts.flat[:, bass.ds(t * parts.block + at, width)],
                                        flat_adj[:, bass.ds(t * NCOL + c * GT * P, n)], start=start and q == 0,
                                        stop=stop and q == last_taken)
            return last

        rounds = (NT - 2) // UNROLL
        tile_sum(0, start=True)
        with pe.Fori(0, rounds) as i:
            for k in range(UNROLL):
                tile_sum(i * UNROLL + (1 + k))
        for t in range(1 + rounds * UNROLL, NT):
            last = tile_sum(t, stop=(t == NT - 1))
        last.then_inc(self.summed, 1)

    def copy_sums(self, act, c):
        n, rows = min(GT * P, NCOL - c * GT * P), self.parts.rows
        act.wait_ge(self.summed, c + 1)
        if c >= 2:
            act.wait_ge(self.agg_read, c - 1)
        self.nc.scalar.copy(self.aggT[0:rows, c % 2, 0:n], self.psum[0:rows, 0, 0:n]).then_inc(self.agg_sb, 1)

    def transpose_h(self, pe, c):
        transpose_parts(self.nc, self.d, self.parts, pe, c, self.ht_psum, self.ht_sb)

    def copy_ht(self, act, c):
        n, rows = len(tiles_of(c)) * P, self.parts.rows
        act.wait_ge(self.ht_psum, c + 1)
        if c >= 2:
            act.wait_ge(self.u_psum, c - 1)
        self.nc.scalar.copy(self.hT[0:rows, c % 2, 0:n], self.psum[0:rows, 1, 0:n]).then_inc(self.ht_sb, 1)


def transpose_parts(nc, d, parts, pe, c, ht_psum, ht_sb):
    if c >= 1:
        pe.wait_ge(ht_sb, c)
    for i, t in enumerate(tiles_of(c)):
        for q, (at, width) in enumerate(parts.taken):
            last = nc.tensor.matmul(d["psum"][0:width, 1, i * P:(i + 1) * P], parts.tiles[:, t, at:at + width],
                                    d["ident_b"][:, :], start=(q == 0), stop=(q == len(parts.taken) - 1))
    last.then_inc(ht_psum, 1)


def wide_layer(nc, new, d):
    with ExitStack() as ctx:
        L = Layer(nc, new, d, "wide", ctx, d["h_in"])
        psum = L.psum
        w1l, w1r = L.sb("w1l", [D, H1], F32), L.sb("w1r", [D, H1], F32)
        w2 = L.sb("w2", [P, 2, 2 * M2], F32)
        h1T = d["h1T"]
        b2 = L.sb("b2", [1, M2], F32)
        h1, b1, v, z = d["h1"], d["b1_wide"], d["y_group"], d["z"]
        out = d["h_out"]
        relued, t_psum, t_sb, yz_psum = L.new("relued"), L.new("t_psum"), L.new("t_sb"), L.new("yz_psum")
        given, hi, rest, mid, done = L.new("given"), L.new("hi"), L.new("rest"), L.new("mid"), L.new("cut")
        with nc.Block() as block:
            @block.sync
            def _(sp):
                sp.dma_start(w1l[:, :], d["L1_W1l"]).then_inc(L.w_in, 16)
                sp.dma_start(w1r[:, :], d["L1_W1r"]).then_inc(L.w_in, 16)
                sp.dma_start(b1[:, :], d["L1_b1"].rearrange("(a f) -> a f", a=1)).then_inc(L.w_in, 16)
                sp.dma_start(b2[:, :], d["L1_b2"].rearrange("(a f) -> a f", a=1)).then_inc(L.w_in, 16)
                sp.dma_start(w2[:, :, 0:M2], d["L1_W2l"].rearrange("(k p) f -> p k f", p=P)).then_inc(L.w_in, 16)
                sp.dma_start(w2[:, :, M2:2 * M2], d["L1_W2r"].rearrange("(k p) f -> p k f", p=P)).then_inc(L.w_in, 16)

            @block.gpsimd
            def _(pool):
                d["h_out"].clear(nc, pool, L.new("cleared"))
                L.load_counts(pool)

            @block.tensor
            def _(pe):
                def products(c):
                    if c == 0:
                        pe.wait_ge(L.w_in, 96)
                    pe.wait_ge(L.agg_sb, c + 1)
                    pe.wait_ge(L.ht_sb, c + 1)
                    if c >= 1:
                        pe.wait_ge(L.combined, c)
                    for i in range(len(tiles_of(c))):
                        at = slice((i % 2) * H1, (i % 2 + 1) * H1)
                        nc.tensor.matmul(psum[:, 2 + i // 2, at], L.aggT[:, c % 2, i * P:(i + 1) * P], w1l[:, :],
                                         start=True, stop=True)
                        nc.tensor.matmul(psum[:, 4 + i // 2, at], L.hT[:, c % 2, i * P:(i + 1) * P], w1r[:, :],
                                         start=True, stop=False)
                        last = nc.tensor.matmul(psum[:, 4 + i // 2, at], L.ones[0:1, :], b1[:, :], start=False,
                                                stop=True)
                    last.then_inc(L.u_psum, 1)

                def transposes(c):
                    pe.wait_ge(relued, c + 1)
                    if c >= 1:
                        pe.wait_ge(t_sb, c)
                    for i in range(len(tiles_of(c))):
                        for k in range(2):
                            at = (2 * i + k) % 4
                            last = nc.tensor.transpose(psum[:, 6 + i // 2, at * P:(at + 1) * P],
                                                       h1[:, i, k * P:(k + 1) * P], L.ident[:, :])
                    last.then_inc(t_psum, 1)

                def second(c):
                    pe.wait_ge(t_sb, c + 1)
                    if c < G - 3:
                        pe.wait_ge(L.ht_sb, c + 4)
                    elif c >= 1:
                        pe.wait_ge(done, c)
                    for i in range(len(tiles_of(c))):
                        out = psum[:, 1, i * 2 * M2:(i + 1) * 2 * M2]
                        nc.tensor.matmul(out, h1T[:, i, 0, :], w2[:, 0, :], start=True, stop=False)
                        nc.tensor.matmul(out, h1T[:, i, 1, :], w2[:, 1, :], start=False, stop=False)
                        last = nc.tensor.matmul(out[:, M2:2 * M2], L.ones[0:1, :], b2[:, :], start=False, stop=True)
                    last.then_inc(yz_psum, 1)

                for c in range(G + 3):
                    if c < G:
                        if c >= 4:
                            pe.wait_ge(given, c - 3)
                        L.transpose_h(pe, c)
                        L.sum_group(pe, c)
                    if c >= 3:
                        second(c - 3)
                    if 2 <= c < G + 2:
                        transposes(c - 2)
                    if 1 <= c < G + 1:
                        products(c - 1)

            @block.scalar
            def _(act):
                def cut(c):
                    n, tiles = len(tiles_of(c)), slice(tiles_of(c)[0], tiles_of(c)[-1] + 1)
                    act.wait_ge(given, c + 1)
                    nc.scalar.copy(out.of(0, tiles), v[:, 0:n, :]).then_inc(hi, 1)
                    act.wait_ge(rest, c + 1)
                    nc.scalar.copy(out.of(1, tiles), v[:, 0:n, :]).then_inc(mid, 1)

                for c in range(G + 3):
                    if c < G:
                        L.copy_ht(act, c)
                        L.copy_sums(act, c)
                    if c >= 3:
                        cut(c - 3)
                    if 2 <= c < G + 2:
                        n = len(tiles_of(c - 2))
                        act.wait_ge(t_psum, c - 1)
                        if c >= 3:
                            act.wait_ge(yz_psum, c - 2)
                        nc.scalar.copy(h1T[:, 0:n].rearrange("p t k f -> p (t k f)"),
                                       psum[:, 6:8, :].rearrange("p b f -> p (b f)")[:, 0:n * H1]).then_inc(t_sb, 1)
                    if 1 <= c < G + 1:
                        n = len(tiles_of(c - 1))
                        act.wait_ge(L.combined, c)
                        nc.scalar.activation(h1[:, 0:n], h1[:, 0:n], ACT.Relu).then_inc(relued, 1)

            @block.vector
            def _(dve):
                link = linker(dve, L.dve_sem)

                def combine(c):
                    dve.wait_ge(L.u_psum, c + 1)
                    dve.sem_inc(L.agg_read, 1)
                    if c >= 1:
                        dve.wait_ge(t_psum, c)
                    for i, t in enumerate(tiles_of(c)):
                        at = slice((i % 2) * H1, (i % 2 + 1) * H1)
                        last = nc.vector.tensor_copy(h1[:, i, :], psum[:, 4 + i // 2, at])
                    link(last)
                    for i, t in enumerate(tiles_of(c)):
                        at = slice((i % 2) * H1, (i % 2 + 1) * H1)
                        last = nc.vector.scalar_tensor_tensor(
                            out=h1[:, i, :], in0=psum[:, 2 + i // 2, at], scalar=d["inv_deg"][:, t:t + 1],
                            in1=h1[:, i, :], op0=ALU.mult, op1=ALU.add)
                    last.then_inc(L.combined, 1)

                def cut(c):
                    n, tiles = len(tiles_of(c)), slice(tiles_of(c)[0], tiles_of(c)[-1] + 1)
                    dve.wait_ge(yz_psum, c + 1)
                    yz = psum[:, 1, 0:n * 2 * M2].rearrange("p (t f) -> p t f", f=2 * M2)
                    nc.vector.tensor_copy(z[:, tiles, :], yz[:, :, M2:2 * M2])
                    nc.vector.tensor_copy(v[:, 0:n, :], yz[:, :, 0:M2]).then_inc(given, 1)
                    dve.wait_ge(hi, c + 1)
                    nc.vector.tensor_tensor(v[:, 0:n, :], v[:, 0:n, :], out.of(0, tiles), ALU.subtract).then_inc(rest, 1)
                    dve.wait_ge(mid, c + 1)
                    nc.vector.tensor_tensor(out.of(2, tiles), v[:, 0:n, :], out.of(1, tiles),
                                            ALU.subtract).then_inc(done, 1)
                    dve.wait_ge(done, c + 1)

                for c in range(G + 3):
                    if c >= 3:
                        cut(c - 3)
                    if 1 <= c < G + 1:
                        combine(c - 1)


def narrow_layer(nc, new, d):
    with ExitStack() as ctx:
        L = Layer(nc, new, d, "narrow", ctx, d["h_in"])
        psum, z = L.psum, d["z"]
        v = L.sb("v", [P, GT, M2], F32)
        fold = L.sb("fold", [2 * M2, M2], F32)
        folded = L.new("folded")
        split = Split(nc, L.new, "split", v, d["h_out"])
        with nc.Block() as block:
            @block.gpsimd
            def _(pool):
                d["h_out"].clear(nc, pool, L.new("cleared"))
                L.load_counts(pool)

            @block.sync
            def _(sp):
                for k in range(2):
                    sp.dma_start(fold[k * M2:(k + 1) * M2, :], L.ident[0:M2, 0:M2]).then_inc(folded, 16)

            @block.tensor
            def _(pe):
                pe.wait_ge(folded, 32)
                for c in range(G + 1):
                    if c < G:
                        L.sum_group(pe, c)
                    if c >= 1:
                        pe.wait_ge(L.agg_sb, c)
                        if c >= 2:
                            pe.wait_ge(L.combined, c - 1)
                        for i in range(len(tiles_of(c - 1))):
                            last = nc.tensor.matmul(psum[:, 2, i * M2:(i + 1) * M2],
                                                    L.aggT[0:2 * M2, (c - 1) % 2, i * P:(i + 1) * P], fold[:, :],
                                                    start=True, stop=True)
                        last.then_inc(L.u_psum, 1)

            @block.scalar
            def _(act):
                for c in range(G + 1):
                    if c < G:
                        L.copy_sums(act, c)
                    if c >= 1:
                        split.on_scalar(act, c - 1)

            @block.vector
            def _(dve):
                for c in range(G):
                    dve.wait_ge(L.u_psum, c + 1)
                    dve.sem_inc(L.agg_read, 1)
                    for i, t in enumerate(tiles_of(c)):
                        last = nc.vector.scalar_tensor_tensor(
                            out=v[:, i, :], in0=psum[:, 2, i * M2:(i + 1) * M2], scalar=d["inv_deg"][:, t:t + 1],
                            in1=z[:, t, :], op0=ALU.mult, op1=ALU.add)
                    last.then_inc(split.given, 1)
                    dve.wait_ge(split.given, c + 1)
                    dve.sem_inc(L.combined, 1)
                    split.on_vector(dve, c)


def out_layer(nc, new, d):
    with ExitStack() as ctx:
        L = Layer(nc, new, d, "out", ctx, d["h_in"])
        psum, rows = L.psum, 2 * M2
        wl, wr, b = L.sb("w3l", [rows, D], F32), L.sb("w3r", [rows, D], F32), L.sb("b3", [1, D], F32)
        x, v = L.sb("x", [P, GT, D], F32), L.sb("v", [P, GT, D], F32)
        norm = Norm(nc, L.new, L.sb, "norm")
        split = Split(nc, L.new, "split", v, d["h_out"], d["h_sq"], d["trash"])
        x_in, x_ready, x_stored, normed = L.new("x_in"), L.new("x_ready"), L.new("x_stored"), L.new("normed")
        with nc.Block() as block:
            @block.sync
            def _(sp):
                for k in range(2):
                    sp.dma_start(wl[k * M2:(k + 1) * M2, :], d["L1_W3l"]).then_inc(L.w_in, 16)
                    sp.dma_start(wr[k * M2:(k + 1) * M2, :], d["L1_W3r"]).then_inc(L.w_in, 16)
                sp.dma_start(b[:, :], d["L1_b3"].rearrange("(a f) -> a f", a=1)).then_inc(L.w_in, 16)
                stream_x(sp, d["x1"], d["x2"], x, x_in, x_ready, x_stored, normed)

            @block.gpsimd
            def _(pool):
                L.load_counts(pool)

            @block.tensor
            def _(pe):
                for c in range(G + 1):
                    if c < G:
                        L.transpose_h(pe, c)
                        L.sum_group(pe, c)
                    if c >= 1:
                        g = c - 1
                        if c == 1:
                            pe.wait_ge(L.w_in, 80)
                        pe.wait_ge(L.agg_sb, c)
                        pe.wait_ge(L.ht_sb, c)
                        if c >= 2:
                            pe.wait_ge(L.combined, c - 1)
                        for i in range(len(tiles_of(g))):
                            at, nodes = slice(i * D, (i + 1) * D), slice(i * P, (i + 1) * P)
                            nc.tensor.matmul(psum[:, 2, at], L.aggT[0:rows, g % 2, nodes], wl[:, :], start=True,
                                             stop=True)
                            nc.tensor.matmul(psum[:, 3, at], L.hT[0:rows, g % 2, nodes], wr[:, :], start=True,
                                             stop=False)
                            last = nc.tensor.matmul(psum[:, 3, at], L.ones[0:1, :], b[:, :], start=False, stop=True)
                        last.then_inc(L.u_psum, 1)

            @block.scalar
            def _(act):
                for c in range(G + 1):
                    if c < G:
                        L.copy_ht(act, c)
                        L.copy_sums(act, c)
                    if c >= 1:
                        norm.on_scalar(act, d["eps"], c - 1)
                        split.on_scalar(act, c - 1)

            @block.vector
            def _(dve):
                link = linker(dve, L.dve_sem)
                for c in range(G):
                    n = len(tiles_of(c))
                    dve.wait_ge(L.u_psum, c + 1)
                    dve.sem_inc(L.agg_read, 1)
                    dve.wait_ge(x_in, 16 * (c + 1))
                    link(nc.vector.tensor_tensor(x[:, 0:n], x[:, 0:n], psum[:, 3, 0:n * D].rearrange(
                        "p (t f) -> p t f", f=D), ALU.add))
                    for i, t in enumerate(tiles_of(c)):
                        last = nc.vector.scalar_tensor_tensor(
                            out=x[:, i, :], in0=psum[:, 2, i * D:(i + 1) * D], scalar=d["inv_deg"][:, t:t + 1],
                            in1=x[:, i, :], op0=ALU.mult, op1=ALU.add)
                    link(last)
                    dve.sem_inc(L.combined, 1)
                    dve.sem_inc(x_ready, 1)
                    link(norm.on_vector(dve, link, v[:, 0:n], x[:, 0:n], c))
                    dve.sem_inc(normed, 1)
                    dve.sem_inc(split.given, 1)
                    split.on_vector(dve, c)


def stream_x(sp, source, target, x, x_in, x_ready, x_stored, normed):
    for c in range(G):
        n = len(tiles_of(c))
        if c >= 1:
            sp.wait_ge(x_stored, 16 * c)
            sp.wait_ge(normed, c)
        sp.dma_start(x[:, 0:n], group_ap(source, c)).then_inc(x_in, 16)
        sp.wait_ge(x_ready, c + 1)
        sp.dma_start(group_ap(target, c), x[:, 0:n]).then_inc(x_stored, 16)
    sp.wait_ge(x_stored, 16 * G)


def norm_layer(nc, new, d, number, layers):
    final = number == layers - 1
    with ExitStack() as ctx:
        L = Layer(nc, new, d, f"l2n{number}", ctx, d["h_in"])
        psum = L.psum
        wl, wr, b = L.sb("wl", [D, D], F32), L.sb("wr", [D, D], F32), L.sb("b", [P, D], F32)
        square = L.sb("square", [P, GT * P], F32)
        v = L.sb("v", [P, GT, D], F32)
        x = d["x_last"]
        s_h = L.sb("s_h", [P, NT], F32)
        s_agg = L.sb("s_agg", [P, GT], F32)
        norm = Norm(nc, L.new, L.sb, "norm")
        split = Split(nc, L.new, "split", v, d["h_out"], None if final else d["h_sq"], d["trash"])
        x_in, x_ready, x_stored, normed = L.new("x_in"), L.new("x_ready"), L.new("x_stored"), L.new("normed")
        squared, n2_psum, rooted, h_rooted = L.new("squared"), L.new("n2_psum"), L.new("rooted"), L.new("h_rooted")
        with nc.Block() as block:
            @block.sync
            def _(sp):
                sp.dma_start(wl[:, :], d["L2_Wl"][number]).then_inc(L.w_in, 16)
                sp.dma_start(wr[:, :], d["L2_Wr"][number]).then_inc(L.w_in, 16)
                sp.dma_start(b[:, :], d["L2_bl"][number:number + 1, :].broadcast_to([P, D])).then_inc(L.w_in, 16)
                if final:
                    stream_x(sp, d["x2"], d["x3"], x, x_in, x_ready, x_stored, normed)

            @block.gpsimd
            def _(pool):
                L.load_counts(pool)

            @block.tensor
            def _(pe):
                for c in range(G + 1):
                    if c < G:
                        L.transpose_h(pe, c)
                        L.sum_group(pe, c)
                    if c >= 1:
                        g = c - 1
                        if c == 1:
                            pe.wait_ge(L.w_in, 48)
                        pe.wait_ge(L.ht_sb, c)
                        pe.wait_ge(squared, c)
                        if c >= 2:
                            pe.wait_ge(L.combined, c - 1)
                        for i in range(len(tiles_of(g))):
                            last = nc.tensor.matmul(psum[:, 4, i:i + 1], square[:, i * P:(i + 1) * P],
                                                    L.ones[:, 0:1], start=True, stop=True)
                        last.then_inc(n2_psum, 1)
                        for i in range(len(tiles_of(g))):
                            at, nodes = slice(i * D, (i + 1) * D), slice(i * P, (i + 1) * P)
                            nc.tensor.matmul(psum[:, 2, at], L.aggT[:, g % 2, nodes], wl[:, :], start=True, stop=True)
                            last = nc.tensor.matmul(psum[:, 3, at], L.hT[:, g % 2, nodes], wr[:, :], start=True,
                                                    stop=True)
                        last.then_inc(L.u_psum, 1)

            @block.scalar
            def _(act):
                nc.scalar.activation(s_h[:, :], d["h_sq"][:, :], ACT.Sqrt).then_inc(h_rooted, 1)
                for c in range(G + 1):
                    if c < G:
                        n = len(tiles_of(c)) * P
                        L.copy_ht(act, c)
                        L.copy_sums(act, c)
                        act.wait_ge(L.agg_sb, c + 1)
                        if c >= 1:
                            act.wait_ge(n2_psum, c)
                        nc.scalar.activation(square[:, 0:n], L.aggT[:, c % 2, 0:n], ACT.Square).then_inc(squared, 1)
                    if c >= 1:
                        act.wait_ge(n2_psum, c)
                        if c >= 2:
                            act.wait_ge(L.combined, c - 1)
                        nc.scalar.activation(s_agg[:, 0:len(tiles_of(c - 1))], psum[:, 4, 0:len(tiles_of(c - 1))],
                                             ACT.Sqrt).then_inc(rooted, 1)
                        if final:
                            norm.on_scalar(act, d["eps"], c - 1)
                        split.on_scalar(act, c - 1)

            @block.vector
            def _(dve):
                link = linker(dve, L.dve_sem)
                dve.wait_ge(h_rooted, 1)
                link(nc.vector.tensor_scalar(s_h[:, :], s_h[:, :], L2_EPS, None, ALU.max))
                link(nc.vector.reciprocal(s_h[:, :], s_h[:, :]))
                dve.wait_ge(L.w_in, 48)
                for c in range(G):
                    n = len(tiles_of(c))
                    t0 = tiles_of(c)[0]
                    dve.wait_ge(rooted, c + 1)
                    link(nc.vector.tensor_tensor(s_agg[:, 0:n], s_agg[:, 0:n], d["eps_deg"][:, t0:t0 + n], ALU.max))
                    link(nc.vector.reciprocal(s_agg[:, 0:n], s_agg[:, 0:n]))
                    dve.wait_ge(L.u_psum, c + 1)
                    dve.sem_inc(L.agg_read, 1)
                    for i, t in enumerate(tiles_of(c)):
                        last = nc.vector.scalar_tensor_tensor(
                            out=v[:, i, :], in0=psum[:, 3, i * D:(i + 1) * D], scalar=s_h[:, t:t + 1],
                            in1=b[:, :], op0=ALU.mult, op1=ALU.add)
                    link(last)
                    for i, t in enumerate(tiles_of(c)):
                        last = nc.vector.scalar_tensor_tensor(
                            out=v[:, i, :], in0=psum[:, 2, i * D:(i + 1) * D], scalar=s_agg[:, i:i + 1],
                            in1=v[:, i, :], op0=ALU.mult, op1=ALU.add)
                    link(last)
                    dve.sem_inc(L.combined, 1)
                    if final:
                        dve.wait_ge(x_in, 16 * (c + 1))
                        link(nc.vector.tensor_tensor(x[:, 0:n], x[:, 0:n], v[:, 0:n], ALU.add))
                        dve.sem_inc(x_ready, 1)
                        link(norm.on_vector(dve, link, v[:, 0:n], x[:, 0:n], c))
                        dve.sem_inc(normed, 1)
                    dve.sem_inc(split.given, 1)
                    split.on_vector(dve, c)


def weighted_layers(nc, new, d):
    SL = SLABS
    with ExitStack() as ctx:
        def sb(name, shape, dt):
            return ctx.enter_context(nc.sbuf_tensor("wl_" + name, shape, dt))

        def sem(name):
            return new("wl_" + name)

        psum, ident = d["psum"], d["ident"]
        slab = counts_slab(d)
        free_a = d["parts_a"][:, :].bitcast(F32)[:, NT * D:]
        free_b = d["parts_b"][:, :].bitcast(F32)
        g = [sb("g1", [P, NT, D], F32), free_b[:, 0:NT * D].rearrange("p (t f) -> p t f", f=D)]
        free_b = free_b[:, NT * D:]
        w = [sb("w1", [D, D], F32), sb("w2", [D, D], F32)]
        b = [sb("b1", [P, D], F32), free_a[:, 2 * GT * D:2 * GT * D + D]]
        hT = free_b[:, 0:GT * P]
        aggT = free_b[:, GT * P:3 * GT * P].rearrange("p (a n) -> p a n", a=2)
        out = free_a[:, 0:GT * D].rearrange("p (t f) -> p t f", f=D)
        x = free_a[:, GT * D:2 * GT * D].rearrange("p (t f) -> p t f", f=D)

        w_in, slab_in = sem("w_in"), [sem(f"slab_in{i}") for i in range(SL)]
        ht_psum, ht_sb, p_psum, scaled = sem("ht_psum"), sem("ht_sb"), sem("p_psum"), sem("scaled")
        summed, agg_sb, t_psum, combined, relued = (sem("summed"), sem("agg_sb"), sem("t_psum"), sem("combined"),
                                                    sem("relued"))
        x_in, x_ready, stored = sem("x_in"), sem("x_ready"), sem("stored")
        dve_sem = sem("dve")

        with nc.Block() as block:
            @block.sync
            def _(sp):
                for k in range(2):
                    sp.dma_start(w[k][:, :], d[f"L3_W{k + 1}"]).then_inc(w_in, 16)
                    sp.dma_start(b[k][:, :], d[f"L3_b{k + 1}"].rearrange("(a f) -> a f", a=1).broadcast_to([P, D])
                                 ).then_inc(w_in, 16)
                for n in range(2 * G):
                    c = n % G
                    m = min(WG, J - c * WG)
                    if n >= SL:
                        sp.wait_ge(summed, n - SL + 1)
                    sp.dma_start(slab[:, n % SL, 0:m, :], d["aw"][c * WG:c * WG + m].rearrange("j p k -> p j k")
                                 ).then_inc(slab_in[n % SL], 16)
                for c in range(G):
                    m = len(tiles_of(c))
                    if c >= 1:
                        sp.wait_ge(stored, 16 * c)
                    sp.dma_start(x[:, 0:m], group_ap(d["x3"], c)).then_inc(x_in, 16)
                    sp.wait_ge(x_ready, c + 1)
                    if c < G - 1:
                        sp.dma_start(group_ap(d["out"], c), x[:, 0:m]).then_inc(stored, 16)
                    else:
                        rows = N - c * GT * P
                        sp.dma_start(d["out"][c * GT * P:N, :], x[0:rows, 0, :]).then_inc(stored, 16)
                sp.wait_ge(stored, 16 * G)

            @block.tensor
            def _(pe):
                def transposed(m):
                    if m < G:
                        transpose_parts(nc, d, d["h_in"], pe, m, ht_psum, ht_sb)
                        return
                    pe.wait_ge(ht_sb, m)
                    for i in range(len(tiles_of(m - G))):
                        last = nc.tensor.transpose(psum[:, 1, i * P:(i + 1) * P], out[:, i, :], ident[:, :])
                    last.then_inc(ht_psum, 1)

                def product(m):
                    c, k = m % G, m // G
                    pe.wait_ge(ht_sb, m + 1)
                    if m >= 1:
                        pe.wait_ge(scaled, m)
                    for i in range(len(tiles_of(c))):
                        last = nc.tensor.matmul(psum[:, 3, i * D:(i + 1) * D], hT[:, i * P:(i + 1) * P], w[k][:, :],
                                                start=True, stop=True)
                    last.then_inc(p_psum, 1)

                def sum_group(n):
                    c, k = n % G, n // G
                    m = min(WG, J - c * WG)
                    pe.wait_ge(slab_in[n % SL], 16 * (n // SL + 1))
                    if n >= 1:
                        pe.wait_ge(agg_sb, n)
                    for t in range(NT):
                        last = nc.tensor.matmul(psum[:, 0, 0:m * W], g[k][:, t, :],
                                                slab[:, n % SL, 0:m, t * W:(t + 1) * W], start=(t == 0),
                                                stop=(t == NT - 1))
                    last.then_inc(summed, 1)

                def back(n):
                    pe.wait_ge(agg_sb, n + 1)
                    if n >= 1:
                        pe.wait_ge(combined, n)
                    for i in range(len(tiles_of(n % G))):
                        last = nc.tensor.transpose(psum[:, 2, i * P:(i + 1) * P], aggT[:, n % 2, i * P:(i + 1) * P],
                                                   ident[:, :])
                    last.then_inc(t_psum, 1)

                pe.wait_ge(w_in, 64)
                for m in range(G):
                    transposed(m)
                    product(m)
                pe.wait_ge(scaled, G)
                for c in range(G + 1):
                    if c < G:
                        sum_group(c)
                    if c >= 1:
                        back(c - 1)
                        pe.wait_ge(relued, c)
                        transposed(G + c - 1)
                        product(G + c - 1)
                pe.wait_ge(scaled, 2 * G)
                for c in range(G + 1):
                    if c < G:
                        sum_group(G + c)
                    if c >= 1:
                        back(G + c - 1)

            @block.scalar
            def _(act):
                def copy_t(m):
                    n = len(tiles_of(m % G)) * P
                    act.wait_ge(ht_psum, m + 1)
                    if m >= 1:
                        act.wait_ge(p_psum, m)
                    nc.scalar.copy(hT[:, 0:n], psum[:, 1, 0:n]).then_inc(ht_sb, 1)

                def copy_sums(n):
                    c = n % G
                    m = min(GT * P, NCOL - c * GT * P)
                    act.wait_ge(summed, n + 1)
                    if n >= 2:
                        act.wait_ge(t_psum, n - 1)
                    nc.scalar.copy(aggT[:, n % 2, 0:m], psum[:, 0, 0:m]).then_inc(agg_sb, 1)

                for m in range(G):
                    copy_t(m)
                for c in range(G + 1):
                    if c < G:
                        copy_sums(c)
                    if c >= 1:
                        n = len(tiles_of(c - 1))
                        act.wait_ge(combined, c)
                        nc.scalar.activation(out[:, 0:n], out[:, 0:n], ACT.Relu).then_inc(relued, 1)
                        copy_t(G + c - 1)
                for c in range(G):
                    copy_sums(G + c)

            @block.vector
            def _(dve):
                link = linker(dve, dve_sem)
                dinv = d["dinv"]

                def scale(m):
                    c, k = m % G, m // G
                    dve.wait_ge(p_psum, m + 1)
                    for i, t in enumerate(tiles_of(c)):
                        last = nc.vector.tensor_scalar(g[k][:, t, :], psum[:, 3, i * D:(i + 1) * D],
                                                       dinv[:, t:t + 1], None, ALU.mult)
                    last.then_inc(scaled, 1)

                def combine(n):
                    c, k = n % G, n // G
                    m = len(tiles_of(c))
                    t0 = tiles_of(c)[0]
                    dve.wait_ge(t_psum, n + 1)
                    if 1 <= n <= G:
                        dve.wait_ge(ht_psum, G + n)
                    link(nc.vector.tensor_tensor(out[:, 0:m], psum[:, 2, 0:m * D].rearrange("p (t f) -> p t f", f=D),
                                                 g[k][:, t0:t0 + m], ALU.add))
                    for i, t in enumerate(tiles_of(c)):
                        last = nc.vector.scalar_tensor_tensor(out=out[:, i, :], in0=out[:, i, :],
                                                              scalar=dinv[:, t:t + 1], in1=b[k][:, :],
                                                              op0=ALU.mult, op1=ALU.add)
                    link(last)
                    dve.sem_inc(combined, 1)

                dve.wait_ge(w_in, 64)
                for m in range(G):
                    scale(m)
                for c in range(G):
                    combine(c)
                    scale(G + c)
                for c in range(G):
                    m = len(tiles_of(c))
                    combine(G + c)
                    dve.wait_ge(x_in, 16 * (c + 1))
                    link(nc.vector.tensor_tensor(x[:, 0:m], x[:, 0:m], out[:, 0:m], ALU.add))
                    dve.sem_inc(x_ready, 1)


def load_crowded(nc, d):
    flag = d["starts"][0:1, J + 1:J + 2]
    d["crowded"] = {}
    with nc.Block() as block:
        @block.sync
        def _(sp):
            d["crowded"]["SP"] = sp.value_load(flag, min_val=0, max_val=E + J)

        @block.gpsimd
        def _(pool):
            d["crowded"]["Pool"] = pool.value_load(flag, min_val=0, max_val=E + J)

        @block.vector
        def _(dve):
            d["crowded"]["DVE"] = dve.value_load(flag, min_val=0, max_val=E + J)

        @block.scalar
        def _(act):
            d["crowded"]["Activation"] = act.value_load(flag, min_val=0, max_val=E + J)

        @block.tensor
        def _(pe):
            d["crowded"]["PE"] = pe.value_load(flag, min_val=0, max_val=E + J)


def build(nc, d):
    with ExitStack() as ctx:
        held = []

        def new(name):
            held.append(nc.alloc_semaphore(name=name))
            return held[-1]

        def end_phase():
            nc.all_engine_barrier()
            nc.clear_and_free_semaphores(held)
            nc.all_engine_barrier()
            held.clear()

        def keep(name, shape, dt):
            d[name] = ctx.enter_context(nc.sbuf_tensor(name, shape, dt))

        d["psum"] = ctx.enter_context(nc.psum_tensor("psum", [P, 8, 512], F32))
        keep("ident", [P, P], F32)
        keep("ones", [P, P], F32)
        keep("eps", [P, 1], F32)
        keep("starts", [1, J + 2], I32)
        keep("inv_deg", [P, NT], F32)
        keep("eps_deg", [P, NT], F32)
        keep("dinv", [P, NT], F32)
        made = new("ident_made")
        with nc.Block() as block:
            @block.gpsimd
            def _(pool):
                nc.gpsimd.memset(d["ident"][:, :], 0.0).then_inc(made, 1)
                nc.gpsimd.memset(d["ones"][:, :], 1.0).then_inc(made, 1)
                nc.gpsimd.memset(d["eps"][:, :], LN_EPS).then_inc(made, 1)
                pool.wait_ge(made, 3)
                nc.gpsimd.affine_select(out=d["ident"][:, :], in_=d["ident"][:, :], compare_op=ALU.not_equal, fill=1.0,
                                        base=0, pattern=[[-1, P]], channel_multiplier=1).then_inc(made, 1)
                pool.wait_ge(made, 4)
        prepare(nc, new, d)
        end_phase()
        load_crowded(nc, d)
        keep("adj", [P, NT, NCOL], F16)
        edge_pass(nc, new, d)
        end_phase()
        crowded_edge_pass(nc, new, d)
        end_phase()
        keep("h_sq", [P, NT], F32)
        keep("trash", [P, D], BF16)
        keep("ident_b", [P, P], BF16)
        keep("parts_a", [P, NT * 3 * D], F16)
        keep("parts_b", [P, NT * 3 * D], F16)
        a, b = d["parts_a"], d["parts_b"]
        a_f32, b_f32 = a[:, :].bitcast(F32), b[:, :].bitcast(F32)
        at = NT * 4 * M2 // 2
        d["z"] = b_f32[:, at:at + NT * M2].rearrange("p (t f) -> p t f", f=M2)
        at += NT * M2
        d["h1"] = b_f32[:, at:at + GT * H1].rearrange("p (t f) -> p t f", f=H1)
        at = NT * D
        d["h1T"] = a_f32[:, at:at + GT * H1].rearrange("p (t k f) -> p t k f", k=2, f=P)
        at += GT * H1
        d["b1_wide"] = a_f32[0:1, at:at + H1]
        at += H1
        d["y_group"] = a_f32[:, at:at + GT * M2].rearrange("p (t f) -> p t f", f=M2)
        d["x_last"] = a_f32[:, NT * D:(NT + GT) * D].rearrange("p (t f) -> p t f", f=D)
        flow = [(first_tail, (), Parts(a, F16, D, 2)),
                (wide_layer, (), Parts(b, BF16, M2, 3)),
                (narrow_layer, (), Parts(a, BF16, M2, 3)),
                (out_layer, (), Parts(b, F16, D, 2)),
                (norm_layer, (0, 3), Parts(a, BF16, D, 3)),
                (norm_layer, (1, 3), Parts(b, BF16, D, 3)),
                (norm_layer, (2, 3), Parts(a, F16, D, 2))]
        for layer, which, out in flow:
            d["h_out"] = out
            layer(nc, new, d, *which)
            end_phase()
            d["h_in"] = out
        weighted_layers(nc, new, d)


def kernel(**inputs):
    import numpy as np
    import concourse.bacc as bacc
    from concourse.bass_utils import run_bass_kernel_spmd

    arr = {k: np.ascontiguousarray(v) for k, v in inputs.items()}

    def padded(a, n, value):
        return np.concatenate([a, np.full((n - a.shape[0],) + a.shape[1:], value, a.dtype)])

    send = {
        "x": padded(arr["x"], NPAD, 0),
        "src": padded(arr["src"], EPAD, 0),
        "dst": padded(arr["dst"], EPAD + P, FAR),
        "w": padded(arr["edge_weight"], EPAD, 0),
        "ea": np.ascontiguousarray(padded(arr["edge_attr_32"], EPAD, 0).T),
        "L0_W1": np.ascontiguousarray(arr["L0_gnn_W1"].T),
        "L0_b1": arr["L0_gnn_b1"],
        "L0_W2": np.ascontiguousarray(arr["L0_gnn_W2"].T),
        "L0_Wu": np.ascontiguousarray(arr["L0_gnn_Wu"].T),
        "L2_Wl": np.ascontiguousarray(arr["L2_gnn_Wl"].transpose(0, 2, 1)),
        "L2_Wr": np.ascontiguousarray(arr["L2_gnn_Wr"].transpose(0, 2, 1)),
    }
    for name in ("L0_b2", "L0_bu", "L0_gamma", "L0_beta", "L1_b1", "L1_b2", "L1_b3", "L2_bl", "L3_W1", "L3_b1",
                 "L3_W2", "L3_b2"):
        send[name] = arr[name.replace("_", "_gnn_")]
    for name in ("L1_W1l", "L1_W1r", "L1_W2l", "L1_W2r", "L1_W3l", "L1_W3r"):
        send[name] = np.ascontiguousarray(arr[name.replace("_", "_gnn_")].T)
    nc = bacc.Bacc("TRN2", target_bir_lowering=False, num_devices=1)
    d = {k: nc.dram_tensor("in_" + k, v.shape, mybir.dt.from_np(v.dtype), kind="ExternalInput").ap()
         for k, v in send.items()}
    for name, shape in (("records", (EPAD, REC)), ("dst_row", (EPAD,)), ("h0", (NPAD, D)), ("P", (NPAD, D)),
                        ("Q", (NPAD, D)), ("aw", (J, P, NKEY)), ("counts", (J, P, NKEY)),
                        ("P_src", (-(-E // BLK) * BLK, D)),
                        ("agg", (D, NPAD)), ("deg", (4, NPAD)),
                        ("x1", (NPAD, D)), ("x2", (NPAD, D)), ("x3", (NPAD, D))):
        d[name] = nc.dram_tensor("dram_" + name, shape, F32, kind="Internal").ap()
    d["out"] = nc.dram_tensor("out", (N, D), F32, kind="ExternalOutput").ap()
    build(nc, d)
    r = run_bass_kernel_spmd(nc, [{"in_" + k: v for k, v in send.items()}], core_ids=[0])
    return r.results[0]["out"]
```

```python
from contextlib import ExitStack

import concourse.bass as bass
from concourse import mybir

F32 = mybir.dt.float32
F16 = mybir.dt.float16
BF16 = mybir.dt.bfloat16
I32 = mybir.dt.int32
ALU = mybir.AluOpType
ACT = mybir.ActivationFunctionType
AX = mybir.AxisListType

P = 128
N = 3125
E = 103125
D = 128
ED = 32
NT = (N + P - 1) // P
NPAD = NT * P
W = 16
J = (N + W - 1) // W
NCOL = J * W
CH = 5
BLK = CH * P
CP = -(-(E + BLK) // P)
CP += CP % 2
EPAD = CP * P
NKEY = W * NT
FAR = 4000
REC = 8
R_KEY, R_D25, R_LO, R_W1, R_W2, R_W, R_UNUSED, R_SRC = range(REC)
UP = 2048.0
F16_ROOM = 16384.0
W_MOST = 30.0
GT = 4
G = (NT + GT - 1) // GT
WG = GT * P // W
SLABS = 3
H1, M2 = 2 * D, 48
UNROLL = 11
LN_EPS = 1e-5
L2_EPS = 1e-12


def tiles_of(c):
    return range(c * GT, min((c + 1) * GT, NT))


def linker(eng, sem):
    count = [0]

    def link(ins):
        count[0] += 1
        ins.then_inc(sem, 1)
        eng.wait_ge(sem, count[0])

    return link


def group_ap(dram, c):
    t0, t1 = tiles_of(c)[0], tiles_of(c)[-1] + 1
    return dram[t0 * P:t1 * P, :].rearrange("(t p) f -> p t f", p=P)


def prepare(nc, new, d):
    with ExitStack() as ctx:
        def sb(name, shape, dt):
            return ctx.enter_context(nc.sbuf_tensor(name, shape, dt))

        psum, ident, ones = d["psum"], d["ident"], d["ones"]
        dst_i = sb("dst_i", [P, CP], I32)
        nxt_i = sb("nxt_i", [P, CP], I32)
        src_i = sb("src_i", [P, CP], I32)
        hi_i = sb("hi_i", [P, CP], I32)
        lo_i = sb("lo_i", [P, CP], I32)
        bad = sb("bad", [P, CP], F16)
        w_sb = sb("w_sb", [P, CP], F32)
        w_up = sb("w_up", [P, CP], F32)
        hi_f = sb("hi_f", [P, CP], F32)
        w_hi = sb("w_hi", [P, CP], F16)
        w_lo = sb("w_lo", [P, CP], F16)
        dst_f = sb("dst_f", [P, CP], F32)
        rec = sb("rec", [P, CP, REC], F32)
        first = sb("first", [P, 2 * P], F32)
        first_col = sb("first_col", [P, 2], F32)
        before = sb("before", [P, 2 * P], F32)
        row_of = sb("row_of", [P, 2], F32)
        row_i = sb("row_i", [P, 2], I32)
        dst_rows = sb("search_rows", [P, 2, CP], I32)
        lower = sb("lower", [P, 2, CP], F16)
        within = sb("within", [P, 2], F32)
        start_col = sb("start_col", [P, 2], F32)
        bad_sum = sb("bad_sum", [P, 1], F32)
        starts_f = sb("starts_f", [1, 2 * P + 1], F32)
        over = sb("over", [1, J], F32)
        over_sum = sb("over_sum", [1, 2], F32)
        x = sb("x_all", [P, NT, D], F32)
        h = sb("h0_all", [P, NT, D], F32)
        pq = sb("pq", [P, NT, 2, D], F32)
        hT = sb("prep_hT", [P, 2, GT * P], F32)
        w_ab = sb("w_ab", [D, 2 * D], F32)
        b1 = sb("b1_row", [1, D], F32)
        stats = sb("stats", [P, NT, 6], F32)
        mv = sb("mv", [P, NT, 2], F32)
        std = sb("std", [P, NT], F32)
        rstd = sb("rstd", [P, NT], F32)

        dst_in, edges_in, w_in = new("dst_in"), new("edges_in"), new("wab_in")
        x_in = [new(f"x_in{c}") for c in range(G)]
        shifted, recs, pool_step, dve_step = new("shifted"), new("recs_built"), new("pool_step"), new("prep_dve")
        firsts, begun, rows_psum, rows_ready, rows_in = (new("firsts"), new("begun"), new("rows_psum"),
                                                         new("rows_ready"), new("rows_in"))
        start_cols, starts_psum = new("start_cols"), new("starts_psum")
        varied, stded, normed, h_ready = new("varied"), new("stded"), new("normed"), new("h_ready")
        ht_psum, ht_sb, pq_psum, pq_sb = new("ht_psum"), new("ht_sb"), new("pq_psum"), new("pq_sb")
        stored = new("prep_stored")

        def normalise(dve, step, c):
            t0, t1 = tiles_of(c)[0], tiles_of(c)[-1] + 1
            dve.wait_ge(stded, c + 1)
            step(nc.vector.reciprocal(rstd[:, t0:t1], std[:, t0:t1]))
            for t in tiles_of(c):
                last = nc.vector.tensor_scalar(h[:, t, :], x[:, t, :], mv[:, t, 0:1], rstd[:, t:t + 1],
                                               ALU.subtract, ALU.mult)
            last.then_inc(normed, 1)

        with nc.Block() as block:
            @block.sync
            def _(sp):
                for dst, src in ((dst_i, d["dst"][0:EPAD]), (nxt_i, d["dst"][1:EPAD + 1])):
                    sp.dma_start(dst[:, :], src.rearrange("(p c) -> p c", p=P)).then_inc(dst_in, 16)
                for c in range(G):
                    t = slice(tiles_of(c)[0], tiles_of(c)[-1] + 1)
                    sp.dma_start(x[:, t], group_ap(d["x"], c)).then_inc(x_in[c], 16)
                    if c == 1:
                        sp.dma_start(w_ab[:, 0:D], d["L0_W1"][0:D, :]).then_inc(w_in, 16)
                        sp.dma_start(w_ab[:, D:2 * D], d["L0_W1"][D:2 * D, :]).then_inc(w_in, 16)
                        sp.dma_start(b1[:, :], d["L0_b1"].rearrange("(a f) -> a f", a=1)).then_inc(w_in, 16)
                        for dst, src in ((src_i, d["src"][0:EPAD]), (w_sb, d["w"][0:EPAD])):
                            sp.dma_start(dst[:, :], src.rearrange("(p c) -> p c", p=P)).then_inc(edges_in, 16)
                for c in range(G):
                    t = slice(tiles_of(c)[0], tiles_of(c)[-1] + 1)
                    if c == 5:
                        sp.wait_ge(recs, 2)
                        sp.dma_start(d["records"].rearrange("(p c) k -> p c k", p=P), rec[:, :, :]).then_inc(stored, 16)
                        sp.dma_start(d["dst_row"].rearrange("(p c) -> p c", p=P), dst_f[:, :]).then_inc(stored, 16)
                    sp.wait_ge(pq_sb, c + 1)
                    sp.dma_start(group_ap(d["h0"], c), h[:, t]).then_inc(stored, 16)
                    sp.dma_start(group_ap(d["P"], c), pq[:, t, 0]).then_inc(stored, 16)
                    sp.dma_start(group_ap(d["Q"], c), pq[:, t, 1]).then_inc(stored, 16)
                sp.wait_ge(stored, 16 * (3 * G + 2))

            @block.gpsimd
            def _(pool):
                steps = [0]

                def step(ins):
                    steps[0] += 1
                    ins.then_inc(pool_step, 1)
                    pool.wait_ge(pool_step, steps[0])

                nc.gpsimd.iota(first[:, :], [[W, 2 * P]], base=0, channel_multiplier=0,
                               allow_small_or_imprecise_dtypes=True).then_inc(firsts, 1)
                nc.gpsimd.iota(first_col[:, :], [[W * P, 2]], base=0, channel_multiplier=W,
                               allow_small_or_imprecise_dtypes=True).then_inc(firsts, 1)
                pool.wait_ge(rows_ready, 1)
                for half in range(2):
                    nc.gpsimd.indirect_dma_start(
                        dst_rows[:, half, :], None, d["dst"][0:EPAD].rearrange("(p c) -> p c", p=P),
                        bass.IndirectOffsetOnAxis(ap=row_i[:, half:half + 1], axis=0)).then_inc(rows_in, 16)
                step(nc.gpsimd.tensor_copy(dst_f[:, :], dst_i[:, :]))
                step(nc.gpsimd.tensor_scalar(rec[:, :, R_D25], dst_f[:, :], float(NT), None, ALU.mult))
                pool.wait_ge(edges_in, 32)
                nc.gpsimd.tensor_copy(rec[:, :, R_SRC].bitcast(I32), src_i[:, :])
                pool.wait_ge(shifted, 1)
                nc.gpsimd.tensor_copy(rec[:, :, R_LO], lo_i[:, :])
                step(nc.gpsimd.tensor_copy(hi_f[:, :], hi_i[:, :]))
                step(nc.gpsimd.tensor_tensor(rec[:, :, R_KEY], rec[:, :, R_D25], hi_f[:, :], ALU.add))
                pool.drain().then_inc(recs, 1)
                pool.wait_ge(rows_in, 32)

            @block.vector
            def _(dve):
                steps = [0]

                def step(ins):
                    steps[0] += 1
                    ins.then_inc(dve_step, 1)
                    dve.wait_ge(dve_step, steps[0])

                dve.wait_ge(firsts, 2)
                dve.wait_ge(dst_in, 32)
                nc.vector.tensor_copy(bad_sum[:, :], dst_i[:, 0:1]).then_inc(dve_step, 1)
                steps[0] += 1
                dve.wait_ge(dve_step, steps[0])
                nc.vector.tensor_scalar(before[:, :], first[:, :], bad_sum[:, 0:1], None, ALU.is_gt).then_inc(begun, 1)
                dve.wait_ge(rows_psum, 1)
                step(nc.vector.tensor_scalar(row_of[:, :], psum[:, 7, 0:2], 1.0, 0.0, ALU.subtract, ALU.max))
                nc.vector.tensor_copy(row_i[:, :], row_of[:, :]).then_inc(rows_ready, 1)
                for c in range(G):
                    dve.wait_ge(x_in[c], 16)
                    for t in tiles_of(c):
                        last = nc.vector.bn_stats(stats[:, t, :], x[:, t, :])
                    step(last)
                    for t in tiles_of(c):
                        last = nc.vector.bn_aggr(mv[:, t, :], stats[:, t, :])
                    last.then_inc(varied, 1)
                    if c == 1:
                        dve.wait_ge(edges_in, 32)
                        nc.vector.tensor_scalar(lo_i[:, :], src_i[:, :], P - 1, None, ALU.bitwise_and)
                        step(nc.vector.tensor_scalar(hi_i[:, :], src_i[:, :], 7, None, ALU.logical_shift_right))
                        dve.sem_inc(shifted, 1)
                    if c == 2:
                        nc.vector.tensor_copy(rec[:, :, R_W], w_sb[:, :])
                        nc.vector.memset(rec[:, :, R_UNUSED], 0.0)
                        step(nc.vector.tensor_scalar(w_up[:, :], w_sb[:, :], UP, None, ALU.mult))
                    if c >= 1:
                        normalise(dve, step, c - 1)
                    if c == 3:
                        step(nc.vector.tensor_copy(w_hi[:, :], w_up[:, :]))
                        nc.vector.tensor_copy(rec[:, :, R_W1], w_hi[:, :])
                    if c == 4:
                        step(nc.vector.tensor_tensor(w_lo[:, :], w_up[:, :], w_hi[:, :], ALU.subtract))
                        nc.vector.tensor_copy(rec[:, :, R_W2], w_lo[:, :]).then_inc(recs, 1)
                normalise(dve, step, G - 1)
                step(nc.vector.tensor_tensor(bad[:, :], nxt_i[:, :], dst_i[:, :], ALU.is_lt))
                step(nc.vector.scalar_tensor_tensor(out=bad[:, :], in0=w_sb[:, :], scalar=W_MOST, in1=bad[:, :],
                                                    op0=ALU.is_gt, op1=ALU.add))
                step(nc.vector.scalar_tensor_tensor(out=bad[:, :], in0=w_sb[:, :], scalar=-W_MOST, in1=bad[:, :],
                                                    op0=ALU.is_lt, op1=ALU.add))
                step(nc.vector.reduce_sum(bad_sum[:, :], bad[:, :], axis=AX.X))
                dve.wait_ge(rows_in, 32)
                for half in range(2):
                    last = nc.vector.tensor_scalar(lower[:, half], dst_rows[:, half], first_col[:, half:half + 1], 0.0,
                                                   ALU.is_lt, ALU.add, accum_out=within[:, half:half + 1])
                step(last)
                nc.vector.scalar_tensor_tensor(out=start_col[:, :], in0=row_of[:, :], scalar=float(CP),
                                               in1=within[:, :], op0=ALU.mult, op1=ALU.add).then_inc(start_cols, 1)
                dve.wait_ge(starts_psum, 1)
                step(nc.vector.tensor_copy(starts_f[:, :], psum[0:1, 6, 0:2 * P + 1]))
                nc.vector.tensor_copy(d["starts"][0:1, 0:J + 1], starts_f[:, 0:J + 1])
                step(nc.vector.tensor_tensor(over[:, :], starts_f[:, 1:J + 1], starts_f[:, 0:J], ALU.subtract))
                step(nc.vector.tensor_scalar(over[:, :], over[:, :], float(BLK), None, ALU.is_gt))
                step(nc.vector.reduce_sum(over_sum[:, 0:1], over[:, :], axis=AX.X))
                step(nc.vector.tensor_tensor(over_sum[:, 1:2], over_sum[:, 0:1], starts_f[:, 2 * P:2 * P + 1], ALU.add))
                step(nc.vector.tensor_copy(d["starts"][0:1, J + 1:J + 2], over_sum[:, 1:2]))

            @block.scalar
            def _(act):
                def copy_pq(c):
                    t0, n = tiles_of(c)[0], len(tiles_of(c))
                    act.wait_ge(pq_psum, c + 1)
                    nc.scalar.copy(pq[:, t0:t0 + n].rearrange("p t a f -> p (t a f)"), psum[:, 2 + 2 * (c % 2):4 + 2 * (
                        c % 2), :].rearrange("p b f -> p (b f)")[:, 0:n * 2 * D]).then_inc(pq_sb, 1)

                def rooted_and_relued(c):
                    t0, n = tiles_of(c)[0], len(tiles_of(c))
                    act.wait_ge(varied, c + 1)
                    nc.scalar.activation(std[:, t0:t0 + n], mv[:, t0:t0 + n, 1], ACT.Sqrt,
                                         bias=d["eps"][:, 0:1]).then_inc(stded, 1)
                    act.wait_ge(normed, c + 1)
                    nc.scalar.activation(h[:, t0:t0 + n], h[:, t0:t0 + n], ACT.Relu).then_inc(h_ready, 1)

                rooted_and_relued(0)
                for c in range(G):
                    if c + 1 < G:
                        rooted_and_relued(c + 1)
                    n = len(tiles_of(c))
                    act.wait_ge(ht_psum, c + 1)
                    if c >= 2:
                        act.wait_ge(pq_psum, c - 1)
                    nc.scalar.copy(hT[:, c % 2, 0:n * P], psum[:, c % 2, 0:n * P]).then_inc(ht_sb, 1)
                    if c >= 1:
                        copy_pq(c - 1)
                copy_pq(G - 1)

            @block.tensor
            def _(pe):
                def rows_of_windows():
                    pe.wait_ge(begun, 1)
                    for half in range(2):
                        last = nc.tensor.matmul(psum[:, 7, half:half + 1], before[:, half * P:(half + 1) * P],
                                                ones[:, 0:1], start=True, stop=True)
                    last.then_inc(rows_psum, 1)

                rows_of_windows()
                pe.wait_ge(w_in, 48)
                def transposes(c):
                    pe.wait_ge(h_ready, c + 1)
                    if c >= 2:
                        pe.wait_ge(ht_sb, c - 1)
                    for i, t in enumerate(tiles_of(c)):
                        last = nc.tensor.transpose(psum[:, c % 2, i * P:(i + 1) * P], h[:, t, :], ident[:, :])
                    last.then_inc(ht_psum, 1)

                transposes(0)
                for c in range(G):
                    if c + 1 < G:
                        transposes(c + 1)
                    pe.wait_ge(ht_sb, c + 1)
                    if c >= 2:
                        pe.wait_ge(pq_sb, c - 1)
                    for i in range(len(tiles_of(c))):
                        out = psum[:, 2 + 2 * (c % 2) + i // 2, (i % 2) * 2 * D:(i % 2 + 1) * 2 * D]
                        nc.tensor.matmul(out, hT[:, c % 2, i * P:(i + 1) * P], w_ab[:, :], start=True, stop=False)
                        last = nc.tensor.matmul(out[:, D:2 * D], ones[0:1, :], b1[:, :], start=False, stop=True)
                    last.then_inc(pq_psum, 1)
                pe.wait_ge(start_cols, 1)
                for half in range(2):
                    nc.tensor.matmul(psum[0:1, 6, half * P:(half + 1) * P], start_col[:, half:half + 1], ident[:, :],
                                     start=True, stop=True)
                nc.tensor.matmul(psum[0:1, 6, 2 * P:2 * P + 1], ones[:, 0:1], bad_sum[:, :], start=True,
                                 stop=True).then_inc(starts_psum, 1)


def edge_pass(nc, new, d):
    S = 4
    with ExitStack() as ctx:
        def sb(name, shape, dt):
            return ctx.enter_context(nc.sbuf_tensor(name, shape, dt))

        adj, psum = d["adj"], d["psum"]
        rec = sb("win_rec", [P, S, CH * REC], F32)
        lhs = sb("lhs", [ED + W, 2, BLK], F32)
        rhs = sb("rhs", [ED + W, S, D], F32)
        dst_row = sb("dst_rows", [ED + W, 2, BLK], F32)
        msg = sb("msg", [P, S, CH, D], F32)
        key = sb("key", [P, S, CH, 2], F32)
        wts = sb("wts", [P, S, CH, 4], F16)
        hot_d = sb("hot_d", [P, S, CH, W], F32)
        hot_db = sb("hot_db", [P, S, CH, W], BF16)
        hot_lo = sb("hot_lo", [P, 2, CH, 3, P], F16)
        hot_key = sb("hot_key", [P, 2, CH, NKEY], BF16)
        aw_out = sb("aw_out", [P, S, NKEY], F32)
        agg_win = sb("agg_win", [P, S, W], F32)
        deg_win = sb("deg_win", [4, S, W], F32)
        key0 = sb("key0", [P, J], F32)
        dst_of = sb("dst_of", [P, J], F32)
        iota_d = sb("iota_d", [P, W], F32)
        iota_lo = sb("iota_lo", [P, P], F16)
        iota_key = sb("iota_key", [P, NKEY], F16)

        consts, w_in = new("edge_consts"), new("w1c_in")
        rec_in = [new(f"rec_in{s}") for s in range(S)]
        lhs_in = [new(f"lhs_in{s}") for s in range(S)]
        gathered = [new(f"gathered{s}") for s in range(S)]
        agg_stored = [new(f"agg_stored{s}") for s in range(S)]
        aw_stored = [new(f"aw_stored{s}") for s in range(S)]
        keyed, hots, hot_t, summed = new("keyed"), new("hots"), new("hot_t"), new("summed")
        multiplied, pre, sums = new("multiplied"), new("pre"), new("sums")
        relued, adj_out, agg_out = new("relued"), new("adj_out"), new("agg_out")
        hot_los, weighted = new("hot_los"), new("weighted")
        pace = new("edge_pace")

        def counts_of(u):
            return psum[:, u % 2, 0:NKEY]

        def weights_of(u):
            return psum[:, 2 + u % 2, 0:NKEY]

        def pre_of(k):
            return psum[:, 4 + k // 4, (k % 4) * D:(k % 4 + 1) * D]

        def await_count(eng, sem, count):
            if not isinstance(count, int):
                eng.wait_ge(sem, count)
                eng.sem_inc(pace, 1)
            elif count > 0:
                eng.wait_ge(sem, count)

        def uses(j, s, n):
            return (j - s) * (n // S)

        def by_window(eng, step):
            for j in range(2 * S):
                step(j, j % S)
            with eng.Fori(2, J // S) as i:
                for s in range(S):
                    step(i * S + s, s)

        def before(s):
            return (s - 1) % S

        with nc.Block() as block:
            @block.sync
            def _(sp):
                def store(j, s):
                    await_count(sp, adj_out, j + 1)
                    await_count(sp, agg_out, j + 1)
                    sp.dma_start(d["aw"][bass.ds(j, 1)].rearrange("a p k -> p (a k)"),
                                 aw_out[:, s, :]).then_inc(aw_stored[s], 16)
                    sp.dma_start(d["agg"][:, bass.ds(j * W, W)],
                                 agg_win[:, s, :]).then_inc(agg_stored[s], 16)
                    sp.dma_start(d["deg"][:, bass.ds(j * W, W)],
                                 deg_win[:, s, :]).then_inc(agg_stored[s], 16)

                def load(j, s):
                    start = sp.value_load(d["starts"][0:1, bass.ds(j, 1)], min_val=0, max_val=E)
                    if not isinstance(j, int) or j >= S:
                        store(j - S, s)
                    sp.dma_start(rec[:, s, :], d["records"][bass.ds(start, BLK), :].rearrange(
                        "(p k) c -> p (k c)", p=P)).then_inc(rec_in[s], 16)
                    await_count(sp, pre, j - 1)
                    sp.dma_start(lhs[0:ED, s % 2, :], d["ea"][:, bass.ds(start, BLK)]).then_inc(lhs_in[s], 16)
                    sp.dma_start(dst_row[ED:ED + W, s % 2, :], d["dst_row"][bass.ds(start, BLK)].rearrange(
                        "(a e) -> a e", a=1).broadcast_to([W, BLK])).then_inc(lhs_in[s], 16)
                    sp.dma_start(rhs[ED:ED + W, s, :], d["Q"][bass.ds(j * W, W), :]).then_inc(lhs_in[s], 16)

                with sp.If(d["crowded"]["SP"] < 1):
                    for s in range(S):
                        sp.dma_start(rhs[0:ED, s, :], d["L0_W1"][2 * D:2 * D + ED, :]).then_inc(w_in, 16)
                    by_window(sp, load)
                    for s in range(S):
                        store(J - S + s, s)
                    for s in range(S):
                        sp.wait_ge(aw_stored[s], 16 * (J // S))
                        sp.wait_ge(agg_stored[s], 32 * (J // S))

            @block.gpsimd
            def _(pool):
                nc.gpsimd.iota(key0[:, :], [[NKEY, J]], base=0, channel_multiplier=0,
                               allow_small_or_imprecise_dtypes=True).then_inc(consts, 1)
                nc.gpsimd.iota(dst_of[:, :], [[W, J]], base=-ED, channel_multiplier=1,
                               allow_small_or_imprecise_dtypes=True).then_inc(consts, 1)
                nc.gpsimd.iota(iota_d[:, :], [[NT, W]], base=0, channel_multiplier=0,
                               allow_small_or_imprecise_dtypes=True).then_inc(consts, 1)
                nc.gpsimd.iota(iota_lo[:, :], [[1, P]], base=0, channel_multiplier=0,
                               allow_small_or_imprecise_dtypes=True).then_inc(consts, 1)
                nc.gpsimd.iota(iota_key[:, :], [[1, NKEY]], base=0, channel_multiplier=0,
                               allow_small_or_imprecise_dtypes=True).then_inc(consts, 1)

                def gather(j, s):
                    await_count(pool, rec_in[s], uses(j, s, 16) + 16)
                    await_count(pool, sums, j - S + 1)
                    for k in range(CH):
                        at = k * REC + R_SRC
                        nc.gpsimd.indirect_dma_start(
                            msg[:, s, k, :], None, d["P"],
                            bass.IndirectOffsetOnAxis(ap=rec[:, s, at:at + 1].bitcast(I32), axis=0)
                        ).then_inc(gathered[s], 16)

                nc.gpsimd.memset(wts[:, :, :, 2:3], 0.0).then_inc(consts, 1)
                nc.gpsimd.memset(wts[:, :, :, 3:4], UP).then_inc(consts, 1)
                with pool.If(d["crowded"]["Pool"] < 1):
                    by_window(pool, gather)

            @block.vector
            def _(dve):
                def one_hots(j, s):
                    u = s % 2
                    row = rec[:, s, :].rearrange("p (k c) -> p k c", c=REC)
                    await_count(dve, rec_in[s], uses(j, s, 16) + 16)
                    await_count(dve, multiplied, j - 1)
                    await_count(dve, sums, j - S + 1)
                    nc.vector.tensor_scalar(key[:, s], row[:, :, 0:2], key0[:, bass.ds(j, 1)], None,
                                            ALU.subtract).then_inc(keyed, 1)
                    nc.vector.tensor_copy(wts[:, s, :, 0:2], row[:, :, R_W1:R_W2 + 1])
                    for k in range(CH):
                        lo = row[:, k, R_LO:R_LO + 1]
                        last = nc.vector.tensor_scalar(hot_lo[:, u, k, 0, :], iota_lo[:, :], lo, None, ALU.is_equal)
                    last.then_inc(hot_los, 1)
                    await_count(dve, keyed, j + 1)
                    for k in range(CH):
                        nc.vector.tensor_scalar(hot_key[:, u, k, :], iota_key[:, :], key[:, s, k, 0:1], None,
                                                ALU.is_equal)
                    lhs_d = iota_d[:, :].rearrange("p (a w) -> p a w", a=1).broadcast_to([P, CH, W])
                    rhs_d = key[:, s, :, 1:2].broadcast_to([P, CH, W])
                    nc.vector.tensor_tensor(hot_d[:, s], lhs_d, rhs_d, ALU.is_equal)
                    nc.vector.tensor_tensor(hot_db[:, s], lhs_d, rhs_d, ALU.is_equal).then_inc(hots, 1)
                    await_count(dve, lhs_in[s], uses(j, s, 48) + 48)
                    nc.vector.tensor_scalar(lhs[ED:ED + W, s % 2, :], dst_row[ED:ED + W, s % 2, :],
                                            dst_of[ED:ED + W, bass.ds(j, 1)], None, ALU.is_equal).then_inc(hot_t, 1)

                def add(j, s):
                    await_count(dve, pre, j + 1)
                    await_count(dve, gathered[s], uses(j, s, 16 * CH) + 16 * CH)
                    out = msg[:, s].rearrange("p k f -> p (k f)")
                    nc.vector.tensor_tensor(out, psum[:, 4:6, :].rearrange("p b f -> p (b f)")[:, 0:BLK], out,
                                            ALU.add).then_inc(summed, 1)

                def step(j, s):
                    one_hots(j, s)
                    if not isinstance(j, int) or j > 0:
                        add(j - 1, before(s))

                dve.wait_ge(consts, 7)
                with dve.If(d["crowded"]["DVE"] < 1):
                    by_window(dve, step)
                    add(J - 1, S - 1)

            @block.scalar
            def _(act):
                def relu_of(j, s):
                    await_count(act, summed, j + 1)
                    nc.scalar.activation(msg[:, s], msg[:, s], ACT.Relu).then_inc(relued, 1)

                def matrix_out(j, s):
                    await_count(act, multiplied, j + 1)
                    await_count(act, aw_stored[s], uses(j, s, 16))
                    nc.scalar.copy(adj[:, :, bass.ds(j * W, W)], counts_of(s).rearrange("p (w t) -> p t w", t=NT))
                    nc.scalar.activation(aw_out[:, s, :].rearrange("p (t w) -> p t w", w=W),
                                         weights_of(s).rearrange("p (w t) -> p t w", t=NT), ACT.Copy,
                                         scale=1 / UP).then_inc(adj_out, 1)

                def sums_out(j, s):
                    await_count(act, sums, j + 1)
                    await_count(act, agg_stored[s], uses(j, s, 32))
                    nc.scalar.copy(agg_win[:, s, :], psum[:, 6 + s % 2, 0:W])
                    nc.scalar.activation(deg_win[:, s, :], psum[0:4, 6 + s % 2, 32:32 + W], ACT.Copy,
                                         scale=1 / UP).then_inc(agg_out, 1)

                def weigh(j, s):
                    row = rec[:, s, :].rearrange("p (k c) -> p k c", c=REC)
                    await_count(act, hot_los, j + 1)
                    for k in range(CH):
                        for q in range(2):
                            last = nc.scalar.activation(hot_lo[:, s % 2, k, 1 + q, :], hot_lo[:, s % 2, k, 0, :],
                                                        ACT.Copy, scale=row[:, k, R_W1 + q:R_W1 + q + 1])
                    last.then_inc(weighted, 1)

                def step(j, s):
                    weigh(j, s)
                    if not isinstance(j, int) or j > 1:
                        sums_out(j - 2, before(before(s)))
                    if not isinstance(j, int) or j > 0:
                        matrix_out(j - 1, before(s))
                        relu_of(j - 1, before(s))

                with act.If(d["crowded"]["Activation"] < 1):
                    by_window(act, step)
                    sums_out(J - 2, S - 2)
                    matrix_out(J - 1, S - 1)
                    relu_of(J - 1, S - 1)
                    sums_out(J - 1, S - 1)

            @block.tensor
            def _(pe):
                def multiply(j, s):
                    u = s % 2
                    await_count(pe, hots, j + 1)
                    await_count(pe, adj_out, j - 1)
                    for k in range(CH):
                        nc.tensor.matmul(counts_of(s), hot_lo[:, u, k, 0, :], hot_key[:, u, k, :],
                                         start=(k == 0), stop=(k == CH - 1))
                    await_count(pe, weighted, j + 1)
                    for k in range(CH):
                        for q in range(2):
                            last = nc.tensor.matmul(weights_of(s), hot_lo[:, u, k, 1 + q, :], hot_key[:, u, k, :],
                                                    start=(k == 0 and q == 0), stop=(k == CH - 1 and q == 1))
                    last.then_inc(multiplied, 1)
                    await_count(pe, hot_t, j + 1)
                    await_count(pe, summed, j)
                    for k in range(CH):
                        last = nc.tensor.matmul(pre_of(k), lhs[:, s % 2, k:BLK:CH], rhs[:, s, :],
                                                start=True, stop=True)
                    last.then_inc(pre, 1)
                    await_count(pe, agg_out, j - 1)
                    for k in range(CH):
                        nc.tensor.matmul(psum[0:4, 6 + u, 32:32 + W], wts[:, s, k, :], hot_db[:, s, k, :],
                                         start=(k == 0), stop=(k == CH - 1))

                def sum_up(j, s):
                    u = s % 2
                    await_count(pe, relued, j + 1)
                    for k in range(CH):
                        last = nc.tensor.matmul(psum[:, 6 + u, 0:W], msg[:, s, k, :], hot_d[:, s, k, :],
                                                start=(k == 0), stop=(k == CH - 1))
                    last.then_inc(sums, 1)

                def step(j, s):
                    multiply(j, s)
                    if not isinstance(j, int) or j > 0:
                        sum_up(j - 1, before(s))

                with pe.If(d["crowded"]["PE"] < 1):
                    pe.wait_ge(w_in, 16 * S)
                    by_window(pe, step)
                    sum_up(J - 1, S - 1)



def crowded_edge_pass(nc, new, d):
    R = -(-E // BLK)
    STEPS = 10
    with ExitStack() as ctx:
        def sb(name, shape, dt):
            return ctx.enter_context(nc.sbuf_tensor("any_" + name, shape, dt))

        def sem(name):
            return new("any_" + name)

        psum = d["psum"]
        rec = sb("rec", [P, CH * REC], F32)
        lhs = sb("lhs", [ED + W, BLK], F32)
        rhs = sb("rhs", [ED + W, D], F32)
        dst_row = sb("dst_row", [ED + W, BLK], F32)
        msg = sb("msg", [P, CH, D], F32)
        key = sb("key", [P, CH, 2], F32)
        wts = sb("wts", [P, CH, 4], BF16)
        w3 = sb("w3", [P, 3, CH], F32)
        hot_d = sb("hot_d", [P, CH, W], F32)
        hot_db = sb("hot_db", [P, CH, W], BF16)
        hot_lo = sb("hot_lo", [P, CH, 4, P], BF16)
        hot_key = sb("hot_key", [P, CH, NKEY], BF16)
        matrix = sb("matrix", [P, 2, NKEY], F32)
        agg_win = sb("agg_win", [P, W], F32)
        deg_win = sb("deg_win", [4, W], F32)
        key0 = sb("key0", [P, J], F32)
        dst_of = sb("dst_of", [P, J], F32)
        iota_d = sb("iota_d", [P, W], F32)
        iota_lo = sb("iota_lo", [P, P], BF16)
        iota_key = sb("iota_key", [P, NKEY], F16)

        consts, w_in, loaded, gathered = sem("consts"), sem("w_in"), sem("loaded"), sem("gathered")
        hots, multiplied, relued, sums = sem("hots"), sem("multiplied"), sem("relued"), sem("sums")
        rec_in, p_stored = sem("rec_in"), sem("p_stored")
        block_done, cleared, stored, out_free = sem("block_done"), sem("cleared"), sem("stored"), sem("out_free")
        dve_step, pace = sem("dve_step"), sem("pace")

        def await_count(eng, sem, count):
            eng.wait_ge(sem, count)
            eng.sem_inc(pace, 1)

        with nc.Block() as block:
            @block.sync
            def _(sp):
                with sp.If(d["crowded"]["SP"] >= 1):
                    sp.dma_start(rhs[0:ED, :], d["L0_W1"][2 * D:2 * D + ED, :]).then_inc(w_in, 16)
                    sp.wait_ge(w_in, 16)
                    sp.sem_inc(out_free, 1)
                    with sp.Fori(0, J) as j:
                        with sp.Fori(0, R) as r:
                            await_count(sp, block_done, j * R + r + 1)
                            sp.dma_start(rec[:, :], d["records"][bass.ds(r * BLK, BLK), :].rearrange(
                                "(p k) c -> p (k c)", p=P)).then_inc(loaded, 16)
                            sp.dma_start(lhs[0:ED, :], d["ea"][:, bass.ds(r * BLK, BLK)]).then_inc(loaded, 16)
                            sp.dma_start(dst_row[ED:ED + W, :], d["dst_row"][bass.ds(r * BLK, BLK)].rearrange(
                                "(a e) -> a e", a=1).broadcast_to([W, BLK])).then_inc(loaded, 16)
                            sp.dma_start(rhs[ED:ED + W, :], d["Q"][bass.ds(j * W, W), :]).then_inc(loaded, 16)
                            sp.dma_start(msg[:, :, :], d["P_src"][bass.ds(r * BLK, BLK), :].rearrange(
                                "(p k) f -> p k f", p=P)).then_inc(loaded, 16)
                        await_count(sp, block_done, (j + 1) * R + 1)
                        sp.dma_start(d["counts"][bass.ds(j, 1)].rearrange("a p k -> p (a k)"),
                                     matrix[:, 0]).then_inc(stored, 16)
                        sp.dma_start(d["aw"][bass.ds(j, 1)].rearrange("a p k -> p (a k)"),
                                     matrix[:, 1]).then_inc(stored, 16)
                        sp.dma_start(d["agg"][:, bass.ds(j * W, W)], agg_win[:, :]).then_inc(stored, 16)
                        sp.dma_start(d["deg"][:, bass.ds(j * W, W)], deg_win[:, :]).then_inc(stored, 16)
                        await_count(sp, stored, (j + 1) * 64)
                        sp.sem_inc(out_free, 1)

            @block.gpsimd
            def _(pool):
                with pool.If(d["crowded"]["Pool"] >= 1):
                    for out, pattern, base, rows in (
                            (key0, [[NKEY, J]], 0, 0), (dst_of, [[W, J]], -ED, 1), (iota_d, [[NT, W]], 0, 0),
                            (iota_lo, [[1, P]], 0, 0), (iota_key, [[1, NKEY]], 0, 0)):
                        nc.gpsimd.iota(out[:, :], pattern, base=base, channel_multiplier=rows,
                                       allow_small_or_imprecise_dtypes=True).then_inc(consts, 1)
                    nc.gpsimd.memset(wts[:, :, 3:4], 1.0).then_inc(consts, 1)
                    with pool.Fori(0, R) as r:
                        pool.dma_start(rec[:, :], d["records"][bass.ds(r * BLK, BLK), :].rearrange(
                            "(p k) c -> p (k c)", p=P)).then_inc(rec_in, 16)
                        await_count(pool, rec_in, (r + 1) * 16)
                        for k in range(CH):
                            at = k * REC + R_SRC
                            nc.gpsimd.indirect_dma_start(
                                msg[:, k, :], None, d["P"],
                                bass.IndirectOffsetOnAxis(ap=rec[:, at:at + 1].bitcast(I32), axis=0)
                            ).then_inc(gathered, 16)
                        await_count(pool, gathered, (r + 1) * 16 * CH)
                        pool.dma_start(d["P_src"][bass.ds(r * BLK, BLK), :].rearrange("(p k) f -> p k f", p=P),
                                       msg[:, :, :]).then_inc(p_stored, 16)
                        await_count(pool, p_stored, (r + 1) * 16)
                    pool.sem_inc(block_done, 1)

            @block.vector
            def _(dve):
                def block_of(j, n):
                    steps = [0]

                    def link(ins):
                        steps[0] += 1
                        ins.then_inc(dve_step, 1)
                        await_count(dve, dve_step, n * STEPS + steps[0])

                    row = rec[:, :].rearrange("p (k c) -> p k c", c=REC)
                    await_count(dve, loaded, (n + 1) * 80)
                    w, rest = row[:, :, R_W], w3[:, 2]
                    link(nc.vector.tensor_copy(wts[:, :, 0], w))
                    nc.vector.tensor_copy(w3[:, 0], wts[:, :, 0])
                    link(nc.vector.tensor_tensor(rest, w, wts[:, :, 0], ALU.subtract))
                    link(nc.vector.tensor_copy(wts[:, :, 1], rest))
                    nc.vector.tensor_copy(w3[:, 1], wts[:, :, 1])
                    link(nc.vector.tensor_tensor(rest, rest, wts[:, :, 1], ALU.subtract))
                    nc.vector.tensor_copy(wts[:, :, 2], rest)
                    for k in range(CH):
                        lo = row[:, k, R_LO:R_LO + 1]
                        nc.vector.tensor_scalar(hot_lo[:, k, 0, :], iota_lo[:, :], lo, None, ALU.is_equal)
                        for q in range(3):
                            nc.vector.tensor_scalar(hot_lo[:, k, 1 + q, :], iota_lo[:, :], lo,
                                                    w3[:, q, k:k + 1], ALU.is_equal, ALU.mult)
                    nc.vector.tensor_scalar(lhs[ED:ED + W, :], dst_row[ED:ED + W, :], dst_of[ED:ED + W, bass.ds(j, 1)],
                                            None, ALU.is_equal)
                    link(nc.vector.tensor_scalar(key[:, :], row[:, :, 0:2], key0[:, bass.ds(j, 1)], None,
                                                 ALU.subtract))
                    for k in range(CH):
                        nc.vector.tensor_scalar(hot_key[:, k, :], iota_key[:, :], key[:, k, 0:1], None,
                                                ALU.is_equal)
                    lhs_d = iota_d[:, :].rearrange("p (a w) -> p a w", a=1).broadcast_to([P, CH, W])
                    rhs_d = key[:, :, 1:2].broadcast_to([P, CH, W])
                    nc.vector.tensor_tensor(hot_d[:, :], lhs_d, rhs_d, ALU.is_equal)
                    link(nc.vector.tensor_tensor(hot_db[:, :], lhs_d, rhs_d, ALU.is_equal))
                    dve.sem_inc(hots, 1)
                    await_count(dve, multiplied, n + 1)
                    out = msg[:, :].rearrange("p k f -> p (k f)")
                    link(nc.vector.tensor_tensor(out, psum[:, 4:6, :].rearrange("p b f -> p (b f)")[:, 0:BLK], out,
                                                 ALU.add))
                    link(nc.vector.tensor_scalar(out, out, 0.0, None, ALU.max))
                    dve.sem_inc(relued, 1)
                    for q in range(2):
                        link(nc.vector.tensor_tensor(
                            matrix[:, q].rearrange("p (t w) -> p t w", w=W), matrix[:, q].rearrange(
                                "p (t w) -> p t w", w=W),
                            psum[:, 2 * q, 0:NKEY].rearrange("p (w t) -> p t w", t=NT), ALU.add))
                    assert steps[0] == STEPS
                    await_count(dve, sums, n + 1)
                    nc.vector.tensor_tensor(agg_win[:, :], agg_win[:, :], psum[:, 6, 0:W], ALU.add)
                    nc.vector.tensor_tensor(deg_win[:, :], deg_win[:, :], psum[0:4, 7, 0:W], ALU.add)
                    dve.drain().then_inc(block_done, 1)
                    await_count(dve, block_done, n + 2)

                with dve.If(d["crowded"]["DVE"] >= 1):
                    dve.wait_ge(consts, 6)
                    with dve.Fori(0, J) as j:
                        await_count(dve, out_free, j + 1)
                        for out in (matrix[:, :], agg_win[:, :], deg_win[:, :]):
                            nc.vector.memset(out, 0.0).then_inc(cleared, 1)
                        await_count(dve, cleared, (j + 1) * 3)
                        with dve.Fori(0, R) as r:
                            block_of(j, j * R + r)

            @block.tensor
            def _(pe):
                with pe.If(d["crowded"]["PE"] >= 1):
                    with pe.Fori(0, J) as j:
                        with pe.Fori(0, R) as r:
                            n = j * R + r
                            await_count(pe, hots, n + 1)
                            for k in range(CH):
                                nc.tensor.matmul(psum[:, 0, 0:NKEY], hot_lo[:, k, 0, :], hot_key[:, k, :],
                                                 start=(k == 0), stop=(k == CH - 1))
                            for k in range(CH):
                                for q in range(3):
                                    nc.tensor.matmul(psum[:, 2, 0:NKEY], hot_lo[:, k, 1 + q, :], hot_key[:, k, :],
                                                     start=(k == 0 and q == 0), stop=(k == CH - 1 and q == 2))
                            for k in range(CH):
                                nc.tensor.matmul(psum[:, 4 + k // 4, (k % 4) * D:(k % 4 + 1) * D], lhs[:, k:BLK:CH],
                                                 rhs[:, :], start=True, stop=True)
                            for k in range(CH):
                                last = nc.tensor.matmul(psum[0:4, 7, 0:W], wts[:, k, :], hot_db[:, k, :],
                                                        start=(k == 0), stop=(k == CH - 1))
                            last.then_inc(multiplied, 1)
                            await_count(pe, relued, n + 1)
                            for k in range(CH):
                                last = nc.tensor.matmul(psum[:, 6, 0:W], msg[:, k, :], hot_d[:, k, :],
                                                        start=(k == 0), stop=(k == CH - 1))
                            last.then_inc(sums, 1)


def counts_slab(d):
    return d["adj"][:, :, :].rearrange("p t n -> p (t n)").bitcast(F32)[:, 0:SLABS * WG * NKEY].rearrange(
        "p (s j k) -> p s j k", s=SLABS, k=NKEY)


def h_copy(d):
    return counts_slab(d)[:, SLABS - 1].rearrange("p j k -> p (j k)")[:, 0:NT * D].rearrange("p (t f) -> p t f", f=D)


class Norm:

    def __init__(self, nc, new, sb, name):
        self.nc = nc
        self.stats = sb(name + "_stats", [P, GT, 6], F32)
        self.mv = sb(name + "_mv", [P, GT, 2], F32)
        self.std = sb(name + "_std", [P, GT], F32)
        self.varied, self.rooted = new(name + "_varied"), new(name + "_rooted")

    def on_vector(self, dve, link, out, x, c):
        nc, n = self.nc, len(tiles_of(c))
        for i in range(n):
            last = nc.vector.bn_stats(self.stats[:, i, :], x[:, i, :])
        link(last)
        for i in range(n):
            last = nc.vector.bn_aggr(self.mv[:, i, :], self.stats[:, i, :])
        last.then_inc(self.varied, 1)
        dve.wait_ge(self.rooted, c + 1)
        link(nc.vector.reciprocal(self.std[:, 0:n], self.std[:, 0:n]))
        for i in range(n):
            last = nc.vector.tensor_scalar(out[:, i, :], x[:, i, :], self.mv[:, i, 0:1], self.std[:, i:i + 1],
                                           ALU.subtract, ALU.mult)
        return last

    def on_scalar(self, act, eps, c):
        n = len(tiles_of(c))
        act.wait_ge(self.varied, c + 1)
        self.nc.scalar.activation(self.std[:, 0:n], self.mv[:, 0:n, 1], ACT.Sqrt,
                                  bias=eps[:, 0:1]).then_inc(self.rooted, 1)


def schedule(lag=1):
    steps = [("sum", 0)]
    for c in range(1, G - 1):
        steps += [("sum", c), ("tail", c - 1)]
    return steps + [("tail", G - 2), ("sum", G - 1)] + [("tail", c) for c in range(G - 1, G - 1 + lag)]


class Parts:

    def __init__(self, buffer, width, up=UP, down=1 / UP):
        self.up, self.down = up, down
        self.width, self.block = width, 2 * width
        self.flat = buffer[:, 0:NT * self.block]
        self.spare = buffer[:, :].bitcast(F32)[:, NT * D:]
        self.tiles = self.flat.rearrange("p (t f) -> p t f", f=self.block)
        self.rows = 2 * width if width == M2 else width
        self.taken = [(0, 2 * width)] if width == M2 else [(0, width), (width, width)]

    def down_of(self, rows):
        return self.down if isinstance(self.down, float) else self.down[0:rows]

    def of(self, q, tiles):
        return self.tiles[:, tiles, q * self.width:(q + 1) * self.width]


class Split:

    def __init__(self, nc, new, name, v, parts, squares=None, trash=None):
        self.nc, self.v, self.parts, self.squares, self.trash = nc, v, parts, squares, trash
        self.given, self.relued, self.hi = new(name + "_given"), new(name + "_relued"), new(name + "_hi")
        self.done = new(name + "_cut")
        self.squared = new(name + "_squared")

    def on_scalar(self, act, c):
        n, tiles = len(tiles_of(c)), slice(tiles_of(c)[0], tiles_of(c)[-1] + 1)
        v = self.v[:, 0:n, 0:self.parts.width]
        act.wait_ge(self.given, c + 1)
        self.nc.scalar.activation(v, v, ACT.Relu, scale=self.parts.up).then_inc(self.relued, 1)
        act.wait_ge(self.relued, c + 1)
        self.nc.scalar.copy(self.parts.of(0, tiles), v).then_inc(self.hi, 1)
        if self.squares is not None:
            for i, t in enumerate(tiles_of(c)):
                if t:
                    act.wait_ge(self.squared, t)
                self.nc.scalar.activation(self.trash[:, :], v[:, i, :], ACT.Square, scale=self.parts.down,
                                          accum_out=self.squares[:, t:t + 1]).then_inc(self.squared, 1)

    def on_vector(self, dve, c):
        n, tiles = len(tiles_of(c)), slice(tiles_of(c)[0], tiles_of(c)[-1] + 1)
        v = self.v[:, 0:n, 0:self.parts.width]
        dve.wait_ge(self.hi, c + 1)
        if self.squares is not None:
            dve.wait_ge(self.squared, tiles_of(c)[-1] + 1)
        self.nc.vector.tensor_tensor(self.parts.of(1, tiles), v, self.parts.of(0, tiles),
                                     ALU.subtract).then_inc(self.done, 1)
        dve.wait_ge(self.done, c + 1)


def first_tail(nc, new, d):
    SLOTS = 3
    with ExitStack() as ctx:
        def sb(name, shape, dt):
            return ctx.enter_context(nc.sbuf_tensor(name, shape, dt))

        psum, ident, ones = d["psum"], d["ident"], d["ones"]
        free = d["parts_b"][:, :].bitcast(F32)
        one = GT * P
        deg_row = free[0:1, 0:SLOTS * one].rearrange("p (a n) -> p a n", a=SLOTS)
        mT = free[:, SLOTS * one:(SLOTS + 2) * one].rearrange("p (a n) -> p a n", a=2)
        h0 = free[:, (SLOTS + 2) * one:(2 * SLOTS + 2) * one].rearrange("p (a t f) -> p a t f", a=SLOTS, f=D)
        agg = d["h_out"].spare[:, 0:SLOTS * one].rearrange("p (a n) -> p a n", a=SLOTS)
        deg_rows = sb("deg_rows", [4 * NT, P], F32)
        x = sb("x_group", [P, SLOTS, GT, D], F32)
        w2, wu = sb("w2", [D, D], F32), sb("wu", [D, D], F32)
        b2, bu = sb("b2_row", [1, D], F32), sb("bu_row", [1, D], F32)
        gamma, beta = sb("gamma_rows", [P, D], F32), sb("beta_rows", [P, D], F32)
        wsum, positive = sb("wsum", [P, NT], F32), sb("positive", [P, NT], F32)
        v = sb("v_group", [P, GT, D], F32)
        split = Split(nc, new, "t_split", v, d["h_out"])
        norm_y, norm_x = Norm(nc, new, sb, "ty"), Norm(nc, new, sb, "tx")

        w_in, deg_in, cleared = new("t_w_in"), new("t_deg_in"), new("t_cleared")
        agg_in = [new(f"t_agg_in{slot}") for slot in range(SLOTS)]
        node_in, x_stored = ([new(f"t_{name}{slot}") for slot in range(SLOTS)] for name in ("node_in", "x_stored"))
        deg_t, wsum_ready, wroot = new("t_deg_t"), new("t_wsum"), new("t_wroot")
        m_psum, m_sb, u_psum = new("t_m_psum"), new("t_m_sb"), new("t_u_psum")
        y_ready, x_ready, normed = new("t_y"), new("t_x"), new("t_normed")
        dve_sem, pool_sem, y_normed = new("t_dve"), new("t_pool"), new("t_y_normed")

        ident_made = new("t_ident_b")

        with nc.Block() as block:
            @block.gpsimd
            def _(pool):
                nc.gpsimd.tensor_copy(d["ident_b"][:, :], ident[:, :]).then_inc(ident_made, 1)
                pool.wait_ge(ident_made, 1)
                pool.wait_ge(cleared, 3)

                def load_sums(c):
                    n = min(GT * P, NCOL - c * GT * P)
                    if c >= SLOTS:
                        pool.wait_ge(m_psum, c - SLOTS + 1)
                    pool.dma_start(agg[:, c % SLOTS, 0:n], d["agg"][:, c * GT * P:c * GT * P + n]).then_inc(
                        agg_in[c % SLOTS], 16)
                    pool.dma_start(deg_row[:, c % SLOTS, 0:n], d["deg"][3:4, c * GT * P:c * GT * P + n]).then_inc(
                        agg_in[c % SLOTS], 16)

                link = linker(pool, pool_sem)
                for c in range(SLOTS):
                    load_sums(c)
                pool.wait_ge(w_in, 96)
                for c in range(G):
                    if c + SLOTS < G:
                        load_sums(c + SLOTS)
                    n = len(tiles_of(c))
                    y, x_c = h0[:, c % SLOTS, 0:n], x[:, c % SLOTS, 0:n]
                    pool.wait_ge(y_normed, c + 1)
                    for row, op in ((gamma, ALU.mult), (beta, ALU.add)):
                        rows = row[:, :].rearrange("p (a f) -> p a f", a=1).broadcast_to([P, n, D])
                        link(nc.gpsimd.tensor_tensor(y, y, rows, op))
                    nc.gpsimd.tensor_tensor(x_c, x_c, y, ALU.add).then_inc(x_ready, 1)

            @block.sync
            def _(sp):
                def store_x(c):
                    sp.wait_ge(x_ready, c + 1)
                    sp.dma_start(group_ap(d["x1"], c), x[:, c % SLOTS, 0:len(tiles_of(c))]).then_inc(
                        x_stored[c % SLOTS], 16)

                sp.wait_ge(cleared, 1)
                last = NT - 1
                for q in range(4):
                    sp.dma_start(deg_rows[q * NT:q * NT + last, :], d["deg"][q, 0:last * P].rearrange(
                        "(t p) -> t p", p=P)).then_inc(deg_in, 16)
                    sp.dma_start(deg_rows[q * NT + last:(q + 1) * NT, 0:NCOL - last * P],
                                 d["deg"][q:q + 1, last * P:NCOL]).then_inc(deg_in, 16)
                for out, src in ((w2[:, :], d["L0_W2"]), (wu[:, :], d["L0_Wu"])):
                    sp.dma_start(out, src).then_inc(w_in, 16)
                for out, src in ((b2, d["L0_b2"]), (bu, d["L0_bu"])):
                    sp.dma_start(out[:, :], src.rearrange("(a f) -> a f", a=1)).then_inc(w_in, 16)
                for out, src in ((gamma, d["L0_gamma"]), (beta, d["L0_beta"])):
                    sp.dma_start(out[:, :], src.rearrange("(a f) -> a f", a=1).broadcast_to([P, D])
                                 ).then_inc(w_in, 16)
                for c in range(G + 1):
                    if c < G:
                        m, slot = len(tiles_of(c)), c % SLOTS
                        if c >= SLOTS:
                            sp.wait_ge(normed, c - SLOTS + 1)
                            sp.wait_ge(x_stored[slot], 16 * (c // SLOTS))
                        sp.dma_start(h0[:, slot, 0:m], group_ap(d["h0"], c)).then_inc(node_in[slot], 16)
                        sp.dma_start(x[:, slot, 0:m], group_ap(d["x"], c)).then_inc(node_in[slot], 16)
                    if c >= 2:
                        store_x(c - 2)
                store_x(G - 1)
                for slot in range(SLOTS):
                    sp.wait_ge(x_stored[slot], 16 * len(range(slot, G, SLOTS)))

            @block.tensor
            def _(pe):
                pe.wait_ge(deg_in, 16 * 8)
                nc.tensor.transpose(psum[:, 0, 0:4 * NT], deg_rows[:, :], ident[0:4 * NT, 0:4 * NT]).then_inc(deg_t, 1)
                pe.wait_ge(w_in, 96)

                def first_product(c):
                    n, half = len(tiles_of(c)) * P, c % 2
                    pe.wait_ge(agg_in[c % SLOTS], 32 * (c // SLOTS + 1))
                    if c >= 2:
                        pe.wait_ge(m_sb, c - 1)
                    nc.tensor.matmul(psum[:, 1 + half, 0:n], w2[:, :], agg[:, c % SLOTS, 0:n], start=True, stop=False)
                    nc.tensor.matmul(psum[:, 1 + half, 0:n], b2[:, :], deg_row[:, c % SLOTS, 0:n], start=False,
                                     stop=True).then_inc(m_psum, 1)

                first_product(0)
                for c in range(G):
                    if c < G - 1:
                        first_product(c + 1)
                    pe.wait_ge(m_sb, c + 1)
                    if c >= 2:
                        pe.wait_ge(y_ready, c - 1)
                    for i in range(len(tiles_of(c))):
                        out = psum[:, 3 + c % 2, i * D:(i + 1) * D]
                        nc.tensor.matmul(out, mT[:, c % 2, i * P:(i + 1) * P], wu[:, :], start=True, stop=False)
                        last = nc.tensor.matmul(out, ones[0:1, :], bu[:, :], start=False, stop=True)
                    last.then_inc(u_psum, 1)

            @block.scalar
            def _(act):
                act.wait_ge(wsum_ready, 1)
                nc.scalar.activation(wsum[:, :], wsum[:, :], ACT.Sqrt).then_inc(wroot, 1)
                def copy_m(c):
                    n, half = len(tiles_of(c)) * P, c % 2
                    act.wait_ge(m_psum, c + 1)
                    if c >= 2:
                        act.wait_ge(u_psum, c - 1)
                    nc.scalar.copy(mT[:, half, 0:n], psum[:, 1 + half, 0:n]).then_inc(m_sb, 1)

                copy_m(0)
                copy_m(1)
                norm_y.on_scalar(act, d["eps"], 0)
                for c in range(G):
                    if c + 2 < G:
                        copy_m(c + 2)
                    if c + 1 < G:
                        norm_y.on_scalar(act, d["eps"], c + 1)
                    norm_x.on_scalar(act, d["eps"], c)
                    split.on_scalar(act, c)

            @block.vector
            def _(dve):
                link = linker(dve, dve_sem)
                for cleared_buffer in (deg_rows[:, :], deg_row, agg):
                    nc.vector.memset(cleared_buffer, 0.0).then_inc(cleared, 1)
                dve.wait_ge(deg_t, 1)
                parts = psum[:, 0, 0:4 * NT].rearrange("p (q t) -> p q t", q=4)
                link(nc.vector.tensor_scalar(d["eps_deg"][:, :], parts[:, 3], 1.0, None, ALU.max))
                nc.vector.reciprocal(d["inv_deg"][:, :], d["eps_deg"][:, :])
                link(nc.vector.tensor_scalar(wsum[:, :], parts[:, 0], 1.0, None, ALU.add))
                link(nc.vector.tensor_tensor(wsum[:, :], wsum[:, :], parts[:, 1], ALU.add))
                link(nc.vector.tensor_tensor(wsum[:, :], wsum[:, :], parts[:, 2], ALU.add))
                link(nc.vector.tensor_scalar(d["eps_deg"][:, :], d["eps_deg"][:, :], L2_EPS, None, ALU.mult))
                link(nc.vector.tensor_scalar(positive[:, :], wsum[:, :], 0.0, None, ALU.is_gt))
                nc.vector.tensor_scalar(wsum[:, :], wsum[:, :], 1e-38, None, ALU.max).then_inc(wsum_ready, 1)
                dve.wait_ge(wroot, 1)
                link(nc.vector.reciprocal(d["dinv"][:, :], wsum[:, :]))
                link(nc.vector.tensor_tensor(d["dinv"][:, :], d["dinv"][:, :], positive[:, :], ALU.mult))

                def sum_and_norm(c):
                    n = len(tiles_of(c))
                    y = h0[:, c % SLOTS, 0:n]
                    dve.wait_ge(u_psum, c + 1)
                    dve.wait_ge(node_in[c % SLOTS], 32 * (c // SLOTS + 1))
                    link(nc.vector.scalar_tensor_tensor(
                        out=y, in0=psum[:, 3 + c % 2, 0:n * D].rearrange("p (t f) -> p t f", f=D), scalar=0.0, in1=y,
                        op0=ALU.max, op1=ALU.add))
                    dve.sem_inc(y_ready, 1)
                    norm_y.on_vector(dve, link, y, y, c).then_inc(y_normed, 1)

                sum_and_norm(0)
                for c in range(G):
                    if c + 1 < G:
                        sum_and_norm(c + 1)
                    n = len(tiles_of(c))
                    dve.wait_ge(x_ready, c + 1)
                    link(norm_x.on_vector(dve, link, v[:, 0:n], x[:, c % SLOTS, 0:n], c))
                    dve.sem_inc(normed, 1)
                    dve.sem_inc(split.given, 1)
                    split.on_vector(dve, c)


class Layer:

    def __init__(self, nc, new, d, name, ctx, parts):
        self.nc, self.d, self.name, self.ctx, self.parts = nc, d, name, ctx, parts
        self.new = lambda n: new(name + "_" + n)
        self.psum, self.ident, self.ones = d["psum"], d["ident"], d["ones"]
        self.aggT = self.sb("aggT", [P, 2, GT * P], F32)
        self.hT = self.sb("hT", [P, 2, GT * P], F32)
        self.summed, self.agg_sb, self.agg_read = self.new("summed"), self.new("agg_sb"), self.new("agg_read")
        self.ht_psum, self.ht_sb = self.new("ht_psum"), self.new("ht_sb")
        self.w_in, self.counts_in, self.h_copied = self.new("w_in"), self.new("counts_in"), self.new("h_copied")
        self.dve_sem, self.u_psum, self.combined = self.new("dve"), self.new("u_psum"), self.new("combined")

    def sb(self, name, shape, dt):
        return self.ctx.enter_context(self.nc.sbuf_tensor(self.name + "_" + name, shape, dt))

    def sum_group(self, pe, c):
        with pe.If(self.d["crowded"]["PE"] < 1):
            self.sum_from_adj(pe, c)
        with pe.If(self.d["crowded"]["PE"] >= 1):
            self.sum_from_dram(pe, c)

    def sum_from_dram(self, pe, c):
        if c == 0:
            pe.wait_ge(self.h_copied, 2)
        pe.wait_ge(self.counts_in, 16 * (c + 1))
        if c >= 1:
            pe.wait_ge(self.agg_sb, c)
        m, rows = min(WG, J - c * WG), self.parts.rows
        for t in range(NT):
            last = self.nc.tensor.matmul(self.psum[0:rows, 0, 0:m * W], h_copy(self.d)[:, t, 0:rows],
                                         counts_slab(self.d)[:, 0, 0:m, t * W:(t + 1) * W], start=(t == 0),
                                         stop=(t == NT - 1))
        last.then_inc(self.summed, 1)

    def load_counts(self, pool):
        every = slice(0, NT)
        copy = h_copy(self.d)
        with pool.If(self.d["crowded"]["Pool"] >= 1):
            self.nc.gpsimd.memset(copy, 0.0).then_inc(self.h_copied, 1)
            pool.wait_ge(self.h_copied, 1)
            self.nc.gpsimd.tensor_tensor(copy[:, :, 0:self.parts.width], self.parts.of(0, every),
                                         self.parts.of(1, every), ALU.add).then_inc(self.h_copied, 1)
            for c in range(G):
                m = min(WG, J - c * WG)
                if c >= 1:
                    pool.wait_ge(self.summed, c)
                pool.dma_start(counts_slab(self.d)[:, 0, 0:m, :], self.d["counts"][c * WG:c * WG + m].rearrange(
                    "j p k -> p j k")).then_inc(self.counts_in, 16)

    def sum_from_adj(self, pe, c):
        nc, adj, parts = self.nc, self.d["adj"], self.parts
        n = min(GT * P, NCOL - c * GT * P)
        flat_adj = adj[:, :, :].rearrange("p t n -> p (t n)")
        last_taken = len(parts.taken) - 1
        if c >= 1:
            pe.wait_ge(self.agg_sb, c)

        def tile_sum(t, start=False, stop=False):
            for q, (at, width) in enumerate(parts.taken):
                last = nc.tensor.matmul(self.psum[0:width, 0, 0:n], parts.flat[:, bass.ds(t * parts.block + at, width)],
                                        flat_adj[:, bass.ds(t * NCOL + c * GT * P, n)], start=start and q == 0,
                                        stop=stop and q == last_taken)
            return last

        rounds = (NT - 2) // UNROLL
        tile_sum(0, start=True)
        with pe.Fori(0, rounds) as i:
            for k in range(UNROLL):
                tile_sum(i * UNROLL + (1 + k))
        for t in range(1 + rounds * UNROLL, NT):
            last = tile_sum(t, stop=(t == NT - 1))
        last.then_inc(self.summed, 1)

    def copy_sums(self, act, c):
        n, rows = min(GT * P, NCOL - c * GT * P), self.parts.rows
        act.wait_ge(self.summed, c + 1)
        if c >= 2:
            act.wait_ge(self.agg_read, c - 1)
        self.nc.scalar.activation(self.aggT[0:rows, c % 2, 0:n], self.psum[0:rows, 0, 0:n], ACT.Copy,
                                  scale=self.parts.down_of(rows)).then_inc(self.agg_sb, 1)

    def transpose_h(self, pe, c):
        transpose_parts(self.nc, self.d, self.parts, pe, c, self.ht_psum, self.ht_sb)

    def copy_ht(self, act, c):
        n, rows = len(tiles_of(c)) * P, self.parts.rows
        act.wait_ge(self.ht_psum, c + 1)
        if c >= 2:
            act.wait_ge(self.u_psum, c - 1)
        self.nc.scalar.activation(self.hT[0:rows, c % 2, 0:n], self.psum[0:rows, 1, 0:n], ACT.Copy,
                                  scale=self.parts.down_of(rows)).then_inc(self.ht_sb, 1)


def transpose_parts(nc, d, parts, pe, c, ht_psum, ht_sb, banks=(1,)):
    if c >= len(banks):
        pe.wait_ge(ht_sb, c + 1 - len(banks))
    bank = banks[c % len(banks)]
    for i, t in enumerate(tiles_of(c)):
        for q, (at, width) in enumerate(parts.taken):
            last = nc.tensor.matmul(d["psum"][0:width, bank, i * P:(i + 1) * P], parts.tiles[:, t, at:at + width],
                                    d["ident_b"][:, :], start=(q == 0), stop=(q == len(parts.taken) - 1))
    last.then_inc(ht_psum, 1)


def wide_layer(nc, new, d):
    with ExitStack() as ctx:
        L = Layer(nc, new, d, "wide", ctx, d["h_in"])
        psum = L.psum
        w1l, w1r = L.sb("w1l", [D, H1], F32), L.sb("w1r", [D, H1], F32)
        w2 = L.sb("w2", [P, 2, 2 * M2], F32)
        h1T = d["h1T"]
        b2 = L.sb("b2", [1, M2], F32)
        h1, b1, v, z = d["h1"], d["b1_wide"], d["y_group"], d["z"]
        out = d["h_out"]
        relued, t_psum, t_sb, yz_psum = L.new("relued"), L.new("t_psum"), L.new("t_sb"), L.new("yz_psum")
        given, hi, done = L.new("given"), L.new("hi"), L.new("cut")
        w1_sq, norms = d["w1_sq"], L.sb("norms", [P, 2, 2], F32)
        b1_col, b1_abs, reach = (L.sb(name, [P, 2], F32) for name in ("b1_col", "b1_abs", "reach"))
        w2_reach, bounds = L.sb("w2_reach", [P, 2, 2 * M2], F32), L.sb("bounds", [P, 2, M2], F32)
        b2_rows, b2_abs = L.sb("b2_rows", [P, M2], F32), L.sb("b2_abs", [P, M2], F32)
        w_squared, w_norms, w_rooted, reached, bounded = (L.new(name) for name in (
            "w_squared", "w_norms", "w_rooted", "reached", "bounded"))
        with nc.Block() as block:
            @block.sync
            def _(sp):
                sp.dma_start(w1l[:, :], d["L1_W1l"]).then_inc(L.w_in, 16)
                sp.dma_start(w1r[:, :], d["L1_W1r"]).then_inc(L.w_in, 16)
                sp.dma_start(b1, d["L1_b1"].rearrange("(a f) -> a f", a=1).broadcast_to([P, H1])).then_inc(L.w_in, 16)
                sp.dma_start(b2[:, :], d["L1_b2"].rearrange("(a f) -> a f", a=1)).then_inc(L.w_in, 16)
                for k in range(2):
                    sp.dma_start(b1_col[:, k:k + 1], d["L1_b1"][k * P:(k + 1) * P].rearrange("(p a) -> p a", a=1)
                                 ).then_inc(L.w_in, 16)
                sp.dma_start(b2_rows[:, :], d["L1_b2"].rearrange("(a f) -> a f", a=1).broadcast_to([P, M2])
                             ).then_inc(L.w_in, 16)
                sp.dma_start(w2[:, :, 0:M2], d["L1_W2l"].rearrange("(k p) f -> p k f", p=P)).then_inc(L.w_in, 16)
                sp.dma_start(w2[:, :, M2:2 * M2], d["L1_W2r"].rearrange("(k p) f -> p k f", p=P)).then_inc(L.w_in, 16)

            @block.gpsimd
            def _(pool):
                L.load_counts(pool)

            @block.tensor
            def _(pe):
                def products(c):
                    if c == 0:
                        pe.wait_ge(L.w_in, 144)
                    pe.wait_ge(L.agg_sb, c + 1)
                    pe.wait_ge(L.ht_sb, c + 1)
                    if c >= 1:
                        pe.wait_ge(L.combined, c)
                    for i in range(len(tiles_of(c))):
                        at = slice((i % 2) * H1, (i % 2 + 1) * H1)
                        nc.tensor.matmul(psum[:, 2 + i // 2, at], L.aggT[:, c % 2, i * P:(i + 1) * P], w1l[:, :],
                                         start=True, stop=True)
                        last = nc.tensor.matmul(psum[:, 4 + i // 2, at], L.hT[:, c % 2, i * P:(i + 1) * P],
                                                w1r[:, :], start=True, stop=True)
                    last.then_inc(L.u_psum, 1)

                def transposes(c):
                    pe.wait_ge(relued, c + 1)
                    if c >= 1:
                        pe.wait_ge(t_sb, c)
                    for i in range(len(tiles_of(c))):
                        for k in range(2):
                            at = (2 * i + k) % 4
                            last = nc.tensor.transpose(psum[:, 6 + i // 2, at * P:(at + 1) * P],
                                                       h1[:, i, k * P:(k + 1) * P], L.ident[:, :])
                    last.then_inc(t_psum, 1)

                def second(c, transposed):
                    pe.wait_ge(t_sb, c + 1)
                    pe.wait_ge(L.ht_sb, transposed)
                    if c >= 1:
                        pe.wait_ge(given, c)
                    for i in range(len(tiles_of(c))):
                        out = psum[:, 1, i * 2 * M2:(i + 1) * 2 * M2]
                        nc.tensor.matmul(out, h1T[:, i, 0, :], w2[:, 0, :], start=True, stop=False)
                        nc.tensor.matmul(out, h1T[:, i, 1, :], w2[:, 1, :], start=False, stop=False)
                        last = nc.tensor.matmul(out[:, M2:2 * M2], L.ones[0:1, :], b2[:, :], start=False, stop=True)
                    last.then_inc(yz_psum, 1)

                summed_groups = 0
                for step, c in schedule(lag=3):
                    if step == "sum":
                        seconds = G - 3 if c == G - 1 else c - 3
                        if seconds > 0:
                            pe.wait_ge(given, seconds)
                        L.transpose_h(pe, c)
                        L.sum_group(pe, c)
                        summed_groups += 1
                        if c == 0:
                            pe.wait_ge(w_squared, 1)
                            for q in range(2):
                                for k in range(2):
                                    last = nc.tensor.matmul(psum[:, 6, 2 * q + k:2 * q + k + 1],
                                                            w1_sq[:, q, k * P:(k + 1) * P], L.ones[:, 0:1],
                                                            start=True, stop=True)
                            last.then_inc(w_norms, 1)
                        if c == 1:
                            pe.wait_ge(reached, 1)
                            nc.tensor.matmul(psum[:, 7, 0:2 * M2], L.ones[:, :], w2_reach[:, 0, :], start=True,
                                             stop=False)
                            nc.tensor.matmul(psum[:, 7, 0:2 * M2], L.ones[:, :], w2_reach[:, 1, :], start=False,
                                             stop=True).then_inc(bounded, 1)
                        continue
                    if c >= 2:
                        second(c - 2, summed_groups)
                    if 1 <= c <= G:
                        transposes(c - 1)
                    if c < G:
                        products(c)

            @block.scalar
            def _(act):
                def cut(c):
                    n, tiles = len(tiles_of(c)), slice(tiles_of(c)[0], tiles_of(c)[-1] + 1)
                    act.wait_ge(given, c + 1)
                    nc.scalar.copy(out.of(0, tiles), v[:, 0:n, :]).then_inc(hi, 1)

                act.wait_ge(L.w_in, 144)
                nc.scalar.activation(w1_sq[:, 0], w1l[:, :], ACT.Square)
                nc.scalar.activation(w1_sq[:, 1], w1r[:, :], ACT.Square).then_inc(w_squared, 1)
                for step, c in schedule(lag=3):
                    if step == "sum":
                        L.copy_ht(act, c)
                        L.copy_sums(act, c)
                        if c == 0:
                            act.wait_ge(w_norms, 1)
                            nc.scalar.activation(norms[:, :].rearrange("p q k -> p (q k)"), psum[:, 6, 0:4],
                                                 ACT.Sqrt).then_inc(w_rooted, 1)
                        continue
                    if c >= 2:
                        cut(c - 2)
                    if 1 <= c <= G:
                        n = len(tiles_of(c - 1))
                        act.wait_ge(t_psum, c)
                        if c >= 2:
                            act.wait_ge(yz_psum, c - 1)
                        nc.scalar.copy(h1T[:, 0:n].rearrange("p t k f -> p (t k f)"),
                                       psum[:, 6:8, :].rearrange("p b f -> p (b f)")[:, 0:n * H1]).then_inc(t_sb, 1)
                    if c < G:
                        n = len(tiles_of(c))
                        act.wait_ge(L.combined, c + 1)
                        nc.scalar.activation(h1[:, 0:n], h1[:, 0:n], ACT.Relu).then_inc(relued, 1)

            @block.vector
            def _(dve):
                link = linker(dve, L.dve_sem)

                def combine(c):
                    dve.wait_ge(L.u_psum, c + 1)
                    dve.sem_inc(L.agg_read, 1)
                    if c >= 1:
                        dve.wait_ge(t_psum, c)
                    for i, t in enumerate(tiles_of(c)):
                        at = slice((i % 2) * H1, (i % 2 + 1) * H1)
                        last = nc.vector.tensor_tensor(h1[:, i, :], psum[:, 4 + i // 2, at], b1, ALU.add)
                    link(last)
                    for i, t in enumerate(tiles_of(c)):
                        at = slice((i % 2) * H1, (i % 2 + 1) * H1)
                        last = nc.vector.scalar_tensor_tensor(
                            out=h1[:, i, :], in0=psum[:, 2 + i // 2, at], scalar=d["inv_deg"][:, t:t + 1],
                            in1=h1[:, i, :], op0=ALU.mult, op1=ALU.add)
                    last.then_inc(L.combined, 1)

                def cut(c):
                    n, tiles = len(tiles_of(c)), slice(tiles_of(c)[0], tiles_of(c)[-1] + 1)
                    dve.wait_ge(yz_psum, c + 1)
                    yz = psum[:, 1, 0:n * 2 * M2].rearrange("p (t f) -> p t f", f=2 * M2)
                    nc.vector.tensor_copy(z[:, tiles, :], yz[:, :, M2:2 * M2])
                    nc.vector.tensor_scalar(v[:, 0:n, :], yz[:, :, 0:M2], out.up, None, ALU.mult).then_inc(given, 1)
                    dve.wait_ge(hi, c + 1)
                    nc.vector.tensor_tensor(out.of(1, tiles), v[:, 0:n, :], out.of(0, tiles),
                                            ALU.subtract).then_inc(done, 1)
                    dve.wait_ge(done, c + 1)

                def magnitude(out, x):
                    return nc.vector.scalar_tensor_tensor(out=out, in0=x, scalar=-1.0, in1=x, op0=ALU.mult, op1=ALU.max)

                dve.wait_ge(L.w_in, 144)
                dve.wait_ge(w_rooted, 1)
                link(nc.vector.tensor_tensor(reach[:, :], norms[:, 0], norms[:, 1], ALU.add))
                link(magnitude(b1_abs[:, :], b1_col[:, :]))
                link(nc.vector.scalar_tensor_tensor(out=reach[:, :], in0=reach[:, :], scalar=float(D) ** 0.5,
                                                    in1=b1_abs[:, :], op0=ALU.mult, op1=ALU.add))
                link(magnitude(w2_reach[:, :, :], w2[:, :, :]))
                for k in range(2):
                    last = nc.vector.tensor_scalar(w2_reach[:, k], w2_reach[:, k], reach[:, k:k + 1], None, ALU.mult)
                last.then_inc(reached, 1)
                link(magnitude(b2_abs[:, :], b2_rows[:, :]))
                dve.wait_ge(bounded, 1)
                link(nc.vector.tensor_copy(bounds[:, 0], psum[:, 7, 0:M2]))
                link(nc.vector.tensor_tensor(bounds[:, 1], psum[:, 7, M2:2 * M2], bounds[:, 0], ALU.add))
                link(nc.vector.tensor_tensor(bounds[:, 1], bounds[:, 1], b2_abs[:, :], ALU.add))
                for k, scale in enumerate((d["scale_y"], d["scale_h2"])):
                    link(nc.vector.reduce_max(scale[:, 1:2], bounds[:, k], axis=AX.X))
                    link(nc.vector.tensor_scalar(scale[:, 1:2], scale[:, 1:2], 1e-30, 1 / F16_ROOM, ALU.max, ALU.mult))
                    link(nc.vector.reciprocal(scale[:, 0:1], scale[:, 1:2]))

                for c in range(G + 2):
                    if c >= 2:
                        cut(c - 2)
                    if c < G:
                        combine(c)


def narrow_layer(nc, new, d):
    with ExitStack() as ctx:
        L = Layer(nc, new, d, "narrow", ctx, d["h_in"])
        psum, z = L.psum, d["z"]
        v = L.sb("v", [P, GT, M2], F32)
        fold = L.sb("fold", [2 * M2, M2], F32)
        folded = L.new("folded")
        split = Split(nc, L.new, "split", v, d["h_out"])
        with nc.Block() as block:
            @block.gpsimd
            def _(pool):
                L.load_counts(pool)

            @block.sync
            def _(sp):
                for k in range(2):
                    sp.dma_start(fold[k * M2:(k + 1) * M2, :], L.ident[0:M2, 0:M2]).then_inc(folded, 16)

            @block.tensor
            def _(pe):
                pe.wait_ge(folded, 32)
                for step, c in schedule():
                    if step == "sum":
                        L.sum_group(pe, c)
                    else:
                        pe.wait_ge(L.agg_sb, c + 1)
                        if c >= 1:
                            pe.wait_ge(L.combined, c)
                        for i in range(len(tiles_of(c))):
                            last = nc.tensor.matmul(psum[:, 2, i * M2:(i + 1) * M2],
                                                    L.aggT[0:2 * M2, c % 2, i * P:(i + 1) * P], fold[:, :],
                                                    start=True, stop=True)
                        last.then_inc(L.u_psum, 1)

            @block.scalar
            def _(act):
                for step, c in schedule():
                    if step == "sum":
                        L.copy_sums(act, c)
                    else:
                        split.on_scalar(act, c)

            @block.vector
            def _(dve):
                for c in range(G):
                    dve.wait_ge(L.u_psum, c + 1)
                    dve.sem_inc(L.agg_read, 1)
                    for i, t in enumerate(tiles_of(c)):
                        last = nc.vector.scalar_tensor_tensor(
                            out=v[:, i, :], in0=psum[:, 2, i * M2:(i + 1) * M2], scalar=d["inv_deg"][:, t:t + 1],
                            in1=z[:, t, :], op0=ALU.mult, op1=ALU.add)
                    last.then_inc(split.given, 1)
                    dve.wait_ge(split.given, c + 1)
                    dve.sem_inc(L.combined, 1)
                    split.on_vector(dve, c)


def out_layer(nc, new, d):
    with ExitStack() as ctx:
        L = Layer(nc, new, d, "out", ctx, d["h_in"])
        psum, rows = L.psum, 2 * M2
        wl, wr, b = L.sb("w3l", [rows, D], F32), L.sb("w3r", [rows, D], F32), L.sb("b3", [1, D], F32)
        x, v = L.sb("x", [P, GT, D], F32), L.sb("v", [P, GT, D], F32)
        norm = Norm(nc, L.new, L.sb, "norm")
        split = Split(nc, L.new, "split", v, d["h_out"], d["h_sq"], d["trash"])
        x_in, x_ready, x_stored, normed = L.new("x_in"), L.new("x_ready"), L.new("x_stored"), L.new("normed")
        with nc.Block() as block:
            @block.sync
            def _(sp):
                for k in range(2):
                    sp.dma_start(wl[k * M2:(k + 1) * M2, :], d["L1_W3l"]).then_inc(L.w_in, 16)
                    sp.dma_start(wr[k * M2:(k + 1) * M2, :], d["L1_W3r"]).then_inc(L.w_in, 16)
                sp.dma_start(b[:, :], d["L1_b3"].rearrange("(a f) -> a f", a=1)).then_inc(L.w_in, 16)
                stream_x(sp, d["x1"], d["x2"], x, x_in, x_ready, x_stored, normed)

            @block.gpsimd
            def _(pool):
                L.load_counts(pool)

            @block.tensor
            def _(pe):
                for step, g in schedule():
                    if step == "sum":
                        L.transpose_h(pe, g)
                        L.sum_group(pe, g)
                    else:
                        if g == 0:
                            pe.wait_ge(L.w_in, 80)
                        pe.wait_ge(L.agg_sb, g + 1)
                        pe.wait_ge(L.ht_sb, g + 1)
                        if g >= 1:
                            pe.wait_ge(L.combined, g)
                        for i in range(len(tiles_of(g))):
                            at, nodes = slice(i * D, (i + 1) * D), slice(i * P, (i + 1) * P)
                            nc.tensor.matmul(psum[:, 2, at], L.aggT[0:rows, g % 2, nodes], wl[:, :], start=True,
                                             stop=True)
                            nc.tensor.matmul(psum[:, 3, at], L.hT[0:rows, g % 2, nodes], wr[:, :], start=True,
                                             stop=False)
                            last = nc.tensor.matmul(psum[:, 3, at], L.ones[0:1, :], b[:, :], start=False, stop=True)
                        last.then_inc(L.u_psum, 1)

            @block.scalar
            def _(act):
                for step, c in schedule():
                    if step == "sum":
                        L.copy_ht(act, c)
                        L.copy_sums(act, c)
                    else:
                        norm.on_scalar(act, d["eps"], c)
                        split.on_scalar(act, c)

            @block.vector
            def _(dve):
                link = linker(dve, L.dve_sem)
                for c in range(G):
                    n = len(tiles_of(c))
                    dve.wait_ge(L.u_psum, c + 1)
                    dve.sem_inc(L.agg_read, 1)
                    dve.wait_ge(x_in, 16 * (c + 1))
                    link(nc.vector.tensor_tensor(x[:, 0:n], x[:, 0:n], psum[:, 3, 0:n * D].rearrange(
                        "p (t f) -> p t f", f=D), ALU.add))
                    for i, t in enumerate(tiles_of(c)):
                        last = nc.vector.scalar_tensor_tensor(
                            out=x[:, i, :], in0=psum[:, 2, i * D:(i + 1) * D], scalar=d["inv_deg"][:, t:t + 1],
                            in1=x[:, i, :], op0=ALU.mult, op1=ALU.add)
                    link(last)
                    dve.sem_inc(L.combined, 1)
                    dve.sem_inc(x_ready, 1)
                    link(norm.on_vector(dve, link, v[:, 0:n], x[:, 0:n], c))
                    dve.sem_inc(normed, 1)
                    dve.sem_inc(split.given, 1)
                    split.on_vector(dve, c)


def stream_x(sp, source, target, x, x_in, x_ready, x_stored, normed):
    for c in range(G):
        n = len(tiles_of(c))
        if c >= 1:
            sp.wait_ge(x_stored, 16 * c)
            sp.wait_ge(normed, c)
        sp.dma_start(x[:, 0:n], group_ap(source, c)).then_inc(x_in, 16)
        sp.wait_ge(x_ready, c + 1)
        sp.dma_start(group_ap(target, c), x[:, 0:n]).then_inc(x_stored, 16)
    sp.wait_ge(x_stored, 16 * G)


def norm_layer(nc, new, d, number, layers):
    final = number == layers - 1
    with ExitStack() as ctx:
        L = Layer(nc, new, d, f"l2n{number}", ctx, d["h_in"])
        psum = L.psum
        wl, wr, b = L.sb("wl", [D, D], F32), L.sb("wr", [D, D], F32), L.sb("b", [P, D], F32)
        square = L.sb("square", [P, GT * P], F32)
        v = L.sb("v", [P, GT, D], F32)
        x = d["x_last"]
        s_h = L.sb("s_h", [P, NT], F32)
        s_agg = L.sb("s_agg", [P, GT], F32)
        norm = Norm(nc, L.new, L.sb, "norm")
        if not final:
            scale = d[f"scale{number}"]
            w_sq, bound = (d["h_out"].spare[:, k * 2 * D:(k + 1) * 2 * D].rearrange("p (a f) -> p a f", a=2)
                           for k in range(2))
            w_squared, w_norms, w_rooted, scaled = (L.new("w_squared"), L.new("w_norms"), L.new("w_rooted"),
                                                    L.new("scaled"))
        split = Split(nc, L.new, "split", v, d["h_out"], None if final else d["h_sq"], d["trash"])
        x_in, x_ready, x_stored, normed = L.new("x_in"), L.new("x_ready"), L.new("x_stored"), L.new("normed")
        squared, n2_psum, rooted, h_rooted = L.new("squared"), L.new("n2_psum"), L.new("rooted"), L.new("h_rooted")
        with nc.Block() as block:
            @block.sync
            def _(sp):
                sp.dma_start(wl[:, :], d["L2_Wl"][number]).then_inc(L.w_in, 16)
                sp.dma_start(wr[:, :], d["L2_Wr"][number]).then_inc(L.w_in, 16)
                sp.dma_start(b[:, :], d["L2_bl"][number:number + 1, :].broadcast_to([P, D])).then_inc(L.w_in, 16)
                if final:
                    stream_x(sp, d["x2"], d["x3"], x, x_in, x_ready, x_stored, normed)

            @block.gpsimd
            def _(pool):
                L.load_counts(pool)

            @block.tensor
            def _(pe):
                for step, g in schedule():
                    if step == "sum":
                        L.transpose_h(pe, g)
                        L.sum_group(pe, g)
                        if g == 0 and not final:
                            pe.wait_ge(w_squared, 1)
                            nc.tensor.matmul(psum[:, 5, 0:2 * D], L.ones[:, :],
                                             w_sq[:, :].rearrange("p a f -> p (a f)"), start=True,
                                             stop=True).then_inc(w_norms, 1)
                    else:
                        if g == 0:
                            pe.wait_ge(L.w_in, 48)
                        pe.wait_ge(L.ht_sb, g + 1)
                        pe.wait_ge(squared, g + 1)
                        if g >= 1:
                            pe.wait_ge(L.combined, g)
                        for i in range(len(tiles_of(g))):
                            last = nc.tensor.matmul(psum[:, 4, i:i + 1], square[:, i * P:(i + 1) * P],
                                                    L.ones[:, 0:1], start=True, stop=True)
                        last.then_inc(n2_psum, 1)
                        for i in range(len(tiles_of(g))):
                            at, nodes = slice(i * D, (i + 1) * D), slice(i * P, (i + 1) * P)
                            nc.tensor.matmul(psum[:, 2, at], L.aggT[:, g % 2, nodes], wl[:, :], start=True, stop=True)
                            last = nc.tensor.matmul(psum[:, 3, at], L.hT[:, g % 2, nodes], wr[:, :], start=True,
                                                    stop=True)
                        last.then_inc(L.u_psum, 1)

            @block.scalar
            def _(act):
                nc.scalar.activation(s_h[:, :], d["h_sq"][:, :], ACT.Sqrt).then_inc(h_rooted, 1)
                if not final:
                    act.wait_ge(L.w_in, 48)
                    nc.scalar.activation(w_sq[:, 0], wl[:, :], ACT.Square)
                    nc.scalar.activation(w_sq[:, 1], wr[:, :], ACT.Square).then_inc(w_squared, 1)
                for step, c in schedule():
                    if step == "sum":
                        n = len(tiles_of(c)) * P
                        L.copy_ht(act, c)
                        L.copy_sums(act, c)
                        if c == 0 and not final:
                            act.wait_ge(w_norms, 1)
                            nc.scalar.activation(bound[:, :].rearrange("p a f -> p (a f)"), psum[:, 5, 0:2 * D],
                                                 ACT.Sqrt).then_inc(w_rooted, 1)
                        act.wait_ge(L.agg_sb, c + 1)
                        if c >= 1:
                            act.wait_ge(n2_psum, c)
                        nc.scalar.activation(square[:, 0:n], L.aggT[:, c % 2, 0:n], ACT.Square).then_inc(squared, 1)
                    else:
                        n = len(tiles_of(c))
                        if c == 0 and not final:
                            act.wait_ge(scaled, 1)
                        act.wait_ge(n2_psum, c + 1)
                        if c >= 1:
                            act.wait_ge(L.combined, c)
                        nc.scalar.activation(s_agg[:, 0:n], psum[:, 4, 0:n], ACT.Sqrt).then_inc(rooted, 1)
                        if final:
                            norm.on_scalar(act, d["eps"], c)
                        split.on_scalar(act, c)

            @block.vector
            def _(dve):
                link = linker(dve, L.dve_sem)
                dve.wait_ge(h_rooted, 1)
                link(nc.vector.tensor_scalar(s_h[:, :], s_h[:, :], L2_EPS, None, ALU.max))
                link(nc.vector.reciprocal(s_h[:, :], s_h[:, :]))
                dve.wait_ge(L.w_in, 48)
                if not final:
                    dve.wait_ge(w_rooted, 1)
                    link(nc.vector.tensor_tensor(bound[:, 0], bound[:, 0], bound[:, 1], ALU.add))
                    link(nc.vector.scalar_tensor_tensor(out=bound[:, 1], in0=b[:, :], scalar=-1.0, in1=b[:, :],
                                                        op0=ALU.mult, op1=ALU.max))
                    link(nc.vector.tensor_tensor(bound[:, 0], bound[:, 0], bound[:, 1], ALU.add))
                    link(nc.vector.reduce_max(scale[:, 1:2], bound[:, 0], axis=AX.X))
                    link(nc.vector.tensor_scalar(scale[:, 1:2], scale[:, 1:2], 1e-30, 1 / F16_ROOM, ALU.max, ALU.mult))
                    nc.vector.reciprocal(scale[:, 0:1], scale[:, 1:2]).then_inc(scaled, 1)
                for c in range(G):
                    n = len(tiles_of(c))
                    t0 = tiles_of(c)[0]
                    dve.wait_ge(rooted, c + 1)
                    link(nc.vector.tensor_tensor(s_agg[:, 0:n], s_agg[:, 0:n], d["eps_deg"][:, t0:t0 + n], ALU.max))
                    link(nc.vector.reciprocal(s_agg[:, 0:n], s_agg[:, 0:n]))
                    dve.wait_ge(L.u_psum, c + 1)
                    dve.sem_inc(L.agg_read, 1)
                    for i, t in enumerate(tiles_of(c)):
                        last = nc.vector.scalar_tensor_tensor(
                            out=v[:, i, :], in0=psum[:, 3, i * D:(i + 1) * D], scalar=s_h[:, t:t + 1],
                            in1=b[:, :], op0=ALU.mult, op1=ALU.add)
                    link(last)
                    for i, t in enumerate(tiles_of(c)):
                        last = nc.vector.scalar_tensor_tensor(
                            out=v[:, i, :], in0=psum[:, 2, i * D:(i + 1) * D], scalar=s_agg[:, i:i + 1],
                            in1=v[:, i, :], op0=ALU.mult, op1=ALU.add)
                    link(last)
                    dve.sem_inc(L.combined, 1)
                    if final:
                        dve.wait_ge(x_in, 16 * (c + 1))
                        link(nc.vector.tensor_tensor(x[:, 0:n], x[:, 0:n], v[:, 0:n], ALU.add))
                        dve.sem_inc(x_ready, 1)
                        link(norm.on_vector(dve, link, v[:, 0:n], x[:, 0:n], c))
                        dve.sem_inc(normed, 1)
                    dve.sem_inc(split.given, 1)
                    split.on_vector(dve, c)


def weighted_layers(nc, new, d):
    SL = SLABS
    with ExitStack() as ctx:
        def sb(name, shape, dt):
            return ctx.enter_context(nc.sbuf_tensor("wl_" + name, shape, dt))

        def sem(name):
            return new("wl_" + name)

        psum, ident = d["psum"], d["ident"]
        slab = counts_slab(d)
        free_a = d["parts_a"][:, :].bitcast(F32)[:, NT * D:]
        free_b = d["parts_b"][:, :].bitcast(F32)
        g = [sb("g1", [P, NT, D], F32), free_b[:, 0:NT * D].rearrange("p (t f) -> p t f", f=D)]
        free_b = free_b[:, NT * D:]
        w = [sb("w1", [D, D], F32), sb("w2", [D, D], F32)]
        b = [sb("b1", [P, D], F32), free_a[:, 2 * GT * D:2 * GT * D + D]]
        hT = free_b[:, 0:GT * P]
        aggT = free_b[:, GT * P:3 * GT * P].rearrange("p (a n) -> p a n", a=2)

        def hT_of(m):
            return aggT[:, m % 2] if m < G else hT

        def product_bank(m):
            return 3 + 2 * (m % 2)

        out = free_a[:, 0:GT * D].rearrange("p (t f) -> p t f", f=D)
        x = free_a[:, GT * D:2 * GT * D].rearrange("p (t f) -> p t f", f=D)

        kept = list(range(G - SL, G - 1))
        order = list(range(G)) + kept + list(range(G - SL)) + [G - 1]
        loads = [n for n in range(2 * G) if not G <= n < G + len(kept)]

        def loaded(n):
            return sum(m <= n and m % SL == n % SL for m in loads)

        w_in, slab_in = sem("w_in"), [sem(f"slab_in{i}") for i in range(SL)]
        ht_psum, ht_sb, p_psum, scaled = sem("ht_psum"), sem("ht_sb"), sem("p_psum"), sem("scaled")
        summed, agg_sb, t_psum, combined, relued = (sem("summed"), sem("agg_sb"), sem("t_psum"), sem("combined"),
                                                    sem("relued"))
        x_in, x_ready, stored = sem("x_in"), sem("x_ready"), sem("stored")
        dve_sem = sem("dve")

        with nc.Block() as block:
            @block.sync
            def _(sp):
                for k in range(2):
                    sp.dma_start(w[k][:, :], d[f"L3_W{k + 1}"]).then_inc(w_in, 16)
                    sp.dma_start(b[k][:, :], d[f"L3_b{k + 1}"].rearrange("(a f) -> a f", a=1).broadcast_to([P, D])
                                 ).then_inc(w_in, 16)
                for n in loads:
                    c = order[n]
                    m = min(WG, J - c * WG)
                    if n >= SL:
                        sp.wait_ge(summed, n - SL + 1)
                    sp.dma_start(slab[:, n % SL, 0:m, :], d["aw"][c * WG:c * WG + m].rearrange("j p k -> p j k")
                                 ).then_inc(slab_in[n % SL], 16)

            @block.gpsimd
            def _(pool):
                for i, c in enumerate(order[G:]):
                    m = len(tiles_of(c))
                    if i >= 1:
                        pool.wait_ge(stored, 16 * i)
                    pool.dma_start(x[:, 0:m], group_ap(d["x3"], c)).then_inc(x_in, 16)
                    pool.wait_ge(x_ready, i + 1)
                    if c < G - 1:
                        pool.dma_start(group_ap(d["out"], c), x[:, 0:m]).then_inc(stored, 16)
                    else:
                        rows = N - c * GT * P
                        pool.dma_start(d["out"][c * GT * P:N, :], x[0:rows, 0, :]).then_inc(stored, 16)
                pool.wait_ge(stored, 16 * G)

            @block.tensor
            def _(pe):
                def transposed(m):
                    if m < G:
                        transpose_parts(nc, d, d["h_in"], pe, m, ht_psum, ht_sb, banks=(1, 4))
                        return
                    pe.wait_ge(ht_sb, m)
                    for i in range(len(tiles_of(m - G))):
                        last = nc.tensor.transpose(psum[:, 1, i * P:(i + 1) * P], out[:, i, :], ident[:, :])
                    last.then_inc(ht_psum, 1)

                def product(m):
                    c, k = m % G, m // G
                    pe.wait_ge(ht_sb, m + 1)
                    if m >= 2:
                        pe.wait_ge(scaled, m - 1)
                    for i in range(len(tiles_of(c))):
                        last = nc.tensor.matmul(psum[:, product_bank(m), i * D:(i + 1) * D],
                                                hT_of(m)[:, i * P:(i + 1) * P], w[k][:, :],
                                                start=True, stop=True)
                    last.then_inc(p_psum, 1)

                def sum_group(n):
                    c, k = order[n], n // G
                    m = min(WG, J - c * WG)
                    pe.wait_ge(slab_in[n % SL], 16 * loaded(n))
                    if n >= 1:
                        pe.wait_ge(agg_sb, n)
                    for t in range(NT):
                        if n % G == 0 and t % GT == 0:
                            pe.wait_ge(scaled, n + t // GT + 1)
                        last = nc.tensor.matmul(psum[:, 0, 0:m * W], g[k][:, t, :],
                                                slab[:, n % SL, 0:m, t * W:(t + 1) * W], start=(t == 0),
                                                stop=(t == NT - 1))
                    last.then_inc(summed, 1)

                def back(n):
                    pe.wait_ge(agg_sb, n + 1)
                    if n >= 1:
                        pe.wait_ge(combined, n)
                    for i in range(len(tiles_of(order[n]))):
                        last = nc.tensor.transpose(psum[:, 2, i * P:(i + 1) * P], aggT[:, n % 2, i * P:(i + 1) * P],
                                                   ident[:, :])
                    last.then_inc(t_psum, 1)

                pe.wait_ge(w_in, 64)
                transposed(0)
                for m in range(G):
                    if m < G - 1:
                        transposed(m + 1)
                    product(m)
                for c in range(G + 2):
                    if c < G:
                        sum_group(c)
                    if c >= 2:
                        pe.wait_ge(relued, c - 1)
                        transposed(G + c - 2)
                    if 1 <= c <= G:
                        back(c - 1)
                    if c >= 2:
                        product(G + c - 2)
                for c in range(G + 1):
                    if c < G:
                        sum_group(G + c)
                    if c >= 1:
                        back(G + c - 1)

            @block.scalar
            def _(act):
                def copy_t(m):
                    n = len(tiles_of(m % G)) * P
                    act.wait_ge(ht_psum, m + 1)
                    if m > G:
                        act.wait_ge(p_psum, m)
                    elif m >= 2:
                        act.wait_ge(p_psum, m - 1)
                    nc.scalar.activation(hT_of(m)[:, 0:n], psum[:, 4 if m < G and m % 2 else 1, 0:n], ACT.Copy,
                                         scale=d["h_in"].down if m < G else 1.0).then_inc(ht_sb, 1)

                def copy_sums(n):
                    c = order[n]
                    m = min(GT * P, NCOL - c * GT * P)
                    act.wait_ge(summed, n + 1)
                    if n >= 2:
                        act.wait_ge(t_psum, n - 1)
                    nc.scalar.copy(aggT[:, n % 2, 0:m], psum[:, 0, 0:m]).then_inc(agg_sb, 1)

                for m in range(G):
                    copy_t(m)
                for c in range(G + 2):
                    if c < G:
                        copy_sums(c)
                    if c >= 2:
                        copy_t(G + c - 2)
                    if 1 <= c <= G:
                        n = len(tiles_of(c - 1))
                        act.wait_ge(combined, c)
                        nc.scalar.activation(out[:, 0:n], out[:, 0:n], ACT.Relu).then_inc(relued, 1)
                for c in range(G):
                    copy_sums(G + c)

            @block.vector
            def _(dve):
                link = linker(dve, dve_sem)
                dinv = d["dinv"]

                def scale(m):
                    c, k = m % G, m // G
                    dve.wait_ge(p_psum, m + 1)
                    for i, t in enumerate(tiles_of(c)):
                        last = nc.vector.tensor_scalar(g[k][:, t, :], psum[:, product_bank(m), i * D:(i + 1) * D],
                                                       dinv[:, t:t + 1], None, ALU.mult)
                    last.then_inc(scaled, 1)

                def combine(n):
                    c, k = order[n], n // G
                    m = len(tiles_of(c))
                    t0 = tiles_of(c)[0]
                    dve.wait_ge(t_psum, n + 1)
                    if 1 <= n <= G:
                        dve.wait_ge(ht_psum, G + n)
                    link(nc.vector.tensor_tensor(out[:, 0:m], psum[:, 2, 0:m * D].rearrange("p (t f) -> p t f", f=D),
                                                 g[k][:, t0:t0 + m], ALU.add))
                    for i, t in enumerate(tiles_of(c)):
                        last = nc.vector.scalar_tensor_tensor(out=out[:, i, :], in0=out[:, i, :],
                                                              scalar=dinv[:, t:t + 1], in1=b[k][:, :],
                                                              op0=ALU.mult, op1=ALU.add)
                    link(last)
                    dve.sem_inc(combined, 1)

                dve.wait_ge(w_in, 64)
                for m in range(G):
                    scale(m)
                for c in range(G + 1):
                    if c < G:
                        combine(c)
                    if c >= 1:
                        scale(G + c - 1)
                for c in range(G):
                    m = len(tiles_of(order[G + c]))
                    combine(G + c)
                    dve.wait_ge(x_in, 16 * (c + 1))
                    link(nc.vector.tensor_tensor(x[:, 0:m], x[:, 0:m], out[:, 0:m], ALU.add))
                    dve.sem_inc(x_ready, 1)


def load_crowded(nc, d):
    flag = d["starts"][0:1, J + 1:J + 2]
    d["crowded"] = {}
    with nc.Block() as block:
        @block.sync
        def _(sp):
            d["crowded"]["SP"] = sp.value_load(flag, min_val=0, max_val=E + J)

        @block.gpsimd
        def _(pool):
            d["crowded"]["Pool"] = pool.value_load(flag, min_val=0, max_val=E + J)

        @block.vector
        def _(dve):
            d["crowded"]["DVE"] = dve.value_load(flag, min_val=0, max_val=E + J)

        @block.scalar
        def _(act):
            d["crowded"]["Activation"] = act.value_load(flag, min_val=0, max_val=E + J)

        @block.tensor
        def _(pe):
            d["crowded"]["PE"] = pe.value_load(flag, min_val=0, max_val=E + J)


def build(nc, d):
    with ExitStack() as ctx:
        held = []

        def new(name):
            held.append(nc.alloc_semaphore(name=name))
            return held[-1]

        def end_phase():
            nc.all_engine_barrier()
            nc.clear_and_free_semaphores(held)
            nc.all_engine_barrier()
            held.clear()

        def keep(name, shape, dt):
            d[name] = ctx.enter_context(nc.sbuf_tensor(name, shape, dt))

        d["psum"] = ctx.enter_context(nc.psum_tensor("psum", [P, 8, 512], F32))
        keep("ident", [P, P], F32)
        keep("ones", [P, P], F32)
        keep("eps", [P, 1], F32)
        keep("starts", [1, J + 2], I32)
        keep("inv_deg", [P, NT], F32)
        keep("eps_deg", [P, NT], F32)
        keep("dinv", [P, NT], F32)
        made = new("ident_made")
        with nc.Block() as block:
            @block.gpsimd
            def _(pool):
                nc.gpsimd.memset(d["ident"][:, :], 0.0).then_inc(made, 1)
                nc.gpsimd.memset(d["ones"][:, :], 1.0).then_inc(made, 1)
                nc.gpsimd.memset(d["eps"][:, :], LN_EPS).then_inc(made, 1)
                pool.wait_ge(made, 3)
                nc.gpsimd.affine_select(out=d["ident"][:, :], in_=d["ident"][:, :], compare_op=ALU.not_equal, fill=1.0,
                                        base=0, pattern=[[-1, P]], channel_multiplier=1).then_inc(made, 1)
                pool.wait_ge(made, 4)
        prepare(nc, new, d)
        end_phase()
        load_crowded(nc, d)
        keep("adj", [P, NT, NCOL], F16)
        edge_pass(nc, new, d)
        end_phase()
        crowded_edge_pass(nc, new, d)
        end_phase()
        keep("h_sq", [P, NT], F32)
        keep("scale_y", [P, 2], F32)
        keep("scale_h2", [P, 2], F32)
        keep("scale0", [P, 2], F32)
        keep("scale1", [P, 2], F32)
        keep("trash", [P, D], BF16)
        keep("ident_b", [P, P], BF16)
        keep("parts_a", [P, NT * 3 * D], F16)
        keep("parts_b", [P, NT * 3 * D], F16)
        a, b = d["parts_a"], d["parts_b"]
        a_f32, b_f32 = a[:, :].bitcast(F32), b[:, :].bitcast(F32)
        at = NT * M2
        d["z"] = b_f32[:, at:at + NT * M2].rearrange("p (t f) -> p t f", f=M2)
        at += NT * M2
        d["h1"] = b_f32[:, at:at + GT * H1].rearrange("p (t f) -> p t f", f=H1)
        at += GT * H1
        d["w1_sq"] = b_f32[:, at:at + 2 * H1].rearrange("p (q f) -> p q f", f=H1)
        at = NT * D
        d["h1T"] = a_f32[:, at:at + GT * H1].rearrange("p (t k f) -> p t k f", k=2, f=P)
        at += GT * H1
        d["b1_wide"] = a_f32[:, at:at + H1]
        at += H1
        d["y_group"] = a_f32[:, at:at + GT * M2].rearrange("p (t f) -> p t f", f=M2)
        d["x_last"] = a_f32[:, NT * D:(NT + GT) * D].rearrange("p (t f) -> p t f", f=D)
        flow = [(first_tail, (), Parts(a, D)),
                (wide_layer, (), Parts(b, M2, d["scale_y"][:, 0:1], d["scale_y"][:, 1:2])),
                (narrow_layer, (), Parts(a, M2, d["scale_h2"][:, 0:1], d["scale_h2"][:, 1:2])),
                (out_layer, (), Parts(b, D)),
                (norm_layer, (0, 3), Parts(a, D, d["scale0"][:, 0:1], d["scale0"][:, 1:2])),
                (norm_layer, (1, 3), Parts(b, D, d["scale1"][:, 0:1], d["scale1"][:, 1:2])),
                (norm_layer, (2, 3), Parts(a, D))]
        for layer, which, out in flow:
            d["h_out"] = out
            layer(nc, new, d, *which)
            end_phase()
            d["h_in"] = out
        weighted_layers(nc, new, d)


def kernel(**inputs):
    import numpy as np
    import concourse.bacc as bacc
    from concourse.bass_utils import run_bass_kernel_spmd

    arr = {k: np.ascontiguousarray(v) for k, v in inputs.items()}

    def padded(a, n, value):
        return np.concatenate([a, np.full((n - a.shape[0],) + a.shape[1:], value, a.dtype)])

    send = {
        "x": padded(arr["x"], NPAD, 0),
        "src": padded(arr["src"], EPAD, 0),
        "dst": padded(arr["dst"], EPAD + P, FAR),
        "w": padded(arr["edge_weight"], EPAD, 0),
        "ea": np.ascontiguousarray(padded(arr["edge_attr_32"], EPAD, 0).T),
        "L0_W1": np.ascontiguousarray(arr["L0_gnn_W1"].T),
        "L0_b1": arr["L0_gnn_b1"],
        "L0_W2": np.ascontiguousarray(arr["L0_gnn_W2"].T),
        "L0_Wu": np.ascontiguousarray(arr["L0_gnn_Wu"].T),
        "L2_Wl": np.ascontiguousarray(arr["L2_gnn_Wl"].transpose(0, 2, 1)),
        "L2_Wr": np.ascontiguousarray(arr["L2_gnn_Wr"].transpose(0, 2, 1)),
    }
    for name in ("L0_b2", "L0_bu", "L0_gamma", "L0_beta", "L1_b1", "L1_b2", "L1_b3", "L2_bl", "L3_W1", "L3_b1",
                 "L3_W2", "L3_b2"):
        send[name] = arr[name.replace("_", "_gnn_")]
    for name in ("L1_W1l", "L1_W1r", "L1_W2l", "L1_W2r", "L1_W3l", "L1_W3r"):
        send[name] = np.ascontiguousarray(arr[name.replace("_", "_gnn_")].T)
    nc = bacc.Bacc("TRN2", target_bir_lowering=False, num_devices=1)
    d = {k: nc.dram_tensor("in_" + k, v.shape, mybir.dt.from_np(v.dtype), kind="ExternalInput").ap()
         for k, v in send.items()}
    for name, shape in (("records", (EPAD, REC)), ("dst_row", (EPAD,)), ("h0", (NPAD, D)), ("P", (NPAD, D)),
                        ("Q", (NPAD, D)), ("aw", (J, P, NKEY)), ("counts", (J, P, NKEY)),
                        ("P_src", (-(-E // BLK) * BLK, D)),
                        ("agg", (D, NPAD)), ("deg", (4, NPAD)),
                        ("x1", (NPAD, D)), ("x2", (NPAD, D)), ("x3", (NPAD, D))):
        d[name] = nc.dram_tensor("dram_" + name, shape, F32, kind="Internal").ap()
    d["out"] = nc.dram_tensor("out", (N, D), F32, kind="ExternalOutput").ap()
    build(nc, d)
    r = run_bass_kernel_spmd(nc, [{"in_" + k: v for k, v in send.items()}], core_ids=[0])
    return r.results[0]["out"]
```
